# Optimizing a Trainium2 kernel written in Bass

```python
import numpy as np
import jax
import jax.numpy as jnp

def _softmax(x, axis=-1):
    return jax.nn.softmax(x, axis=axis)

def _gelu(x):
    return jax.nn.gelu(x, approximate=True)

def _silu(x):
    return jax.nn.silu(x)

def _sigmoid(x):
    return jax.nn.sigmoid(x)

def _layernorm(x, axis=-1, eps=1e-05):
    m = jnp.mean(x, axis=axis, keepdims=True)
    v = jnp.var(x, axis=axis, keepdims=True)
    return (x - m) / jnp.sqrt(v + eps)

def _scatter_add(tgt, idx, src, axis=0):
    return tgt.at[idx].add(src)

def _segment_sum(src, seg, n):
    return jax.ops.segment_sum(src, seg, n)
kernel_name = 'mk_gps_d1_gnn_r32_681c2f'

def setup_inputs(seed: int=0):
    np.random.seed(seed)
    _w = jnp.asarray

    def _rec_inputs():
        import jax
        import jax.numpy as jnp
        _gk = jax.random.key(seed)
        x = -0.0002117 + 1 * jax.random.normal(jax.random.fold_in(_gk, 1), (3125, 256), jnp.float32)
        src = jax.random.randint(jax.random.fold_in(_gk, 2), (50000,), 0, 3125, jnp.int32)
        dst = jnp.minimum((3125 * jax.random.uniform(jax.random.fold_in(_gk, 3), (50000,)) ** 2.0).astype(jnp.int32), 99999)
        _o = jnp.argsort(dst, stable=True)
        src = src[_o]
        dst = dst[_o]
        return (x, src, dst)
    x, src, dst = _rec_inputs()

    def _L0_gnn_setup():
        import jax, jax.numpy as jnp
        import numpy as np
        N_NODES = 3125
        N_EDGES = 100000
        D_IN = 256
        D_OUT = 256
        key = jax.random.key(seed)
        k1, k2, k3, k4 = jax.random.split(key, 4)
        x = jax.random.normal(k1, (N_NODES, D_IN), dtype=jnp.float32)
        edge_index = jax.random.randint(k2, (2, N_EDGES), 0, N_NODES, dtype=jnp.int64)
        limit = np.sqrt(6.0 / (D_IN + D_OUT)).astype(np.float32)
        W = jax.random.uniform(k3, (D_IN, D_OUT), dtype=jnp.float32, minval=-limit, maxval=limit)
        b = jnp.zeros((D_OUT,), dtype=jnp.float32)
        return {'x': x, 'edge_index': edge_index, 'W': W, 'b': b}
    _L0_gnn_all = _L0_gnn_setup()
    _L0_gnn_in = {k: v for k, v in _L0_gnn_all.items() if k in ('W', 'b')}
    del _L0_gnn_all

    def _L0_mix_setup():
        import jax, jax.numpy as jnp
        import numpy as np
        EMB, HEADS, DEPTH, SEQ, BATCH = (256, 8, 4, 256, 4)
        DH = EMB // HEADS
        FF = 4 * EMB
        EPS = 1e-05

        def _layernorm(x, g, b):
            mu = x.mean(-1, keepdims=True)
            var = ((x - mu) ** 2).mean(-1, keepdims=True)
            return (x - mu) * jax.lax.rsqrt(var + EPS) * g + b

        def _linear_attn(x, Wq, Wk, Wv, Wo, bo):
            b, n, dm = x.shape
            split = lambda t: t.reshape(b, n, HEADS, DH).transpose(0, 2, 1, 3)
            scale = DH ** (-0.25)
            q = jax.nn.softmax(split(x @ Wq) * scale, axis=-1)
            k = jax.nn.softmax(split(x @ Wk) * scale, axis=-2)
            v = split(x @ Wv)
            context = jnp.einsum('bhnd,bhne->bhde', k, v)
            out = jnp.einsum('bhnd,bhde->bhne', q, context)
            out = out.transpose(0, 2, 1, 3).reshape(b, n, dm)
            return out @ Wo + bo

        def _forward(x, Wq, Wk, Wv, Wo, bo, ln1_g, ln1_b, W1, b1, W2, b2, ln2_g, ln2_b):
            for i in range(DEPTH):
                h = _layernorm(x, ln1_g[i], ln1_b[i])
                x = x + _linear_attn(h, Wq[i], Wk[i], Wv[i], Wo[i], bo[i])
                h = _layernorm(x, ln2_g[i], ln2_b[i])
                x = x + (jax.nn.gelu(h @ W1[i] + b1[i], approximate=False) @ W2[i] + b2[i])
            return x
        key = jax.random.key(seed)
        ks = jax.random.split(key, 8)
        w = lambda k, shape: jax.random.normal(k, shape, dtype=jnp.float32) * 0.02
        D = DEPTH
        return {'x': jax.random.normal(ks[0], (BATCH, SEQ, EMB), dtype=jnp.float32), 'Wq': w(ks[1], (D, EMB, EMB)), 'Wk': w(ks[2], (D, EMB, EMB)), 'Wv': w(ks[3], (D, EMB, EMB)), 'Wo': w(ks[4], (D, EMB, EMB)), 'bo': jnp.zeros((D, EMB), jnp.float32), 'ln1_g': jnp.ones((D, EMB), jnp.float32), 'ln1_b': jnp.zeros((D, EMB), jnp.float32), 'W1': w(ks[5], (D, EMB, FF)), 'b1': jnp.zeros((D, FF), jnp.float32), 'W2': w(ks[6], (D, FF, EMB)), 'b2': jnp.zeros((D, EMB), jnp.float32), 'ln2_g': jnp.ones((D, EMB), jnp.float32), 'ln2_b': jnp.zeros((D, EMB), jnp.float32)}
    _L0_mix_all = _L0_mix_setup()
    _L0_mix_in = {k: v for k, v in _L0_mix_all.items() if k in ('Wq', 'Wk', 'Wv', 'Wo', 'bo', 'ln1_g', 'ln1_b', 'W1', 'b1', 'W2', 'b2', 'ln2_g', 'ln2_b')}
    del _L0_mix_all

    def _L0_ffn_setup():
        import math
        import jax, jax.numpy as jnp
        import numpy as np
        CAPACITY_FACTOR = 1.25
        key = jax.random.key(seed)
        ks = jax.random.split(key, 5)
        B, L, D, F, E = (8, 256, 256, 1024, 8)
        h = jax.random.normal(ks[0], (B, L, D), dtype=jnp.float32)
        gate_w = jax.random.normal(ks[1], (D, E), dtype=jnp.float32) * 0.02
        gate_b = jnp.zeros((E,), dtype=jnp.float32)
        w1 = jax.random.normal(ks[2], (E, D, F), dtype=jnp.float32) * (1.0 / math.sqrt(D))
        b1 = jnp.zeros((E, F), dtype=jnp.float32)
        w2 = jax.random.normal(ks[3], (E, F, D), dtype=jnp.float32) * (1.0 / math.sqrt(F))
        b2 = jnp.zeros((E, D), dtype=jnp.float32)
        return {'h': h, 'gate_w': gate_w, 'gate_b': gate_b, 'w1': w1, 'b1': b1, 'w2': w2, 'b2': b2}
    _L0_ffn_all = _L0_ffn_setup()
    _L0_ffn_in = {k: v for k, v in _L0_ffn_all.items() if k in ('gate_w', 'gate_b', 'w1', 'b1', 'w2', 'b2')}
    del _L0_ffn_all
    return {'x': x, 'src': src, 'dst': dst, 'L0_gnn_W': _L0_gnn_in['W'], 'L0_gnn_b': _L0_gnn_in['b'], 'L0_mix_Wq': _L0_mix_in['Wq'], 'L0_mix_Wk': _L0_mix_in['Wk'], 'L0_mix_Wv': _L0_mix_in['Wv'], 'L0_mix_Wo': _L0_mix_in['Wo'], 'L0_mix_bo': _L0_mix_in['bo'], 'L0_mix_ln1_g': _L0_mix_in['ln1_g'], 'L0_mix_ln1_b': _L0_mix_in['ln1_b'], 'L0_mix_W1': _L0_mix_in['W1'], 'L0_mix_b1': _L0_mix_in['b1'], 'L0_mix_W2': _L0_mix_in['W2'], 'L0_mix_b2': _L0_mix_in['b2'], 'L0_mix_ln2_g': _L0_mix_in['ln2_g'], 'L0_mix_ln2_b': _L0_mix_in['ln2_b'], 'L0_ffn_gate_w': _L0_ffn_in['gate_w'], 'L0_ffn_gate_b': _L0_ffn_in['gate_b'], 'L0_ffn_w1': _L0_ffn_in['w1'], 'L0_ffn_b1': _L0_ffn_in['b1'], 'L0_ffn_w2': _L0_ffn_in['w2'], 'L0_ffn_b2': _L0_ffn_in['b2']}

def reference(x, src, dst, L0_gnn_W, L0_gnn_b, L0_mix_Wq, L0_mix_Wk, L0_mix_Wv, L0_mix_Wo, L0_mix_bo, L0_mix_ln1_g, L0_mix_ln1_b, L0_mix_W1, L0_mix_b1, L0_mix_W2, L0_mix_b2, L0_mix_ln2_g, L0_mix_ln2_b, L0_ffn_gate_w, L0_ffn_gate_b, L0_ffn_w1, L0_ffn_b1, L0_ffn_w2, L0_ffn_b2):
    import jax
    import jax.numpy as jnp

    def _L0_gnn_ref(x, edge_index, W, b):
        import jax, jax.numpy as jnp
        import numpy as np
        N_NODES = 3125
        N_EDGES = 100000
        D_IN = 256
        D_OUT = 256
        N = x.shape[0]
        h = x @ W
        loop = jnp.arange(N, dtype=edge_index.dtype)
        src = jnp.concatenate([edge_index[0], loop])
        dst = jnp.concatenate([edge_index[1], loop])
        deg = jax.ops.segment_sum(jnp.ones(dst.shape, dtype=h.dtype), dst, num_segments=N)
        dinv = jnp.where(deg > 0, jax.lax.rsqrt(deg), 0.0)
        norm = dinv[src] * dinv[dst]
        out = jax.ops.segment_sum(norm[:, None] * h[src], dst, num_segments=N) + b
        return jax.nn.leaky_relu(out, negative_slope=0.2)

    def _L0_mix_ref(x, Wq, Wk, Wv, Wo, bo, ln1_g, ln1_b, W1, b1, W2, b2, ln2_g, ln2_b):
        import jax, jax.numpy as jnp
        import numpy as np
        EMB, HEADS, DEPTH, SEQ, BATCH = (256, 8, 4, 256, 4)
        DH = EMB // HEADS
        FF = 4 * EMB
        EPS = 1e-05

        def _layernorm(x, g, b):
            mu = x.mean(-1, keepdims=True)
            var = ((x - mu) ** 2).mean(-1, keepdims=True)
            return (x - mu) * jax.lax.rsqrt(var + EPS) * g + b

        def _linear_attn(x, Wq, Wk, Wv, Wo, bo):
            b, n, dm = x.shape
            split = lambda t: t.reshape(b, n, HEADS, DH).transpose(0, 2, 1, 3)
            scale = DH ** (-0.25)
            q = jax.nn.softmax(split(x @ Wq) * scale, axis=-1)
            k = jax.nn.softmax(split(x @ Wk) * scale, axis=-2)
            v = split(x @ Wv)
            context = jnp.einsum('bhnd,bhne->bhde', k, v)
            out = jnp.einsum('bhnd,bhde->bhne', q, context)
            out = out.transpose(0, 2, 1, 3).reshape(b, n, dm)
            return out @ Wo + bo

        def _forward(x, Wq, Wk, Wv, Wo, bo, ln1_g, ln1_b, W1, b1, W2, b2, ln2_g, ln2_b):
            for i in range(DEPTH):
                h = _layernorm(x, ln1_g[i], ln1_b[i])
                x = x + _linear_attn(h, Wq[i], Wk[i], Wv[i], Wo[i], bo[i])
                h = _layernorm(x, ln2_g[i], ln2_b[i])
                x = x + (jax.nn.gelu(h @ W1[i] + b1[i], approximate=False) @ W2[i] + b2[i])
            return x
        return _forward(x, Wq, Wk, Wv, Wo, bo, ln1_g, ln1_b, W1, b1, W2, b2, ln2_g, ln2_b)

    def _L0_ffn_ref(h, gate_w, gate_b, w1, b1, w2, b2):
        import math
        import jax, jax.numpy as jnp
        import numpy as np
        CAPACITY_FACTOR = 1.25
        B, L, D = h.shape
        E = gate_w.shape[1]
        T = B * L
        C = max(1, math.ceil(CAPACITY_FACTOR * T / E))
        x = h.reshape(T, D)
        logits = x @ gate_w + gate_b
        probs = jax.nn.softmax(logits, axis=-1)
        idx = jnp.argmax(probs, axis=-1)
        prb = jnp.take_along_axis(probs, idx[:, None], axis=1)[:, 0]
        one_hot = jax.nn.one_hot(idx, E, dtype=jnp.float32)
        pos = (jnp.cumsum(one_hot, axis=0) * one_hot).sum(-1).astype(jnp.int32) - 1
        kept = pos < C
        pos_safe = jnp.where(kept, pos, C)
        buf = jnp.zeros((E, C, D), dtype=h.dtype).at[idx, pos_safe].set(x, mode='drop')
        hmid = jax.nn.relu(jnp.einsum('ecd,edf->ecf', buf, w1) + b1[:, None, :])
        ybuf = jnp.einsum('ecf,efd->ecd', hmid, w2) + b2[:, None, :]
        pos_g = jnp.minimum(pos, C - 1)
        y_tok = ybuf[idx, pos_g] * (prb * kept)[:, None]
        y = y_tok.reshape(B, L, D)
        y = jnp.nan_to_num(y, nan=0.0, posinf=10000.0, neginf=-10000.0)
        return y
    edge_index = jnp.stack([src, dst])
    xn = _layernorm(x, axis=-1)
    x = x + _L0_gnn_ref(xn, edge_index, L0_gnn_W, L0_gnn_b) + _L0_mix_ref(xn[None], L0_mix_Wq, L0_mix_Wk, L0_mix_Wv, L0_mix_Wo, L0_mix_bo, L0_mix_ln1_g, L0_mix_ln1_b, L0_mix_W1, L0_mix_b1, L0_mix_W2, L0_mix_b2, L0_mix_ln2_g, L0_mix_ln2_b)[0]
    x = x + _L0_ffn_ref(_layernorm(x, axis=-1)[None], L0_ffn_gate_w, L0_ffn_gate_b, L0_ffn_w1, L0_ffn_b1, L0_ffn_w2, L0_ffn_b2)[0]
    return x

_drawn_inputs = setup_inputs


def setup_inputs(seed=0):
    import zlib

    import numpy as np

    out = dict(_drawn_inputs(seed))
    spreads = {'L0_gnn_b': (0.0, 0.1),
     'L0_mix_bo': (0.0, 0.1),
     'L0_mix_ln1_g': (1.0, 0.6),
     'L0_mix_ln1_b': (0.0, 0.675),
     'L0_mix_b1': (0.0, 0.1),
     'L0_mix_b2': (0.0, 0.1),
     'L0_mix_ln2_g': (1.0, 0.6),
     'L0_mix_ln2_b': (0.0, 0.573),
     'L0_ffn_gate_b': (0.0, 0.1),
     'L0_ffn_b1': (0.0, 0.8),
     'L0_ffn_b2': (0.0, 0.8)}
    factors = {'L0_mix_Wq': 34.337, 'L0_mix_Wk': 29.717}
    for name, (base, spread) in spreads.items():
        noise = np.random.default_rng([zlib.crc32(name.encode()), seed]).standard_normal(out[name].shape)
        drawn = base * np.exp(spread * noise) if base else spread * noise
        out[name] = jnp.asarray(drawn.astype(out[name].dtype))
    for name, factor in factors.items():
        out[name] = (out[name] * factor).astype(out[name].dtype)
    return out
```

```python
import concourse.bass as bass
from concourse import mybir
from contextlib import ExitStack

def build(nc, A, out):
    f32 = mybir.dt.float32
    f16 = mybir.dt.float16
    i32 = mybir.dt.int32
    ALU = mybir.AluOpType
    ACT = mybir.ActivationFunctionType
    AX = mybir.AxisListType
    ds = bass.ds

    def some_missed(eng, flag, ready):
        eng.wait_ge(ready, 1)
        return eng.If(eng.value_load(flag, min_val=0, max_val=1) != 0)

    RMAX = bass.bass_isa.ReduceOp.max

    N, D = A["x"].shape
    L = A["L0_mix_Wq"].shape[0]
    FF = A["L0_mix_W1"].shape[2]
    P = 125
    T = N // P
    TG = 5
    G = T // TG
    NG = P * TG
    KD = D // 128
    NF = FF // 128
    HEADS, DH = 8, 32
    CH = [(0, 3), (3, 2)]
    EPS = 1e-5
    SCALE = DH ** -0.25
    WS = 64.0
    QS_ = 1024.0
    ES = 4096.0
    W = 64
    TS = 256.0
    EW = A["edge_src"].shape[1]
    EI = EW // (L * G)
    NP_ = EI // 2
    SLOTS = 5
    EX = A["L0_ffn_w1"].shape[0]
    C = -(-5 * N // (4 * EX))
    CT_ = 124
    NCT = -(-C // CT_)
    CP = CT_ * NCT
    RW = 2 * D + 2
    BIG = 1.0e6
    ZD = EX * CP // (2 * CT_)
    assert T * P == N and G * TG == T and EI * L * G == EW and CP <= 512

    ctx = ExitStack()
    with ctx:
        def sb(name, shape, dt):
            return ctx.enter_context(nc.sbuf_tensor(name, shape, dt))

        def pb(name):
            return ctx.enter_context(nc.psum_tensor(name, [128, 512], f32))

        def sem(name):
            return ctx.enter_context(nc.semaphore(name))

        X = sb("X", [P, T, D], f32)
        ZB = sb("ZB", [128, T * RW], f16)
        Z1H = ZB[:, 0:KD * N].rearrange("p (k n) -> p k n", k=KD)
        Z1L = ZB[:, KD * N:2 * KD * N].rearrange("p (k n) -> p k n", k=KD)
        ROW = ZB[0:P, :].rearrange("p (t n) -> p t n", t=T)
        ROWI = ZB[0:P, :].bitcast(i32).rearrange("p (t n) -> p t n", t=T)
        NWIN = -(-N // W)
        NW = NWIN * W
        AB = sb("AB", [128, T * D], f32)
        AGG = AB[:, 0:KD * NW].rearrange("p (k n) -> p k n", k=KD)
        SWE = AB[:, 0:2 * KD * FF].rearrange("p (b n) -> p b n", b=2)
        YG = AB[0:P, :].rearrange("p (t d) -> p t d", t=T)
        SW = sb("SW", [128, KD * FF], f32)
        GB = sb("GB", [128, SLOTS, 2, 2 * D], f16)
        OH = sb("OH", [128, EI, W], f16)
        EIX = sb("EIX", [128, EW], i32)
        REL = sb("REL", [128, EW], f32)
        MIS = sb("MIS", [128, EW], f32)
        slot = lambda n, dt: GB[:, n, :, :].rearrange("p i n -> p (i n)").bitcast(dt)
        EDI = slot(0, i32)[:, 0:EW]
        EDF = slot(1, f32)[:, 0:EW]
        EDT = slot(2, f32)[:, 0:EW]
        EHI = slot(3, f32)[:, 0:EW]
        BSF = slot(4, f32)[:, 0:EW // 2]
        IB = sb("IB", [128, EI], i32)
        BASE = sb("BASE", [128, EW // 2], i32)
        DNT = sb("DNT", [P, 3, T], f32)
        DNI = sb("DNI", [P, T], i32)
        DT = sb("DT", [P, T], f32)
        DO = sb("DO", [P, T], f32)
        ZN = sb("ZN", [P, TG, D], f32)
        ZN2 = sb("ZN2", [P, TG, D], f32)
        Z2B = sb("Z2B", [128, 2 * KD * NG], f16)
        Z2H = Z2B[:, 0:KD * NG].rearrange("p (k n) -> p k n", k=KD)
        Z2L = Z2B[:, KD * NG:2 * KD * NG].rearrange("p (k n) -> p k n", k=KD)
        SKV = sb("SKV", [128, KD, 2, D], f32)
        SQO = sb("SQO", [128, 2, KD, D], f32)
        KVH = sb("KVH", [128, KD, 2, D], f16)
        KVL = sb("KVL", [128, KD, 2, D], f16)
        QOH = sb("QOH", [128, 2, KD, D], f16)
        QOL = sb("QOL", [128, 2, KD, D], f16)
        W1H = sb("W1H", [128, KD, FF], f16)
        W1L = sb("W1L", [128, KD, FF], f16)
        W2H = sb("W2H", [128, NF, D], f16)
        W2L = sb("W2L", [128, NF, D], f16)
        VEC = sb("VEC", [128, 4 * KD + NF], f32)
        LNP = VEC[:, 0:4 * KD].rearrange("p (n k) -> p n k", n=4)
        B1F = VEC[:, 4 * KD:4 * KD + NF]
        G64 = sb("G64", [128, 2, KD], f32)
        B2 = sb("B2", [128, KD, 2], f32)
        B1C = sb("B1C", [128, NF], f32)
        BR = sb("BR", [2, 2, D], f32)
        BV = sb("BV", [128, KD, 2], f32)
        RF = sb("RF", [2, 3, D], f32)
        RT = sb("RT", [2, 3, D], f16)
        RM = sb("RM", [2, 3, D], f16)
        RB = sb("RB", [2, 3, D], f16)
        LOW = sb("LOW", [2, 1], f32)
        ONE = sb("ONE", [2, 2, 128], f16)
        ZR = sb("ZR", [1, 512], f16)
        ID = sb("ID", [128, 128], f32)
        IDH = sb("IDH", [128, 128], f16)
        BM = sb("BM", [128, 128], f32)
        KM = sb("KM", [128, KD, 2 * G], f32)
        KX = sb("KX", [128, KD], f32)
        KR = sb("KR", [1, D], f16)
        VH = sb("VH", [P, 2, KD, 130], f16)
        VL = sb("VL", [P, 2, KD, 130], f16)
        RS = sb("RS", [128, KD], f32)
        CN = sb("CN", [128, KD, 128], f32)
        CTH = sb("CTH", [128, KD, 128], f16)
        CTL = sb("CTL", [128, KD, 128], f16)
        CWH = sb("CWH", [128, KD, D], f16)
        CWL = sb("CWL", [128, KD, D], f16)
        QM = sb("QM", [P, TG, HEADS], f32)
        QS = sb("QS", [P, TG, D], f32)
        EF = QS[:, 0:2, :]
        EH = QS[:, 2, :].bitcast(f16).rearrange("p (b d) -> p b d", b=2)
        EL = QS[:, 3, :].bitcast(f16).rearrange("p (b d) -> p b d", b=2)
        QR = sb("QR", [P, TG * HEADS], f32)
        QTB = sb("QTB", [128, 2 * KD * NG], f16)
        QTH = QTB[:, 0:KD * NG].rearrange("p (k n) -> p k n", k=KD)
        QTL = QTB[:, KD * NG:2 * KD * NG].rearrange("p (k n) -> p k n", k=KD)
        HF = sb("HF", [128, 2, CP], f32)
        HHB = sb("HHB", [128, NF * NG], f16)
        HH = HHB[:, :].rearrange("p (f n) -> p f n", f=NF)
        HL = sb("HL", [128, NF, NG], f16)
        HB = EI
        SW2 = HHB[:, :].bitcast(f32)[:, 0:NF * D]
        OHL = HHB[:, :].rearrange("p (b i n) -> p b i n", b=2, n=P)
        OHH = HL[:, :, :].rearrange("p a n -> p (a n)")[:, 0:2 * HB * T].rearrange("p (b i n) -> p b i n", b=2, n=T)
        TH = HHB[0:P, 0:TG * 2 * D].rearrange("p (j n) -> p j n", j=TG)
        IOTA = sb("IOTA", [128, 128], f16)
        IOC = sb("IOC", [P, EX], f32)
        IOE = sb("IOE", [P, EX], f32)
        TRI = sb("TRI", [P, P], f16)
        ON1 = sb("ON1", [P, P], f16)
        ONF = sb("ONF", [1, P], f32)
        GBR = sb("GBR", [1, EX], f32)
        GNW = SW[:, 0:KD * D].rearrange("p (k n) -> p k n", k=KD)
        GNB = SW[0:P, KD * D:(KD + 1) * D]
        GW = SW[:, (KD + 1) * D:(KD + 1) * D + KD * EX].rearrange("p (k n) -> p k n", k=KD)
        SKF = SKV[:, :, :, :].rearrange("p k a d -> p (k a d)")
        lg = lambda n: SKF[0:P, n * T * EX:(n + 1) * T * EX].rearrange("p (t e) -> p t e", e=EX)
        LG, L1, L2 = lg(0), lg(1), lg(2)
        OE = sb("OE", [P, T, EX], f16)
        R1 = sb("R1", [P, 6, T], f32)
        SIX = sb("SIX", [P, T], i32)
        MW = sb("MW", [128, 1], f32)
        FL1 = sb("FL1", [128, 1], f32)
        FLG = sb("FLG", [128, 1], f32)
        FLI = sb("FLI", [128, 1], i32)
        GIX = sb("GIX", [P, T], i32)
        ST = sb("ST", [P, TG, 6], f32)
        MV = sb("MV", [P, TG, 2], f32)
        NT = sb("NT", [P, 3, TG], f32)
        PAD = sb("PAD", [P, 2], f32)
        PPAD = sb("PPAD", [128, 2 + NP_], f32)
        NI = sb("NI", [P, TG], i32)

        TAB = nc.dram_tensor("node_table", (N, 2 * D), f16).ap()
        BUF = nc.dram_tensor("dispatched", (EX * CP, RW // 2), i32).ap()
        YD = nc.dram_tensor("expert_out", (EX * CP, D), f32).ap()

        PT = [pb("PT0"), pb("PT1")]
        PA = [pb("PA0"), pb("PA1")]
        PH = [pb("PH0"), pb("PH1")]
        PC = [pb("PC0"), pb("PC1")]

        EFT = KVH[:, :, :, :].rearrange("p k a d -> p (k a d)").bitcast(f32)[:, 0:4 * P].rearrange("p (b n) -> p b n", b=2)
        BSI = QTB[0:CT_, :].bitcast(i32)[:, 0:NCT * RW // 2].rearrange("p (j n) -> p j n", j=NCT)
        BS = QTB[0:CT_, 0:NCT * RW].rearrange("p (j n) -> p j n", j=NCT)
        BTH = Z2B[:, 0:KD * CP].rearrange("p (k n) -> p k n", k=KD)
        BTL = Z2B[:, KD * CP:2 * KD * CP].rearrange("p (k n) -> p k n", k=KD)
        YV = ZN[0:CT_, 0:NCT, :]
        YC = QS[0:CT_, 0:NCT, :]
        YR = ZN2[0:CT_, 0:NCT, :]
        YF = SQO[0:CT_, :, :, :].rearrange("p a k d -> p (a k) d")
        YE = SKV[0:CT_, :, :, :].rearrange("p a k d -> p (a k) d")
        x_in = sem("x_in")
        const_done = sem("const_done")
        pool_chain = sem("pool_chain")
        kv_in = sem("kv_in")
        qo_in = sem("qo_in")
        ff_in = sem("ff_in")
        ln_in = sem("ln_in")
        stage_free = sem("stage_free")
        lnp_done = sem("lnp_done")
        whi_done = sem("whi_done")
        wlo_done = sem("wlo_done")
        bq_mm = sem("bq_mm")
        bv_mm = sem("bv_mm")
        b1_mm = sem("b1_mm")
        bo_mm = sem("bo_mm")
        bv_done = sem("bv_done")
        rows_done = sem("rows_done")
        rt_done = sem("rt_done")
        z1_done = sem("z1_done")
        t1_mm = sem("t1_mm")
        t1_hi = sem("t1_hi")
        t1_lo = sem("t1_lo")
        km_mm = sem("km_mm")
        km_read = sem("km_read")
        kx_done = sem("kx_done")
        kr_mm = sem("kr_mm")
        kr_done = sem("kr_done")
        kv_mm = sem("kv_mm")
        exp_done = sem("exp_done")
        vh_done = sem("vh_done")
        vl_done = sem("vl_done")
        el_done = sem("el_done")
        ctx_mm = sem("ctx_mm")
        edges_in = sem("edges_in")
        gin = [sem(f"gathered_{i}") for i in range(SLOTS)]
        hist_oh = sem("hist_oh")
        hist_mm = sem("hist_mm")
        deg_mm = sem("deg_mm")
        xs_done = sem("xs_done")
        xt_mm = sem("xt_mm")
        agg_init = sem("agg_init")
        th_done = sem("th_done")
        tl_done = sem("tl_done")
        tab_out = [sem("tab_out0"), sem("tab_out1")]
        d_edge = sem("d_edge")
        neg_done = sem("neg_done")
        par_done = sem("par_done")
        base_done = sem("base_done")
        miss_idx = sem("miss_idx")
        miss_in = sem("miss_in")
        miss_col = sem("miss_col")
        miss_oh = sem("miss_oh")
        miss_mm = sem("miss_mm")
        miss_added = sem("miss_added")
        idx_copied = sem("idx_copied")
        oh_done = sem("oh_done")
        pair_mm = sem("pair_mm")
        agg_done = sem("agg_done")
        late_in = sem("late_in")
        xr_in = sem("xr_in")
        gn_mm = sem("gn_mm")
        gn_read = sem("gn_read")
        gn_done = sem("gn_done")
        xt_done = sem("xt_done")
        zf_done = sem("zf_done")
        tf_mm = sem("tf_mm")
        tf_done = sem("tf_done")
        lg_mm = sem("lg_mm")
        lg_read = sem("lg_read")
        row_hi = sem("row_hi")
        row_done = sem("row_done")
        top_done = sem("top_done")
        es_done = sem("es_done")
        oe_done = sem("oe_done")
        pos_mm = sem("pos_mm")
        route_done = sem("route_done")
        d_fin = sem("d_fin")
        d_route = sem("d_route")
        zero_in = sem("zero_in")
        scattered = sem("scattered")
        slot_in = sem("slot_in")
        ew_in = sem("ew_in")
        ev_in = sem("ev_in")
        estage_free = sem("estage_free")
        ehi_done = sem("ehi_done")
        elo_done = sem("elo_done")
        ebias_done = sem("ebias_done")
        et_mm = sem("et_mm")
        bt_hi = sem("bt_hi")
        bt_lo = sem("bt_lo")
        e1_mm = sem("e1_mm")
        er_done = sem("er_done")
        eh_done = sem("eh_done")
        ehl_done = sem("ehl_done")
        ey_mm = sem("ey_mm")
        ey_read = sem("ey_read")
        ey_clean = sem("ey_clean")
        ey_out = sem("ey_out")
        d_exp = sem("d_exp")
        back_in = [sem(f"back_in{i}") for i in range(G)]
        fin_done = sem("fin_done")
        ctx_end = sem("ctx_end")
        cn_done = sem("cn_done")
        ct_mm = sem("ct_mm")
        ct_hi = sem("ct_hi")
        ct_lo = sem("ct_lo")
        cw_mm = sem("cw_mm")
        cw_hi = sem("cw_hi")
        cw_lo = sem("cw_lo")
        q_mm = sem("q_mm")
        q_read = sem("q_read")
        qe_done = sem("qe_done")
        qn_done = sem("qn_done")
        tq_mm = sem("tq_mm")
        tq_hi = sem("tq_hi")
        tq_lo = sem("tq_lo")
        at_mm = sem("at_mm")
        x1_done = sem("x1_done")
        z2_done = sem("z2_done")
        t2_mm = sem("t2_mm")
        t2_hi = sem("t2_hi")
        t2_lo = sem("t2_lo")
        f1_mm = sem("f1_mm")
        gelu_done = sem("gelu_done")
        hh_done = sem("hh_done")
        hl_done = sem("hl_done")
        y_mm = sem("y_mm")
        x2_done = sem("x2_done")
        d_head = sem("d_head")
        d_prep = sem("d_prep")
        d_ln1 = sem("d_ln1")
        d_ln2 = sem("d_ln2")
        d_kv = sem("d_kv")
        d_mid = sem("d_mid")
        d_q = sem("d_q")
        out_done = sem("out_done")

        block = ctx.enter_context(nc.Block())

        class Chain:

            def __init__(self, eng, s, r, n):
                self.eng, self.s, self.base, self.n, self.k = eng, s, r * n, n, 0

            def __call__(self, ins):
                self.k += 1
                ins.then_inc(self.s, 1)
                self.eng.wait_ge(self.s, self.base + self.k)

            def end(self):
                assert self.k == self.n, self.k

        def halves(b):
            return b.rearrange("p (k c) -> p k c", k=KD)

        x_t = A["x"].rearrange("(t p) d -> p t d", p=P)
        o_t = out.rearrange("(t p) d -> p t d", p=P)

        @block.sync
        def _(sp):
            for n in range(G):
                sp.dma_start(X[:, n * TG:(n + 1) * TG, :], x_t[:, n * TG:(n + 1) * TG, :]).then_inc(x_in, 16)
            sp.dma_start(EDI, A["edge_dst"]).then_inc(edges_in, 16)
            sp.dma_start(EIX[:, :], A["edge_src"]).then_inc(edges_in, 16)

            with sp.Fori(0, L) as l:
                sp.wait_ge(stage_free, l * 3 + 3)
                w = lambda n: A["L0_mix_" + n][ds(l, 1), :, :].rearrange("a (k p) n -> p (a k) n", p=128)
                sp.dma_start(SKV[:, :, 0, :], w("Wk")).then_inc(kv_in, 16)
                sp.dma_start(SKV[:, :, 1, :], w("Wv")).then_inc(kv_in, 16)
                sp.dma_start(VEC[:, :], A["mix_vec"][ds(l, 1), :, :].rearrange("a p n -> (a p) n")).then_inc(ln_in, 16)
                sp.dma_start(BR[:, :, :], A["mix_rows"][ds(l, 1), :, :, :].rearrange("a r n d -> (a r) n d")).then_inc(ln_in, 16)
                sp.dma_start(SQO[:, 0, :, :], w("Wq")).then_inc(qo_in, 16)
                sp.dma_start(SQO[:, 1, :, :], w("Wo")).then_inc(qo_in, 16)
                sp.dma_start(SW[:, :].rearrange("p (k n) -> p k n", k=KD), w("W1")).then_inc(ff_in, 16)
                for b in range(2):
                    sp.wait_ge(tab_out[b], 16 * (3 - b))
                sp.wait_ge(y_mm, l * T + 1)
                sp.dma_start(SW2.rearrange("p (k n) -> p k n", k=NF), w("W2")).then_inc(ff_in, 16)
            sp.wait_ge(y_mm, L * T + 1)
            for n, (dst, src) in enumerate(((GNW, A["L0_gnn_W"].rearrange("(k p) n -> p k n", p=128)),
                                            (GW, A["L0_ffn_gate_w"].rearrange("(k p) n -> p k n", p=128)),
                                            (GBR[:, :], A["L0_ffn_gate_b"].rearrange("(a n) -> a n", a=1)),
                                            (GNB, A["gnn_bias"]))):
                sp.dma_start(dst, src).then_inc(late_in, 16)
            for g in range(G):
                if g >= 1:
                    sp.wait_ge(xt_done, g * TG)
                sp.dma_start(QS[:, :, :], x_t[:, g * TG:(g + 1) * TG, :]).then_inc(xr_in, 16)

            sp.sem_inc(ey_out, 16)
            rows = lambda ap, e: ap[ds(e * CP, CP), :].rearrange("(j p) n -> p j n", p=CT_)
            with sp.Fori(0, EX) as e:
                sp.wait_ge(estage_free, e * 2 + 2)
                sp.dma_start(SWE[:, 0, :].rearrange("p (k n) -> p k n", k=KD),
                             A["L0_ffn_w1"][ds(e, 1), :, :].rearrange("a (k p) n -> p (a k) n", p=128)).then_inc(ew_in, 16)
                sp.dma_start(SWE[:, 1, :].rearrange("p (k n) -> p k n", k=NF),
                             A["L0_ffn_w2"][ds(e, 1), :, :].rearrange("a (k p) n -> p (a k) n", p=128)).then_inc(ew_in, 16)
                sp.dma_start(B1C[:, :], A["ffn_vec"][ds(e, 1), :, :].rearrange("a p n -> (a p) n")).then_inc(ev_in, 16)
                sp.dma_start(BR[:, 1, :], A["ffn_rows"][ds(e, 1), :, :].rearrange("a r d -> (a r) d")).then_inc(ev_in, 16)
                sp.wait_ge(scattered, 16 * T)
                sp.dma_start(BSI, rows(BUF, e)).then_inc(slot_in, 16)
                sp.wait_ge(ey_clean, e + 1)
                sp.dma_start(rows(YD, e), YR).then_inc(ey_out, 16)
            for g in range(G):
                sp.wait_ge(fin_done, (g + 1) * TG)
                sp.dma_start(o_t[:, g * TG:(g + 1) * TG, :], X[:, g * TG:(g + 1) * TG, :]).then_inc(out_done, 16)
            sp.wait_ge(out_done, 16 * G)

        @block.gpsimd
        def _(pool):
            n = [0]

            def step(ins):
                n[0] += 1
                ins.then_inc(pool_chain, 1)
                pool.wait_ge(pool_chain, n[0])

            step(pool.memset(ID[:, :], 0.0))
            step(pool.memset(IDH[:, :], 0.0))
            step(pool.affine_select(out=IDH[:, :], in_=IDH[:, :], compare_op=ALU.not_equal, fill=1.0, base=0,
                                    pattern=[[-1, 128]], channel_multiplier=1))
            step(pool.affine_select(out=ID[:, :], in_=ID[:, :], compare_op=ALU.not_equal, fill=1.0, base=0,
                                    pattern=[[-1, 128]], channel_multiplier=1))
            step(pool.memset(BM[:, :], 1.0))
            bm = BM[:, :].rearrange("p (h c) -> p h c", h=128 // DH)
            step(pool.affine_select(out=bm, in_=bm, compare_op=ALU.is_ge, fill=0.0, base=0,
                                    pattern=[[-DH, 128 // DH], [0, DH]], channel_multiplier=1))
            step(pool.affine_select(out=bm, in_=bm, compare_op=ALU.is_ge, fill=0.0, base=DH - 1,
                                    pattern=[[DH, 128 // DH], [0, DH]], channel_multiplier=-1))
            step(pool.memset(LOW[:, :], 0.0))
            step(pool.affine_select(out=LOW[:, :], in_=LOW[:, :], compare_op=ALU.not_equal, fill=1.0, base=-1,
                                    pattern=[[0, 1]], channel_multiplier=1))
            step(pool.memset(ONE[:, 0, :], 1.0))
            step(pool.memset(ONE[:, 1, :], QS_))
            step(pool.memset(ZR[:, :], 0.0))
            step(pool.memset(PPAD[:, :], 0.0))
            step(pool.memset(VH[:, :, :, 128:130], 1.0))
            step(pool.memset(VL[:, :, :, 128:130], 0.0))
            step(pool.iota(IOTA[:, :], [[1, 128]], base=0, channel_multiplier=0, allow_small_or_imprecise_dtypes=True))
            step(pool.iota(IOC[:, :], [[-1, EX]], base=EX, channel_multiplier=0, allow_small_or_imprecise_dtypes=True))
            step(pool.iota(IOE[:, :], [[CP, EX]], base=0, channel_multiplier=0, allow_small_or_imprecise_dtypes=True))
            step(pool.memset(ON1[:, :], 1.0))
            step(pool.memset(ONF[:, :], 1.0))
            step(pool.memset(AGG[:, :, N:NW], 0.0))
            step(pool.memset(TRI[:, :], 1.0))
            step(pool.affine_select(out=TRI[:, :], in_=TRI[:, :], compare_op=ALU.is_ge, fill=0.0, base=0,
                                    pattern=[[1, P]], channel_multiplier=-1))
            pool.memset(OH[:, :, :], 0.0).then_inc(const_done, 1)
            pool.wait_ge(const_done, 1)
            zero = OH[0:CT_, :, :].rearrange("p i n -> p (i n)").bitcast(i32)[:, 0:RW]
            for n in range(ZD):
                pool.dma_start(BUF[n * 2 * CT_:(n + 1) * 2 * CT_, :].rearrange("(p j) n -> p (j n)", j=2), zero).then_inc(zero_in, 16)

            pool.wait_ge(neg_done, 1)
            pool.partition_all_reduce(EDF, MIS[:, :], 128, RMAX).then_inc(par_done, 1)
            pool.wait_ge(neg_done, 2)
            pool.partition_all_reduce(FLG[:, :], FL1[:, :], 128, RMAX).then_inc(par_done, 1)

            pool.wait_ge(edges_in, 32)
            for b in range(2):
                pool.wait_ge(tab_out[b], 16 * (3 - b))
            with pool.Fori(0, L * G) as it:
                for b in range(NP_ // SLOTS):
                    pool.wait_ge(pair_mm, it * NP_ + b * SLOTS + 1)
                    cols = 2 * SLOTS
                    pool.tensor_copy(IB[:, b * cols:(b + 1) * cols], EIX[:, ds(it * EI + b * cols, cols)]).then_inc(idx_copied, 1)
                    pool.wait_ge(idx_copied, it * (NP_ // SLOTS) + b + 1)
                    for s in range(SLOTS):
                        q = b * SLOTS + s
                        pool.wait_ge(pair_mm, it * NP_ + q + 2)
                        pool.tensor_tensor(PPAD[:, 2 + q:3 + q], PPAD[:, 0:1], PPAD[:, 1:2], ALU.add)
                        for i in range(2):
                            pool.indirect_dma_start(
                                out=GB[:, s, i, :], out_offset=None, in_=TAB,
                                in_offset=bass.IndirectOffsetOnAxis(ap=IB[:, 2 * q + i:2 * q + i + 1], axis=0),
                            ).then_inc(gin[s], 16)

            with some_missed(pool, FLI[0:1, 0:1], base_done):
                pool.sem_inc(miss_mm, 1)
                with pool.Fori(0, EW) as t:
                    pool.wait_ge(miss_mm, t * NWIN + 1)
                    pool.tensor_copy(IB[:, 0:1], EIX[:, ds(t, 1)]).then_inc(miss_idx, 1)
                    pool.wait_ge(miss_idx, t + 1)
                    pool.tensor_tensor(PPAD[:, 2:3], PPAD[:, 0:1], PPAD[:, 1:2], ALU.add)
                    pool.indirect_dma_start(out=GB[:, 0, 0, :], out_offset=None, in_=TAB,
                                            in_offset=bass.IndirectOffsetOnAxis(ap=IB[:, 0:1], axis=0)).then_inc(miss_in, 16)

            pool.wait_ge(route_done, 1)
            pool.wait_ge(row_done, T)
            pool.wait_ge(zero_in, 16 * ZD)
            for t in range(T):
                pool.indirect_dma_start(out=BUF, out_offset=bass.IndirectOffsetOnAxis(ap=SIX[:, t:t + 1], axis=0),
                                        in_=ROWI[:, t, :], in_offset=None, bounds_check=EX * CP - 1,
                                        oob_is_err=False).then_inc(scattered, 16)
            pool.wait_ge(ey_out, 16 * EX + 16)
            pool.wait_ge(route_done, 2)
            for t in range(T):
                pool.indirect_dma_start(out=YG[:, t, :], out_offset=None, in_=YD,
                                        in_offset=bass.IndirectOffsetOnAxis(ap=GIX[:, t:t + 1], axis=0)).then_inc(back_in[t // TG], 16)

        @block.scalar
        def _(act):
            def hi_split(l):
                act.wait_ge(y_mm, l * T + 1)
                act.wait_ge(lnp_done, l * 3 + 1)
                act.wait_ge(kv_in, (l + 1) * 32)
                for k in range(KD):
                    act.activation(KVH[:, k, :, :], SKV[:, k, :, :], ACT.Copy, scale=G64[:, 0, k:k + 1]).then_inc(whi_done, 1)
                act.wait_ge(qo_in, (l + 1) * 32)
                for k in range(KD):
                    act.activation(QOH[:, 0, k, :], SQO[:, 0, k, :], ACT.Copy, scale=G64[:, 0, k:k + 1]).then_inc(whi_done, 1)
                act.activation(QOH[:, 1, :, :], SQO[:, 1, :, :], ACT.Copy, scale=WS).then_inc(whi_done, 1)
                act.wait_ge(ff_in, (l + 1) * 32)
                for k in range(KD):
                    act.activation(W1H[:, k, :], SW[:, k * FF:(k + 1) * FF], ACT.Copy, scale=G64[:, 1, k:k + 1]).then_inc(whi_done, 1)
                act.activation(W2H[:, :, :], SW2.rearrange("p (k n) -> p k n", k=NF), ACT.Copy, scale=WS).then_inc(whi_done, 1)

            def ln1_hi(l, g, it):
                for j in range(TG):
                    act.wait_ge(t1_mm, it * TG + j + 1)
                    act.activation(Z1H[:, :, ds((g * TG + j) * P, P)], halves(PT[j % 2][:, 0:2 * P]),
                                   ACT.Copy).then_inc(t1_hi, 1)

            def head(l):
                act.wait_ge(kr_mm, l + 1)
                act.activation(KR[:, :], PA[0][0:1, 0:D], ACT.Copy, scale=-1.0).then_inc(kr_done, 1)

            def kv(l, g, it):
                for j in range(TG):
                    n = it * TG + j
                    act.wait_ge(kv_mm, n + 1)
                    act.wait_ge(el_done, n + 1 + (j == 0))
                    act.activation(EF[:, j % 2, :], PA[j % 2][0:P, 0:D], ACT.Exp, scale=SCALE / WS).then_inc(exp_done, 1)
                    act.wait_ge(ctx_mm, n + 1 + (j == 0))
                    act.activation(VH[:, j % 2, :, 0:128], halves(PA[j % 2][0:P, D:2 * D]), ACT.Copy,
                                   scale=1.0 / WS).then_inc(vh_done, 1)

            def mid(l):
                act.wait_ge(ct_mm, l + 1)
                act.activation(CTH[:, :, :], halves(PT[0][:, 0:D]), ACT.Copy).then_inc(ct_hi, 1)
                for h in range(KD):
                    act.wait_ge(cw_mm, l * KD + h + 1)
                    act.activation(CWH[:, h, :], PA[h][:, 0:D], ACT.Copy).then_inc(cw_hi, 1)

            def attn(l, g, it):
                act.wait_ge(q_read, (it + 1) * TG)
                act.activation(QS[:, :, :], QS[:, :, :], ACT.Exp, scale=SCALE / WS).then_inc(qe_done, 1)
                for j in range(TG):
                    act.wait_ge(tq_mm, it * TG + j + 1)
                    act.activation(QTH[:, :, j * P:(j + 1) * P], halves(PT[j % 2][:, 0:2 * P]), ACT.Copy,
                                   scale=QS_).then_inc(tq_hi, 1)
                for j in range(TG):
                    act.wait_ge(t2_mm, it * TG + j + 1)
                    act.activation(Z2H[:, :, j * P:(j + 1) * P], halves(PT[j % 2][:, 0:2 * P]),
                                   ACT.Copy).then_inc(t2_hi, 1)

            def ffn(l, g, it):
                u = 0
                act.wait_ge(y_mm, it * TG + 1)
                for c, (t0, tn) in enumerate(CH):
                    for f in range(NF):
                        n = it * 2 * NF + u
                        act.wait_ge(f1_mm, n + 1)
                        act.wait_ge(hl_done, n + 1)
                        act.activation(HF[:, u % 2, 0:tn * P], PH[u % 2][:, 0:tn * P], ACT.Gelu, scale=1.0 / WS,
                                       bias=B1C[:, f:f + 1]).then_inc(gelu_done, 1)
                        act.wait_ge(gelu_done, n + 1)
                        act.activation(HH[:, f, t0 * P:(t0 + tn) * P], HF[:, u % 2, 0:tn * P], ACT.Copy).then_inc(hh_done, 1)
                        u += 1

            for g in range(G):
                if g >= 1:
                    act.wait_ge(tab_out[(g - 1) % 2], 16 * ((g - 1) // 2 + 1))
                act.wait_ge(deg_mm, 1)
                act.wait_ge(xs_done, (g + 1) * TG)
                act.activation(TH[:, :, 0:D], ZN[:, :, :], ACT.Copy).then_inc(th_done, 1)
                for j in range(TG):
                    t = g * TG + j
                    act.wait_ge(xt_mm, t + 1)
                    act.activation(AGG[:, :, t * P:(t + 1) * P], halves(PT[j % 2][:, 0:2 * P]), ACT.Copy).then_inc(agg_init, 1)
                act.wait_ge(tl_done, g + 1)
                act.dma_start(TAB.rearrange("(t p) n -> p t n", p=P)[:, g * TG:(g + 1) * TG, :],
                              TH).then_inc(tab_out[g % 2], 16)
            act.wait_ge(tab_out[0], 48)
            with act.Fori(0, L) as l:
                hi_split(l)
                with act.Fori(0, G) as g:
                    ln1_hi(l, g, l * G + g)
                head(l)
                with act.Fori(0, G) as g:
                    kv(l, g, l * G + g)
                mid(l)
                with act.Fori(0, G) as g:
                    attn(l, g, l * G + g)
                    ffn(l, g, l * G + g)

            for g in range(G):
                act.wait_ge(zf_done, (g + 1) * TG)
                act.activation(ROW[:, g * TG:(g + 1) * TG, 0:D], ZN[:, :, :], ACT.Copy).then_inc(row_hi, 1)
                for j in range(TG):
                    t = g * TG + j
                    act.wait_ge(tf_mm, t + 1)
                    if t >= 2:
                        act.wait_ge(lg_mm, t - 1)
                    act.activation(EFT[:, j % 2, :], PT[j % 2][:, 0:2 * P], ACT.Copy).then_inc(tf_done, 1)
            act.wait_ge(top_done, 1)
            act.activation(L2, L2, ACT.Exp).then_inc(es_done, 1)

            with act.Fori(0, EX) as e:
                act.wait_ge(ey_mm, e * NCT + 1)
                act.wait_ge(ew_in, (e + 1) * 32)
                act.activation(W1H[:, :, :], SWE[:, 0, :].rearrange("p (k n) -> p k n", k=KD), ACT.Copy, scale=WS).then_inc(ehi_done, 1)
                act.activation(W2H[:, :, :], SWE[:, 1, :].rearrange("p (k n) -> p k n", k=NF), ACT.Copy, scale=WS).then_inc(ehi_done, 1)
                act.wait_ge(et_mm, e * 2 + 1)
                act.activation(BTH, PT[0][:, :].bitcast(f16)[:, 0:KD * CP].rearrange("p (k n) -> p k n", k=KD), ACT.Copy).then_inc(bt_hi, 1)
                for f in range(NF):
                    n = e * NF + f
                    act.wait_ge(e1_mm, n + 1)
                    act.wait_ge(ehl_done, n + 1)
                    act.activation(HF[:, f % 2, :], PH[f % 2][:, 0:CP], ACT.Relu, scale=1.0 / WS, bias=B1C[:, f:f + 1]).then_inc(er_done, 1)
                    act.wait_ge(er_done, n + 1)
                    act.activation(HH[:, f, 0:CP], HF[:, f % 2, :], ACT.Copy).then_inc(eh_done, 1)

        @block.vector
        def _(dve):
            dve.sem_inc(stage_free, 3)
            dve.sem_inc(el_done, 2)
            dve.sem_inc(hl_done, 2)

            def newton(ch, var, add, nt, ni):
                s = lambda n: nt[:, n, :]
                ch(dve.tensor_scalar(s(1), var, add, None, ALU.add))
                ch(dve.tensor_scalar(ni[:, :], s(1).bitcast(i32), 1, None, ALU.logical_shift_right))
                ch(dve.tensor_scalar(s(0).bitcast(i32), ni[:, :], -1.0, float(0x5f3759df), ALU.mult, ALU.add))
                for _ in range(3):
                    ch(dve.tensor_tensor(s(2), s(0), s(0), ALU.mult))
                    ch(dve.scalar_tensor_tensor(s(2), s(2), -0.5, s(1), ALU.mult, ALU.mult))
                    ch(dve.scalar_tensor_tensor(s(0), s(2), 1.5, s(0), ALU.add, ALU.mult))

            NEWTON = 12
            LN = NEWTON + 2

            def norm(ch, tiles, dst, done):
                dve.memset(PAD[:, 0:1], 0.0)
                for j, t in enumerate(tiles):
                    ins = dve.bn_stats(ST[:, j, :], t)
                ch(ins)
                dve.memset(PAD[:, 1:2], 0.0)
                for j in range(TG):
                    ins = dve.bn_aggr(MV[:, j, :], ST[:, j, :])
                ch(ins)
                newton(ch, MV[:, :, 1], EPS, NT, NI)
                for j, t in enumerate(tiles):
                    dve.tensor_scalar(dst(j), t, MV[:, j, 0:1], NT[:, 0, j:j + 1], ALU.subtract, ALU.mult).then_inc(done, 1)

            def tile(g, j):
                return X[:, ds(g * TG + j, 1), :].rearrange("p a d -> p (a d)")

            def prep(l):
                ch = Chain(dve, d_prep, l, 6)
                dve.wait_ge(x2_done, l * T + 1)
                dve.wait_ge(ln_in, (l + 1) * 32)
                dve.tensor_scalar(G64[:, 0, :], LNP[:, 0, :], WS, None, ALU.mult)
                ins = dve.tensor_scalar(G64[:, 1, :], LNP[:, 2, :], WS, None, ALU.mult)
                ins.then_inc(lnp_done, 1)
                for r in range(2):
                    dve.tensor_copy(B2[:, :, r], LNP[:, 1, :]).then_inc(lnp_done, 1)
                dve.wait_ge(lnp_done, l * 3 + 3)
                n = l * 8
                for k in range(KD):
                    dve.wait_ge(whi_done, n + 1 + k)
                    dve.scalar_tensor_tensor(KVL[:, k, :, :], SKV[:, k, :, :], G64[:, 0, k:k + 1], KVH[:, k, :, :],
                                             ALU.mult, ALU.subtract).then_inc(wlo_done, 1)
                for k in range(KD):
                    dve.wait_ge(whi_done, n + 3 + k)
                    dve.scalar_tensor_tensor(QOL[:, 0, k, :], SQO[:, 0, k, :], G64[:, 0, k:k + 1], QOH[:, 0, k, :],
                                             ALU.mult, ALU.subtract).then_inc(wlo_done, 1)
                dve.wait_ge(whi_done, n + 5)
                dve.scalar_tensor_tensor(QOL[:, 1, :, :], SQO[:, 1, :, :], WS, QOH[:, 1, :, :],
                                         ALU.mult, ALU.subtract).then_inc(wlo_done, 1)
                for k in range(KD):
                    dve.wait_ge(whi_done, n + 6 + k)
                    dve.scalar_tensor_tensor(W1L[:, k, :], SW[:, k * FF:(k + 1) * FF], G64[:, 1, k:k + 1], W1H[:, k, :],
                                             ALU.mult, ALU.subtract).then_inc(wlo_done, 1)
                dve.wait_ge(whi_done, n + 8)
                dve.scalar_tensor_tensor(W2L[:, :, :], SW2.rearrange("p (k n) -> p k n", k=NF), WS, W2H[:, :, :],
                                         ALU.mult, ALU.subtract).then_inc(wlo_done, 1)
                dve.wait_ge(bq_mm, l + 1)
                dve.tensor_scalar(RF[:, 0, :], PA[0][0:2, 0:D], WS, None, ALU.mult).then_inc(rt_done, 1)
                dve.wait_ge(bv_mm, l + 1)
                for r in range(2):
                    ins = dve.tensor_copy(BV[:, :, r], PT[0][:, 0:KD])
                ins.then_inc(bv_done, 1)
                dve.wait_ge(b1_mm, l + 1)
                dve.tensor_tensor(B1C[:, :], PT[1][:, 0:NF], B1F, ALU.add).then_inc(rt_done, 1)
                dve.wait_ge(bo_mm, l + 1)
                ch(dve.tensor_tensor(RF[:, 1, :], PA[1][0:2, 0:D], BR[:, 0, :], ALU.add))
                ch(dve.tensor_scalar(RF[:, 1, :], RF[:, 1, :], WS, None, ALU.mult))
                ch(dve.tensor_scalar(RF[:, 2, :], BR[:, 1, :], WS, None, ALU.mult))
                dve.wait_ge(rt_done, (l + 1) * 2)
                ch(dve.tensor_copy(RT[:, :, :], RF[:, :, :]))
                ch(dve.tensor_scalar(RM[:, :, :], RT[:, :, :], LOW[:, 0:1], None, ALU.mult))
                ch(dve.tensor_tensor(RB[:, :, :], RF[:, :, :], RM[:, :, :], ALU.subtract))
                ch.end()
                dve.sem_inc(rows_done, 1)
                dve.wait_ge(wlo_done, (l + 1) * 8)
                dve.sem_inc(stage_free, 3)

            def ln1(l, g, it):
                ch = Chain(dve, d_ln1, it, LN)
                norm(ch, [tile(g, j) for j in range(TG)], lambda j: ZN[:, j, :], z1_done)
                ch.end()
                for j in range(TG):
                    dve.wait_ge(t1_hi, it * TG + j + 1)
                    cols = ds((g * TG + j) * P, P)
                    dve.tensor_tensor(Z1L[:, :, cols], halves(PT[j % 2][:, 0:2 * P]), Z1H[:, :, cols],
                                      ALU.subtract).then_inc(t1_lo, 1)
                u = 0
                for m in range(KD):
                    for c, (t0, tn) in enumerate(CH):
                        dve.wait_ge(km_mm, it * 4 + u + 1)
                        dve.tensor_reduce(KM[:, m, ds(g * 2 + c, 1)], PH[u % 2][:, 0:tn * P], AX.X,
                                          ALU.max).then_inc(km_read, 1)
                        u += 1

            def head(l):
                dve.wait_ge(km_read, (l + 1) * 4 * G + 1)
                dve.tensor_reduce(KX[:, :], KM[:, :, :], AX.X, ALU.max).then_inc(kx_done, 1)

            def kv(l, g, it):
                ch = Chain(dve, d_kv, it, TG)
                for j in range(TG):
                    n = it * TG + j
                    dve.wait_ge(exp_done, n + 1)
                    dve.wait_ge(ctx_mm, n + 1 + (j == 0))
                    ch(dve.tensor_scalar(EH[:, j % 2, :], EF[:, j % 2, :], ES, None, ALU.mult))
                    dve.scalar_tensor_tensor(EL[:, j % 2, :], EF[:, j % 2, :], ES, EH[:, j % 2, :],
                                             ALU.mult, ALU.subtract).then_inc(el_done, 1)
                    dve.wait_ge(vh_done, n + 1)
                    dve.scalar_tensor_tensor(VL[:, j % 2, :, 0:128], halves(PA[j % 2][0:P, D:2 * D]), 1.0 / WS,
                                             VH[:, j % 2, :, 0:128], ALU.mult, ALU.subtract).then_inc(vl_done, 1)
                ch.end()

            def mid(l):
                ch = Chain(dve, d_mid, l, 1)
                dve.wait_ge(ctx_end, l + 1)
                for h in range(KD):
                    ins = dve.reciprocal(RS[:, h:h + 1], PC[h][:, 128:129])
                ch(ins)
                for h in range(KD):
                    dve.scalar_tensor_tensor(CN[:, h, :], PC[h][:, 0:128], RS[:, h:h + 1], BM[:, :],
                                             ALU.mult, ALU.mult).then_inc(cn_done, 1)
                ch.end()
                dve.wait_ge(ct_hi, l + 1)
                dve.tensor_tensor(CTL[:, :, :], halves(PT[0][:, 0:D]), CTH[:, :, :], ALU.subtract).then_inc(ct_lo, 1)
                for h in range(KD):
                    dve.wait_ge(cw_hi, l * KD + h + 1)
                    dve.tensor_tensor(CWL[:, h, :], PA[h][:, 0:D], CWH[:, h, :], ALU.subtract).then_inc(cw_lo, 1)

            def attn(l, g, it):
                ch = Chain(dve, d_q, it, TG + 2)
                for j in range(TG):
                    dve.wait_ge(q_mm, it * TG + j + 1)
                    pq = PA[j % 2][0:P, 0:D].rearrange("p (h c) -> p h c", h=HEADS)
                    ch(dve.tensor_reduce(QM[:, j, :], pq, AX.X, ALU.max))
                    dve.tensor_tensor(QS[:, j, :].rearrange("p (h c) -> p h c", h=HEADS), pq,
                                      QM[:, j, :].unsqueeze(2).to_broadcast([P, HEADS, DH]), ALU.subtract).then_inc(q_read, 1)
                dve.wait_ge(qe_done, it + 1)
                qv = QS[:, :, :].rearrange("p t (h c) -> p (t h) c", h=HEADS)
                ch(dve.tensor_reduce(QR[:, :], qv, AX.X, ALU.add))
                ch(dve.reciprocal(QR[:, :], QR[:, :]))
                dve.tensor_tensor(qv, qv, QR[:, :].unsqueeze(2).to_broadcast([P, TG * HEADS, DH]), ALU.mult).then_inc(qn_done, 1)
                for j in range(TG):
                    dve.wait_ge(tq_hi, it * TG + j + 1)
                    dve.scalar_tensor_tensor(QTL[:, :, j * P:(j + 1) * P], halves(PT[j % 2][:, 0:2 * P]), QS_,
                                             QTH[:, :, j * P:(j + 1) * P], ALU.mult, ALU.subtract).then_inc(tq_lo, 1)
                for j in range(TG):
                    dve.wait_ge(at_mm, it * TG + j + 1)
                    dve.scalar_tensor_tensor(tile(g, j), PA[j % 2][0:P, 0:D], 1.0 / (WS * QS_), tile(g, j),
                                             ALU.mult, ALU.add).then_inc(x1_done, 1)
                ch.end()
                ch = Chain(dve, d_ln2, it, LN)
                dve.wait_ge(x1_done, (it + 1) * TG)
                norm(ch, [tile(g, j) for j in range(TG)], lambda j: ZN2[:, j, :], z2_done)
                ch.end()
                for j in range(TG):
                    dve.wait_ge(t2_hi, it * TG + j + 1)
                    dve.tensor_tensor(Z2L[:, :, j * P:(j + 1) * P], halves(PT[j % 2][:, 0:2 * P]),
                                      Z2H[:, :, j * P:(j + 1) * P], ALU.subtract).then_inc(t2_lo, 1)

            def ffn(l, g, it):
                u = 0
                for c, (t0, tn) in enumerate(CH):
                    for f in range(NF):
                        dve.wait_ge(hh_done, it * 2 * NF + u + 1)
                        cols = slice(t0 * P, (t0 + tn) * P)
                        dve.tensor_tensor(HL[:, f, cols], HF[:, u % 2, 0:tn * P], HH[:, f, cols],
                                          ALU.subtract).then_inc(hl_done, 1)
                        u += 1
                for j in range(TG):
                    dve.wait_ge(y_mm, it * TG + j + 2)
                    dve.scalar_tensor_tensor(tile(g, j), PA[j % 2][0:P, 0:D], 1.0 / WS, tile(g, j),
                                             ALU.mult, ALU.add).then_inc(x2_done, 1)

            def onehot(it):
                dve.wait_ge(zero_in, 16 * ZD)
                dve.wait_ge(pair_mm, it * NP_ + SLOTS + 1)
                dve.tensor_tensor(OH[:, :, :], IOTA[:, 0:W].unsqueeze(1).to_broadcast([128, EI, W]),
                                  REL[:, ds(it * EI, EI)].unsqueeze(2).to_broadcast([128, EI, W]), ALU.is_equal).then_inc(oh_done, 1)

            def collect(it):
                for q in range(NP_):
                    n = it * NP_ + q
                    dve.wait_ge(pair_mm, n + 2 + SLOTS)
                    dve.wait_ge(agg_done, n + 1)
                    first = dve.value_load(BASE[0:1, ds(n, 1)], min_val=0, max_val=NW - W)
                    o = AGG[:, :, ds(first, W)]
                    dve.tensor_tensor(o, PC[q % 2][:, 0:2 * W].rearrange("p (k n) -> p k n", k=KD), o, ALU.add).then_inc(agg_done, 1)

            dve.wait_ge(x_in, 16 * G)
            ch0 = Chain(dve, d_head, 0, LN * G)
            for g in range(G):
                norm(ch0, [X[:, g * TG + j, :] for j in range(TG)], lambda j: X[:, g * TG + j, :], z1_done)
            ch0.end()
            dve.wait_ge(z1_done, T)

            ce = Chain(dve, d_edge, 0, 17)
            dve.wait_ge(edges_in, 32)
            ce(dve.tensor_copy(EDF, EDI))
            ce(dve.tensor_scalar(REL[:, :], EDF, 0.0, -BIG, ALU.is_lt, ALU.mult))
            dve.tensor_tensor(MIS[:, :], REL[:, :], EDF, ALU.subtract).then_inc(neg_done, 1)
            dve.wait_ge(par_done, 1)
            low = EDF.rearrange("p (q i) -> p q i", i=2)
            ce(dve.tensor_tensor(BSF, low[:, :, 0], low[:, :, 1], ALU.max))
            ce(dve.tensor_scalar(BSF, BSF, -1.0, float(NW - W), ALU.mult, ALU.min))
            ce(dve.tensor_copy(BASE[:, :], BSF))
            ce(dve.tensor_copy(EDF, EDI))
            ce(dve.tensor_tensor(REL[:, :].rearrange("p (q i) -> p q i", i=2), EDF.rearrange("p (q i) -> p q i", i=2),
                                 BSF.unsqueeze(2).to_broadcast([128, EW // 2, 2]), ALU.subtract))
            ce(dve.tensor_scalar(MIS[:, :], REL[:, :], 0.0, None, ALU.is_ge))
            ce(dve.scalar_tensor_tensor(MIS[:, :], REL[:, :], float(W), MIS[:, :], ALU.is_lt, ALU.mult))
            ce(dve.tensor_scalar(EDT, MIS[:, :], -1.0, 1.0, ALU.mult, ALU.add))
            ce(dve.tensor_tensor(EDT, EDT, EDF, ALU.mult))
            ce(dve.tensor_tensor(MIS[:, :], EDT, MIS[:, :], ALU.subtract))
            ce(dve.tensor_reduce(FL1[:, :], MIS[:, :], AX.X, ALU.max))
            dve.sem_inc(neg_done, 1)
            ce(dve.tensor_scalar(EHI, EDF, 1.0 / P, -0.496, ALU.mult, ALU.add))
            ce(dve.tensor_scalar(EHI, EHI, 12582912.0, 12582912.0, ALU.add, ALU.subtract))
            ce(dve.scalar_tensor_tensor(EDT, EHI, -float(P), EDF, ALU.mult, ALU.add))
            dve.wait_ge(par_done, 2)
            ce(dve.tensor_scalar(FLI[:, :], FLG[:, :], 0.0, None, ALU.is_ge))
            ce.end()
            dve.sem_inc(base_done, 1)

            dve.wait_ge(const_done, 1)
            dve.sem_inc(hist_mm, 2)
            with dve.Fori(0, EW // (2 * HB)) as r:
                for b in range(2):
                    dve.wait_ge(hist_mm, r * 2 + b + 1)
                    dve.tensor_tensor(OHH[:, b, :, :], IOTA[:, 0:T].unsqueeze(1).to_broadcast([128, HB, T]),
                                      EHI[:, ds((r * 2 + b) * HB, HB)].unsqueeze(2).to_broadcast([128, HB, T]), ALU.is_equal)
                    for i in range(HB):
                        ins = dve.tensor_scalar(OHL[:, b, i, :], IOTA[:, 0:P], EDT[:, ds((r * 2 + b) * HB + i, 1)], None, ALU.is_equal)
                    ins.then_inc(hist_oh, 1)
            dve.wait_ge(deg_mm, 1)
            cd = Chain(dve, d_fin, 0, NEWTON + 1)
            newton(cd, PH[0][0:P, 0:T], 1.0, DNT, DNI)
            dve.tensor_scalar(DO[:, :], DNT[:, 0, :], 1.0 / TS, None, ALU.mult)
            cd(dve.tensor_scalar(DT[:, :], DNT[:, 0, :], TS, None, ALU.mult))
            cd.end()
            for g in range(G):
                if g >= 1:
                    dve.wait_ge(th_done, g)
                    dve.wait_ge(xt_mm, g * TG)
                    dve.wait_ge(tl_done, g)
                for j in range(TG):
                    t = g * TG + j
                    dve.tensor_scalar(ZN[:, j, :], X[:, t, :], DT[:, t:t + 1], None, ALU.mult).then_inc(xs_done, 1)
                dve.wait_ge(th_done, g + 1)
                dve.tensor_tensor(TH[:, :, D:2 * D], ZN[:, :, :], TH[:, :, 0:D], ALU.subtract).then_inc(tl_done, 1)
            dve.wait_ge(tl_done, G)
            dve.wait_ge(xt_mm, T)
            dve.wait_ge(agg_init, T)
            dve.sem_inc(km_read, 1)
            dve.sem_inc(x2_done, 1)
            dve.sem_inc(vl_done, 1)
            dve.sem_inc(agg_done, 1)
            with dve.Fori(0, L) as l:
                prep(l)
                with dve.Fori(0, G) as g:
                    ln1(l, g, l * G + g)
                head(l)
                with dve.Fori(0, G) as g:
                    kv(l, g, l * G + g)
                mid(l)
                with dve.Fori(0, G) as g:
                    onehot(l * G + g)
                    attn(l, g, l * G + g)
                    ffn(l, g, l * G + g)
                    collect(l * G + g)

            with some_missed(dve, FLI[0:1, 0:1], base_done):
                dve.wait_ge(agg_done, L * G * NP_ + 1)
                with dve.Fori(0, EW) as t:
                    dve.tensor_copy(MW[:, :], MIS[:, ds(t, 1)]).then_inc(miss_col, 1)
                    with dve.Fori(0, NWIN) as w:
                        n = t * NWIN + w
                        dve.wait_ge(miss_mm, n + 1)
                        dve.wait_ge(miss_col, t * (NWIN + 1) + w + 1)
                        dve.tensor_scalar(OH[:, 0, :], IOTA[:, 0:W], MW[:, 0:1], None, ALU.is_equal).then_inc(miss_oh, 1)
                        dve.tensor_scalar(MW[:, :], MW[:, :], -float(W), None, ALU.add).then_inc(miss_col, 1)
                        dve.wait_ge(miss_mm, n + 2)
                        o = AGG[:, :, ds(w * W, W)]
                        dve.tensor_tensor(o, PC[0][:, 0:2 * W].rearrange("p (k n) -> p k n", k=KD), o, ALU.add).then_inc(miss_added, 1)
                        dve.wait_ge(miss_added, n + 1)

            cf = Chain(dve, d_route, 0, G * (LN + 4) + 15)
            dve.wait_ge(late_in, 64)
            dve.wait_ge(x2_done, L * T + 1)
            for g in range(G):
                for j in range(TG):
                    t = g * TG + j
                    dve.wait_ge(gn_mm, t + 1)
                    ins = dve.scalar_tensor_tensor(ZN2[:, j, :], PA[j % 2][0:P, 0:D], DO[:, t:t + 1], GNB, ALU.mult, ALU.add)
                    ins.then_inc(gn_read, 1)
                dve.wait_ge(gn_read, (g + 1) * TG)
                cf(dve.scalar_tensor_tensor(ZN2[:, :, :], ZN2[:, :, :], 0.2, ZN2[:, :, :], ALU.mult, ALU.max))
                xg = X[:, g * TG:(g + 1) * TG, :]
                cf(dve.tensor_tensor(xg, xg, ZN2[:, :, :], ALU.add))
                dve.wait_ge(xr_in, 16 * (g + 1))
                cf(dve.tensor_tensor(xg, xg, QS[:, :, :], ALU.add))
                dve.sem_inc(xt_done, TG)
                if g >= 1:
                    dve.wait_ge(row_done, g * TG)
                    dve.wait_ge(row_hi, g)
                    dve.wait_ge(tf_mm, g * TG)
                norm(cf, [X[:, g * TG + j, :] for j in range(TG)], lambda j: ZN[:, j, :], zf_done)
                cf(dve.memset(PAD[:, 0:1], 0.0))
                dve.wait_ge(row_hi, g + 1)
                dve.wait_ge(zf_done, (g + 1) * TG)
                dve.tensor_tensor(ROW[:, g * TG:(g + 1) * TG, D:2 * D], ZN[:, :, :], ROW[:, g * TG:(g + 1) * TG, 0:D],
                                  ALU.subtract).then_inc(row_done, TG)
                for j in range(TG):
                    t = g * TG + j
                    dve.wait_ge(lg_mm, t + 1)
                    dve.tensor_copy(LG[:, t, :], PH[j % 2][0:P, 0:EX]).then_inc(lg_read, 1)
            dve.wait_ge(lg_read, T)
            bc = lambda v: v.unsqueeze(2).to_broadcast([P, T, EX])
            be = lambda v: v.unsqueeze(1).to_broadcast([P, T, EX])
            r = lambda n: R1[:, n, :]
            cf(dve.tensor_reduce(r(0), LG, AX.X, ALU.max))
            dve.tensor_tensor(L2, LG, bc(r(0)), ALU.subtract).then_inc(top_done, 1)
            cf(dve.tensor_tensor(L1, LG, bc(r(0)), ALU.is_equal))
            cf(dve.tensor_tensor(L1, L1, be(IOC[:, :]), ALU.mult))
            cf(dve.tensor_reduce(r(1), L1, AX.X, ALU.max))
            cf(dve.tensor_tensor(LG, L1, bc(r(1)), ALU.is_equal))
            dve.tensor_copy(OE[:, :, :], LG).then_inc(oe_done, 1)
            dve.wait_ge(es_done, 1)
            cf(dve.tensor_reduce(r(2), L2, AX.X, ALU.add))
            cf(dve.reciprocal(r(2), r(2)))
            dve.wait_ge(row_done, T)
            dve.tensor_copy(ROW[:, :, 2 * D:RW].bitcast(f32), r(2).unsqueeze(2)).then_inc(row_done, 1)
            cf(dve.tensor_tensor(L1, LG, be(IOE[:, :]), ALU.mult))
            cf(dve.tensor_reduce(r(3), L1, AX.X, ALU.add))
            dve.wait_ge(pos_mm, 1)
            cf(dve.tensor_tensor(L1, PA[0][0:P, 0:T * EX].rearrange("p (t e) -> p t e", e=EX), LG, ALU.mult))
            cf(dve.tensor_reduce(r(4), L1, AX.X, ALU.add))
            cf(dve.tensor_scalar(r(5), r(4), float(C), None, ALU.is_le))
            cf(dve.scalar_tensor_tensor(r(0), r(4), -1.0, r(3), ALU.add, ALU.add))
            cf(dve.tensor_scalar(r(1), r(5), -BIG, BIG, ALU.mult, ALU.add))
            cf(dve.tensor_tensor(SIX[:, :], r(0), r(1), ALU.add))
            dve.tensor_scalar(r(4), r(4), float(C), -1.0, ALU.min, ALU.add).then_inc(route_done, 1)
            dve.wait_ge(route_done, 1)
            dve.tensor_tensor(GIX[:, :], r(4), r(3), ALU.add).then_inc(route_done, 1)
            cf.end()

            dve.sem_inc(estage_free, 2)
            dve.sem_inc(ehl_done, 2)
            dve.sem_inc(ey_read, 2)
            with dve.Fori(0, EX) as e:
                ch = Chain(dve, d_exp, e, 10)
                for n, (hi, lo, k) in enumerate(((W1H, W1L, KD), (W2H, W2L, NF))):
                    dve.wait_ge(ehi_done, e * 2 + n + 1)
                    dve.scalar_tensor_tensor(lo[:, :, :], SWE[:, n, :].rearrange("p (k n) -> p k n", k=k), WS, hi[:, :, :],
                                             ALU.mult, ALU.subtract).then_inc(elo_done, 1)
                dve.wait_ge(ev_in, (e + 1) * 32)
                ch(dve.tensor_scalar(RF[:, 2, :], BR[:, 1, :], WS, None, ALU.mult))
                ch(dve.tensor_copy(RT[:, 2, :], RF[:, 2, :]))
                ch(dve.tensor_scalar(RM[:, 2, :], RT[:, 2, :], LOW[:, 0:1], None, ALU.mult))
                ch(dve.tensor_tensor(RB[:, 2, :], RF[:, 2, :], RM[:, 2, :], ALU.subtract))
                dve.sem_inc(ebias_done, 1)
                dve.wait_ge(et_mm, e * 2 + 2)
                dve.tensor_copy(BTL, PT[1][:, :].bitcast(f16)[:, 0:KD * CP].rearrange("p (k n) -> p k n", k=KD)).then_inc(bt_lo, 1)
                for f in range(NF):
                    dve.wait_ge(eh_done, e * NF + f + 1)
                    dve.tensor_tensor(HL[:, f, 0:CP], HF[:, f % 2, :], HH[:, f, 0:CP], ALU.subtract).then_inc(ehl_done, 1)
                for j in range(NCT):
                    dve.wait_ge(ey_mm, e * NCT + j + 2)
                    ins = dve.tensor_scalar(YV[:, j, :], PA[j % 2][0:CT_, 0:D], BS[:, j, 2 * D:RW].bitcast(f32), 1.0 / WS,
                                            ALU.mult, ALU.mult)
                    ins.then_inc(ey_read, 1)
                dve.wait_ge(ey_read, (e + 1) * NCT + 2)
                dve.wait_ge(ey_out, e * 16 + 16)
                ch(dve.tensor_scalar(YF, YV, 0.0, 0.0, ALU.mult, ALU.is_equal))
                ch(dve.tensor_scalar(YC[:, :, :], YV, -1.0e4, 1.0e4, ALU.max, ALU.min))
                ch(dve.tensor_tensor(YE, YV, YV, ALU.is_equal))
                ch(dve.memset(YR, 0.0))
                dve.memset(PAD[:, 0:1], 0.0)
                ch(dve.copy_predicated(YR, YE.bitcast(i32), YC[:, :, :]))
                dve.memset(PAD[:, 0:1], 0.0)
                ch(dve.copy_predicated(YR, YF.bitcast(i32), YV))
                ch.end()
                dve.sem_inc(ey_clean, 1)
                dve.wait_ge(elo_done, (e + 1) * 2)
                dve.sem_inc(estage_free, 2)
            for t in range(T):
                if t % TG == 0:
                    dve.wait_ge(back_in[t // TG], 16 * TG)
                dve.scalar_tensor_tensor(X[:, t, :], YG[:, t, :], R1[:, 5, t:t + 1], X[:, t, :], ALU.mult, ALU.add).then_inc(fin_done, 1)

        @block.tensor
        def _(pe):
            pe.sem_inc(ctx_mm, 2)
            pe.sem_inc(y_mm, 1)

            def three(o, st, mv, k, start=False, stop=False, **kw):
                n = 0
                for c in range(k):
                    for a, b in ((0, 0), (0, 1), (1, 0)):
                        ins = pe.matmul(o, st(a, c), mv(b, c), start=(start and n == 0), stop=(stop and n == 3 * k - 1), **kw)
                        n += 1
                return ins

            Z1 = (Z1H, Z1L)
            Z2 = (Z2H, Z2L)
            KV = (KVH, KVL)
            QO = (QOH, QOL)
            W1 = (W1H, W1L)
            W2 = (W2H, W2L)
            CT = (CTH, CTL)
            CW = (CWH, CWL)
            QT = (QTH, QTL)
            HX = (HH, HL)
            EXP = (EH, EL)
            VX = (VH, VL)

            def prep(l):
                pe.wait_ge(lnp_done, l * 3 + 3)
                pe.wait_ge(qo_in, (l + 1) * 32)
                pe.wait_ge(kv_in, (l + 1) * 32)
                pe.wait_ge(ff_in, (l + 1) * 32)
                pe.wait_ge(x2_done, l * T + 1)
                for k in range(KD):
                    ins = pe.matmul(PA[0][0:2, 0:D], B2[:, k, :], SQO[:, 0, k, :], start=(k == 0), stop=(k == KD - 1))
                ins.then_inc(bq_mm, 1)
                for h in range(KD):
                    for k in range(KD):
                        ins = pe.matmul(PT[0][:, h:h + 1], SKV[:, k, 1, h * 128:(h + 1) * 128], B2[:, k, 0:1],
                                        start=(k == 0), stop=(k == KD - 1))
                ins.then_inc(bv_mm, 1)
                for f in range(NF):
                    for k in range(KD):
                        ins = pe.matmul(PT[1][:, f:f + 1], SW[:, k * FF + f * 128:k * FF + (f + 1) * 128],
                                        LNP[:, 3, k:k + 1], start=(k == 0), stop=(k == KD - 1))
                ins.then_inc(b1_mm, 1)
                pe.wait_ge(bv_done, l + 1)
                for k in range(KD):
                    ins = pe.matmul(PA[1][0:2, 0:D], BV[:, k, :], SQO[:, 1, k, :], start=(k == 0), stop=(k == KD - 1))
                ins.then_inc(bo_mm, 1)

            def ln1_t(l, g, it):
                pe.wait_ge(rows_done, l + 1)
                pe.wait_ge(wlo_done, (l + 1) * 8)
                for j in range(TG):
                    n = it * TG + j
                    pe.wait_ge(z1_done, T + n + 1)
                    if j >= 2:
                        pe.wait_ge(t1_lo, n - 1)
                    for h in range(KD):
                        ins = pe.transpose(PT[j % 2][:, h * P:(h + 1) * P], ZN[:, j, h * 128:(h + 1) * 128], ID[0:P, 0:P])
                    ins.then_inc(t1_mm, 1)
                pe.wait_ge(t1_lo, (it + 1) * TG)
                u = 0
                for m in range(KD):
                    for c, (t0, tn) in enumerate(CH):
                        if u < 2:
                            pe.wait_ge(km_read, it * 4 + 1)
                        else:
                            pe.wait_ge(km_read, it * 4 + u - 1 + 1)
                        three(PH[u % 2][:, 0:tn * P],
                              lambda a, k: KV[a][:, k, 0, m * 128:(m + 1) * 128],
                              lambda b, k: Z1[b][:, k, ds((g * TG + t0) * P, tn * P)], KD, True, True).then_inc(km_mm, 1)
                        u += 1

            def head(l):
                pe.wait_ge(kx_done, l + 1)
                for m in range(KD):
                    ins = pe.matmul(PA[0][0:1, m * 128:(m + 1) * 128], KX[:, m:m + 1], ID[:, :], start=True, stop=True)
                ins.then_inc(kr_mm, 1)
                for h in range(KD):
                    ins = pe.matmul(PC[h][:, 0:129], ZR[0:1, 0:128], ZR[0:1, 0:129], start=True, stop=False,
                                    skip_group_check=True)

            def kv(l, g, it):
                pe.wait_ge(kr_done, l + 1)
                for j in range(TG):
                    n = it * TG + j
                    t = g * TG + j
                    if j >= 2:
                        pe.wait_ge(vl_done, n)
                    else:
                        pe.wait_ge(vl_done, it * TG + 1)
                    o = PA[j % 2][0:P, 0:2 * D]
                    three(o, lambda a, k: Z1[a][:, k, ds(t * P, P)],
                          lambda b, k: KV[b][:, k, :, :].rearrange("p a d -> p (a d)"), KD, True, False, skip_group_check=True)
                    pe.matmul(PA[j % 2][0:P, 0:D], ONE[0:1, 0, 0:P], KR[0:1, :], start=False, stop=True,
                              skip_group_check=True).then_inc(kv_mm, 1)
                    if j > 0:
                        context(it, j - 1)
                context(it, TG - 1)

            def context(it, j):
                n = it * TG + j
                pe.wait_ge(el_done, n + 3)
                pe.wait_ge(vl_done, n + 1 + 1)
                for h in range(KD):
                    for a, b in ((0, 0), (0, 1), (1, 0)):
                        ins = pe.matmul(PC[h][:, 0:129], EXP[a][:, j % 2, h * 128:(h + 1) * 128], VX[b][:, j % 2, h, 0:129],
                                        start=False, stop=False, skip_group_check=True)
                ins.then_inc(ctx_mm, 1)

            def mid(l):
                for h in range(KD):
                    ins = pe.matmul(PC[h][:, 0:129], ZR[0:1, 0:128], ZR[0:1, 0:129], start=False, stop=True,
                                    skip_group_check=True)
                ins.then_inc(ctx_end, 1)
                pe.wait_ge(cn_done, (l + 1) * KD)
                for h in range(KD):
                    ins = pe.transpose(PT[0][:, h * 128:(h + 1) * 128], CN[:, h, :], ID[:, :])
                ins.then_inc(ct_mm, 1)
                pe.wait_ge(ct_lo, l + 1)
                for h in range(KD):
                    three(PA[h][:, 0:D], lambda a, k: CT[a][:, h, :], lambda b, k: QO[b][:, 1, h, :], 1,
                          True, True).then_inc(cw_mm, 1)

            def attn(l, g, it):
                pe.wait_ge(cw_lo, (l + 1) * KD)
                for j in range(TG):
                    n = it * TG + j
                    if j >= 2:
                        pe.wait_ge(q_read, n - 1)
                    else:
                        pe.wait_ge(x2_done, it * TG + 1)
                    o = PA[j % 2][0:P, 0:D]
                    pe.matmul(o, ONE[0:2, 0, 0:P], RB[:, 0, :], start=True, stop=False)
                    three(o, lambda a, k: Z1[a][:, k, ds((g * TG + j) * P, P)], lambda b, k: QO[b][:, 0, k, :], KD,
                          False, True).then_inc(q_mm, 1)
                pe.wait_ge(qn_done, it + 1)
                for j in range(TG):
                    if j >= 2:
                        pe.wait_ge(tq_lo, it * TG + j - 1)
                    for h in range(KD):
                        ins = pe.transpose(PT[j % 2][:, h * P:(h + 1) * P], QS[:, j, h * 128:(h + 1) * 128], ID[0:P, 0:P])
                    ins.then_inc(tq_mm, 1)
                pe.wait_ge(q_read, (it + 1) * TG)
                for j in range(TG):
                    n = it * TG + j
                    pe.wait_ge(tq_lo, n + 1)
                    if j >= 2:
                        pe.wait_ge(x1_done, n - 1)
                    o = PA[j % 2][0:P, 0:D]
                    pe.matmul(o, ONE[0:2, 1, 0:P], RB[:, 1, :], start=True, stop=False)
                    three(o, lambda a, k: QT[a][:, k, j * P:(j + 1) * P], lambda b, k: CW[b][:, k, :], KD,
                          False, True).then_inc(at_mm, 1)
                for j in range(TG):
                    n = it * TG + j
                    pe.wait_ge(z2_done, n + 1)
                    if j >= 2:
                        pe.wait_ge(t2_lo, n - 1)
                    for h in range(KD):
                        ins = pe.transpose(PT[j % 2][:, h * P:(h + 1) * P], ZN2[:, j, h * 128:(h + 1) * 128], ID[0:P, 0:P])
                    ins.then_inc(t2_mm, 1)

            def ffn(l, g, it):
                u = 0
                pe.wait_ge(t2_lo, (it + 1) * TG)
                for c, (t0, tn) in enumerate(CH):
                    for f in range(NF):
                        n = it * 2 * NF + u
                        if u >= 2:
                            pe.wait_ge(gelu_done, n - 1)
                        else:
                            pe.wait_ge(hl_done, it * 2 * NF + 2)
                        three(PH[u % 2][:, 0:tn * P], lambda a, k: W1[a][:, k, f * 128:(f + 1) * 128],
                              lambda b, k: Z2[b][:, k, t0 * P:(t0 + tn) * P], KD, True, True).then_inc(f1_mm, 1)
                        u += 1
                for j in range(TG):
                    n = it * TG + j
                    if j in (0, 3):
                        pe.wait_ge(hl_done, it * 2 * NF + (NF if j == 0 else 2 * NF) + 2)
                    if j >= 2:
                        pe.wait_ge(x2_done, n - 1 + 1)
                    else:
                        pe.wait_ge(x1_done, (it + 1) * TG)
                    o = PA[j % 2][0:P, 0:D]
                    pe.matmul(o, ONE[0:2, 0, 0:P], RB[:, 2, :], start=True, stop=False)
                    three(o, lambda a, f: HX[a][:, f, j * P:(j + 1) * P], lambda b, f: W2[b][:, f, :], NF,
                          False, True).then_inc(y_mm, 1)

            def route(g):
                for j in range(TG):
                    t = g * TG + j
                    pe.wait_ge(zf_done, t + 1)
                    if t >= 1:
                        pe.wait_ge(tf_done, max(1, t - 1 if j >= 2 else g * TG))
                    for h in range(KD):
                        ins = pe.transpose(PT[j % 2][:, h * P:(h + 1) * P], ZN[:, j, h * 128:(h + 1) * 128], ID[0:P, 0:P])
                    ins.then_inc(tf_mm, 1)
                    pe.wait_ge(tf_done, t + 1)
                    if t >= 1:
                        pe.wait_ge(lg_read, max(1, t - 1 if j >= 2 else g * TG))
                    o = PH[j % 2][0:P, 0:EX]
                    pe.matmul(o, ONF[:, :], GBR[:, :], start=True, stop=False)
                    for k in range(KD):
                        ins = pe.matmul(o, EFT[:, j % 2, k * P:(k + 1) * P], GW[:, k, :], start=False, stop=(k == KD - 1))
                    ins.then_inc(lg_mm, 1)

            def pairs(it):
                pe.wait_ge(oh_done, it + 1)
                for q in range(NP_):
                    n = it * NP_ + q
                    s = q % SLOTS
                    pe.wait_ge(gin[s], (it * (NP_ // SLOTS) + q // SLOTS + 1) * 32)
                    if q < 2:
                        pe.wait_ge(agg_done, it * NP_ + 1)
                    else:
                        pe.wait_ge(agg_done, n)
                    for h in range(KD):
                        for i in range(2):
                            for part in range(2):
                                c = part * D + h * 128
                                ins = pe.matmul(PC[q % 2][:, h * W:(h + 1) * W], GB[:, s, i, c:c + 128], OH[:, 2 * q + i, :],
                                                start=(i + part == 0), stop=(i + part == 2))
                    ins.then_inc(pair_mm, 1)

            pe.wait_ge(const_done, 1)
            pe.sem_inc(pair_mm, SLOTS + 1)
            deg = PH[0][0:P, 0:T]
            pe.matmul(deg, ZR[0:1, 0:P], ZR[0:1, 0:T], start=True, stop=False, skip_group_check=True)
            with pe.Fori(0, EW // (2 * HB)) as r:
                for b in range(2):
                    pe.wait_ge(hist_oh, r * 2 + b + 1)
                    for i in range(HB):
                        ins = pe.matmul(deg, OHL[:, b, i, :], OHH[:, b, i, :], start=False, stop=False, skip_group_check=True)
                    ins.then_inc(hist_mm, 1)
            pe.matmul(deg, ZR[0:1, 0:P], ZR[0:1, 0:T], start=False, stop=True, skip_group_check=True).then_inc(deg_mm, 1)
            for t in range(T):
                j = t % 2
                pe.wait_ge(xs_done, t + 1)
                if t % TG >= 2:
                    pe.wait_ge(agg_init, t - 1)
                elif t >= TG:
                    pe.wait_ge(agg_init, t // TG * TG)
                for h in range(KD):
                    b = t % TG % 2
                    ins = pe.transpose(PT[b][:, h * P:(h + 1) * P], ZN[:, t % TG, h * 128:(h + 1) * 128], ID[0:P, 0:P])
                ins.then_inc(xt_mm, 1)
            pe.wait_ge(agg_init, T)
            with pe.Fori(0, L) as l:
                prep(l)
                with pe.Fori(0, G) as g:
                    ln1_t(l, g, l * G + g)
                head(l)
                with pe.Fori(0, G) as g:
                    kv(l, g, l * G + g)
                mid(l)
                with pe.Fori(0, G) as g:
                    attn(l, g, l * G + g)
                    ffn(l, g, l * G + g)
                    pairs(l * G + g)

            with some_missed(pe, FLI[0:1, 0:1], base_done):
                with pe.Fori(0, EW) as t:
                    with pe.Fori(0, NWIN) as w:
                        n = t * NWIN + w
                        pe.wait_ge(miss_in, t * 16 + 16)
                        pe.wait_ge(miss_oh, n + 1)
                        for h in range(KD):
                            for part in range(2):
                                c = part * D + h * 128
                                ins = pe.matmul(PC[0][:, h * W:(h + 1) * W], GB[:, 0, 0, c:c + 128], OH[:, 0, :],
                                                start=(part == 0), stop=(part == 1))
                        ins.then_inc(miss_mm, 1)
                pe.wait_ge(miss_added, EW * NWIN)

            pe.wait_ge(agg_done, L * G * NP_ + 1)
            pe.wait_ge(late_in, 64)
            pe.wait_ge(x2_done, L * T + 1)
            for t in range(T):
                j = t % TG
                if t >= 2:
                    pe.wait_ge(gn_read, t - 1 if j >= 2 else t // TG * TG)
                for k in range(KD):
                    ins = pe.matmul(PA[j % 2][0:P, 0:D], AGG[:, k, t * P:(t + 1) * P], GNW[:, k, :], start=(k == 0), stop=(k == KD - 1))
                ins.then_inc(gn_mm, 1)
                if j == TG - 1:
                    route(t // TG)

            pe.wait_ge(oe_done, 1)
            pe.wait_ge(gn_read, T)
            pos = PA[0][0:P, 0:T * EX]
            pe.matmul(pos, TRI[:, :], OE[:, :, :].rearrange("p t e -> p (t e)"), start=True, stop=False, skip_group_check=True)
            for t in range(T - 1):
                ins = pe.matmul(PA[0][0:P, (t + 1) * EX:T * EX].rearrange("p (t e) -> p t e", e=EX), ON1[:, :],
                                OE[:, t, :].unsqueeze(1).to_broadcast([P, T - 1 - t, EX]), start=False, stop=(t == T - 2),
                                skip_group_check=True)
            ins.then_inc(pos_mm, 1)

            pe.sem_inc(ey_mm, 1)
            pe.wait_ge(route_done, 2)
            with pe.Fori(0, EX) as e:
                pe.wait_ge(slot_in, (e + 1) * 16)
                for part in range(2):
                    o = PT[part][:, :].bitcast(f16)
                    for k in range(KD):
                        for j in range(NCT):
                            c = part * D + k * 128
                            ins = pe.transpose(o[:, k * CP + j * CT_:k * CP + (j + 1) * CT_], BS[:, j, c:c + 128], IDH[0:CT_, 0:CT_])
                    ins.then_inc(et_mm, 1)
                pe.wait_ge(bt_hi, e + 1)
                pe.wait_ge(bt_lo, e + 1)
                pe.wait_ge(elo_done, (e + 1) * 2)
                BT = (BTH, BTL)
                for f in range(NF):
                    n = e * NF + f
                    pe.wait_ge(ehl_done, n + 1 if f >= 2 else e * NF + 2)
                    three(PH[f % 2][:, 0:CP], lambda a, k: W1[a][:, k, f * 128:(f + 1) * 128], lambda b, k: BT[b][:, k, :],
                          KD, True, True).then_inc(e1_mm, 1)
                pe.wait_ge(ehl_done, (e + 1) * NF + 2)
                pe.wait_ge(ebias_done, e + 1)
                for j in range(NCT):
                    n = e * NCT + j
                    pe.wait_ge(ey_read, n + 1)
                    o = PA[j % 2][0:CT_, 0:D]
                    pe.matmul(o, ONE[0:2, 0, 0:CT_], RB[:, 2, :], start=True, stop=False)
                    three(o, lambda a, f: HX[a][:, f, j * CT_:(j + 1) * CT_], lambda b, f: W2[b][:, f, :], NF,
                          False, True).then_inc(ey_mm, 1)


def kernel(**inputs):
    import numpy as _np
    import concourse.bacc as _bacc
    from concourse import mybir as _mybir
    from concourse.bass_utils import run_bass_kernel_spmd as _run

    nc = _bacc.Bacc("TRN2", target_bir_lowering=False, num_devices=1)
    arrays, args = {}, {}
    mix = {name[7:]: _np.asarray(value) for name, value in inputs.items() if name.startswith("L0_mix_")}
    columns = [mix[n].reshape(mix[n].shape[0], -1, 128).transpose(0, 2, 1) for n in ("ln1_g", "ln1_b", "ln2_g", "ln2_b", "b1")]
    rows = _np.stack([mix["bo"], mix["b2"]], axis=1)
    laid = dict(inputs, mix_vec=_np.concatenate(columns, axis=2), mix_rows=_np.stack([rows, rows], axis=1))
    for name in ("ln1_g", "ln1_b", "ln2_g", "ln2_b", "b1", "bo", "b2"):
        del laid["L0_mix_" + name]
    tiles = 400
    for name, pad in (("src", 0), ("dst", -1)):
        a = _np.asarray(laid.pop(name))
        a = _np.concatenate([a, _np.full(tiles * 128 - a.shape[0], pad, a.dtype)])
        laid["edge_" + name] = a.reshape(tiles, 128).T
    laid["gnn_bias"] = _np.tile(_np.asarray(laid.pop("L0_gnn_b"))[None, :], (125, 1))
    b1, b2 = _np.asarray(laid.pop("L0_ffn_b1")), _np.asarray(laid.pop("L0_ffn_b2"))
    laid["ffn_vec"] = b1.reshape(b1.shape[0], -1, 128).transpose(0, 2, 1)
    laid["ffn_rows"] = _np.stack([b2, b2], axis=1)
    for name, value in laid.items():
        a = _np.ascontiguousarray(value)
        arrays[f"in_{name}"] = a
        args[name] = nc.dram_tensor(f"in_{name}", a.shape, _mybir.dt.from_np(a.dtype), kind="ExternalInput").ap()
    out = nc.dram_tensor("out_0", (3125, 256), _mybir.dt.float32, kind="ExternalOutput").ap()
    build(nc, args, out)
    r = _run(nc, [arrays], core_ids=[0])
    return r.results[0]["out_0"]
```

```python
import concourse.bass as bass
from concourse import mybir
from contextlib import ExitStack

def build(nc, A, out):
    f32 = mybir.dt.float32
    f16 = mybir.dt.float16
    i32 = mybir.dt.int32
    ALU = mybir.AluOpType
    ACT = mybir.ActivationFunctionType
    AX = mybir.AxisListType
    ds = bass.ds

    def some_missed(eng, flag, ready):
        eng.wait_ge(ready, 1)
        return eng.If(eng.value_load(flag, min_val=0, max_val=1) != 0)

    RMAX = bass.bass_isa.ReduceOp.max

    N, D = A["x"].shape
    L = A["L0_mix_Wq"].shape[0]
    FF = A["L0_mix_W1"].shape[2]
    P = 125
    T = N // P
    TG = 5
    G = T // TG
    NG = P * TG
    KD = D // 128
    NF = FF // 128
    HEADS, DH = 8, 32
    CH = [(0, 3), (3, 2)]
    EPS = 1e-5
    SCALE = DH ** -0.25
    WS = 64.0
    QS_ = 1024.0
    ES = 4096.0
    NK = 7
    KC = [N * n // NK for n in range(NK + 1)]
    W = 64
    TS = 256.0
    EW = A["edge_src"].shape[1]
    EI = EW // (L * G)
    NP_ = EI // 2
    SLOTS = 5
    EX = A["L0_ffn_w1"].shape[0]
    C = -(-5 * N // (4 * EX))
    CT_ = 124
    NCT = -(-C // CT_)
    CP = CT_ * NCT
    RW = 2 * D + 2
    BIG = 1.0e6
    ZD = EX * CP // (2 * CT_)
    T2_AT = ((), (), (0, 1), (2, 3), (4,))
    W2_AT = (0, 2, 4, 5)
    CLEAN_AT = 3
    T1_AT = range(2, 2 + TG)
    TQ_AT = range(NF, NF + TG)
    assert T * P == N and G * TG == T and EI * L * G == EW and CP <= 512

    ctx = ExitStack()
    with ctx:
        def sb(name, shape, dt):
            return ctx.enter_context(nc.sbuf_tensor(name, shape, dt))

        def pb(name):
            return ctx.enter_context(nc.psum_tensor(name, [128, 512], f32))

        def sem(name):
            return ctx.enter_context(nc.semaphore(name))

        X = sb("X", [P, T, D], f32)
        ZB = sb("ZB", [128, T * RW], f16)
        Z1H = ZB[:, 0:KD * N].rearrange("p (k n) -> p k n", k=KD)
        Z1L = ZB[:, KD * N:2 * KD * N].rearrange("p (k n) -> p k n", k=KD)
        ROW = ZB[0:P, :].rearrange("p (t n) -> p t n", t=T)
        ROWI = ZB[0:P, :].bitcast(i32).rearrange("p (t n) -> p t n", t=T)
        NWIN = -(-N // W)
        NW = NWIN * W
        AB = sb("AB", [128, T * D], f32)
        AGG = AB[:, 0:KD * NW].rearrange("p (k n) -> p k n", k=KD)
        YG = AB[0:P, :].rearrange("p (t d) -> p t d", t=T)
        SW = sb("SW", [128, KD * FF], f32)
        GB = sb("GB", [128, SLOTS, 2, 2 * D], f16)
        OH = sb("OH", [128, EI, W], f16)
        EIX = sb("EIX", [128, EW], i32)
        REL = sb("REL", [128, EW], f32)
        MIS = sb("MIS", [128, EW], f32)
        slot = lambda n, dt: GB[:, n, :, :].rearrange("p i n -> p (i n)").bitcast(dt)
        EDI = slot(0, i32)[:, 0:EW]
        EDF = slot(1, f32)[:, 0:EW]
        EDT = slot(2, f32)[:, 0:EW]
        EHI = slot(3, f32)[:, 0:EW]
        BSF = slot(4, f32)[:, 0:EW // 2]
        IB = sb("IB", [128, EI], i32)
        BASE = sb("BASE", [128, EW // 2], i32)
        DNT = sb("DNT", [P, 3, T], f32)
        DNI = sb("DNI", [P, T], i32)
        DT = sb("DT", [P, T], f32)
        DO = sb("DO", [P, T], f32)
        ZN = sb("ZN", [P, TG, D], f32)
        ZN2 = sb("ZN2", [P, TG, D], f32)
        Z2B = sb("Z2B", [128, 2 * KD * NG], f16)
        Z2H = Z2B[:, 0:KD * NG].rearrange("p (k n) -> p k n", k=KD)
        Z2L = Z2B[:, KD * NG:2 * KD * NG].rearrange("p (k n) -> p k n", k=KD)
        SKV = sb("SKV", [128, KD, 2, D], f32)
        SQO = sb("SQO", [128, 2, KD, D], f32)
        KVH = sb("KVH", [128, KD, 2, D], f16)
        KVL = sb("KVL", [128, KD, 2, D], f16)
        QOH = sb("QOH", [128, 2, KD, D], f16)
        QOL = sb("QOL", [128, 2, KD, D], f16)
        W1H = sb("W1H", [128, KD, FF], f16)
        W1L = sb("W1L", [128, KD, FF], f16)
        W2H = sb("W2H", [128, NF, D], f16)
        W2L = sb("W2L", [128, NF, D], f16)
        VEC = sb("VEC", [128, 4 * KD + NF], f32)
        LNP = VEC[:, 0:4 * KD].rearrange("p (n k) -> p n k", n=4)
        B1F = VEC[:, 4 * KD:4 * KD + NF]
        G64 = sb("G64", [128, 2, KD], f32)
        B2 = sb("B2", [128, KD, 2], f32)
        B1C = sb("B1C", [128, NF], f32)
        BR = sb("BR", [2, 2, D], f32)
        BV = sb("BV", [128, KD, 2], f32)
        RF = sb("RF", [2, 3, D], f32)
        RT = sb("RT", [2, 3, D], f16)
        RM = sb("RM", [2, 3, D], f16)
        RB = sb("RB", [2, 3, D], f16)
        LOW = sb("LOW", [2, 1], f32)
        ONE = sb("ONE", [2, 2, 128], f16)
        ZR = sb("ZR", [1, 512], f16)
        ID = sb("ID", [128, 128], f32)
        IDH = sb("IDH", [128, 128], f16)
        BM = sb("BM", [128, 128], f32)
        KM = sb("KM", [128, KD, NK], f32)
        KX = sb("KX", [128, KD], f32)
        KR = sb("KR", [1, D], f16)
        VH = sb("VH", [P, 2, KD, 130], f16)
        VL = sb("VL", [P, 2, KD, 130], f16)
        RS = sb("RS", [128, KD], f32)
        CN = sb("CN", [128, KD, 128], f32)
        CTH = sb("CTH", [128, KD, 128], f16)
        CTL = sb("CTL", [128, KD, 128], f16)
        CWH = sb("CWH", [128, KD, D], f16)
        CWL = sb("CWL", [128, KD, D], f16)
        QM = sb("QM", [P, TG, HEADS], f32)
        QS = sb("QS", [P, TG, D], f32)
        EF = QS[:, 0:2, :]
        EH = QS[:, 2, :].bitcast(f16).rearrange("p (b d) -> p b d", b=2)
        EL = QS[:, 3, :].bitcast(f16).rearrange("p (b d) -> p b d", b=2)
        QR = sb("QR", [P, TG * HEADS], f32)
        QTB = sb("QTB", [128, 2 * KD * NG], f16)
        QTH = QTB[:, 0:KD * NG].rearrange("p (k n) -> p k n", k=KD)
        QTL = QTB[:, KD * NG:2 * KD * NG].rearrange("p (k n) -> p k n", k=KD)
        HF = sb("HF", [128, 2, CP], f32)
        HHB = sb("HHB", [128, NF * NG], f16)
        HH = HHB[:, :].rearrange("p (f n) -> p f n", f=NF)
        HL = sb("HL", [128, NF, NG], f16)
        HB = EI
        SW2 = HHB[:, :].bitcast(f32)[:, 0:NF * D]
        OHL = HHB[:, :].rearrange("p (b i n) -> p b i n", b=2, n=P)
        OHH = HL[:, :, :].rearrange("p a n -> p (a n)")[:, 0:2 * HB * T].rearrange("p (b i n) -> p b i n", b=2, n=T)
        TH = HHB[0:P, 0:TG * 2 * D].rearrange("p (j n) -> p j n", j=TG)
        IOTA = sb("IOTA", [128, 128], f16)
        IOC = sb("IOC", [P, EX], f32)
        IOE = sb("IOE", [P, EX], f32)
        TRI = sb("TRI", [P, P], f16)
        ON1 = sb("ON1", [P, P], f16)
        ONF = sb("ONF", [1, P], f32)
        GBR = sb("GBR", [1, EX], f32)
        GNW = SW[:, 0:KD * D].rearrange("p (k n) -> p k n", k=KD)
        GNB = SW[0:P, KD * D:(KD + 1) * D]
        GW = SW[:, (KD + 1) * D:(KD + 1) * D + KD * EX].rearrange("p (k n) -> p k n", k=KD)
        SKF = SKV[:, :, :, :].rearrange("p k a d -> p (k a d)")
        lg = lambda n: SKF[0:P, n * T * EX:(n + 1) * T * EX].rearrange("p (t e) -> p t e", e=EX)
        LG, L1, L2 = lg(0), lg(1), lg(2)
        OE = sb("OE", [P, T, EX], f16)
        R1 = sb("R1", [P, 6, T], f32)
        SIX = sb("SIX", [P, T], i32)
        PW = sb("PW", [CT_, EX * NCT], f32)
        MW = sb("MW", [128, 1], f32)
        FL1 = sb("FL1", [128, 1], f32)
        FLG = sb("FLG", [128, 1], f32)
        FLI = sb("FLI", [128, 1], i32)
        GIX = sb("GIX", [P, T], i32)
        ST = sb("ST", [P, TG, 6], f32)
        MV = sb("MV", [P, TG, 2], f32)
        ST2 = sb("ST2", [P, TG, 6], f32)
        NT = sb("NT", [P, 3, TG], f32)
        PAD = sb("PAD", [P, 2 * TG + 4], f32)
        PPAD = sb("PPAD", [128, 2 + NP_], f32)
        NI = sb("NI", [P, TG], i32)

        TAB = nc.dram_tensor("node_table", (N, 2 * D), f16).ap()
        BUF = nc.dram_tensor("dispatched", (EX * CP, RW // 2), i32).ap()
        YD = nc.dram_tensor("expert_out", (EX * CP, D), f32).ap()

        PT = [pb("PT0"), pb("PT1")]
        PA = [pb("PA0"), pb("PA1")]
        PH = [pb("PH0"), pb("PH1")]
        PC = [pb("PC0"), pb("PC1")]

        EFT = KVH[:, :, :, :].rearrange("p k a d -> p (k a d)").bitcast(f32)[:, 0:4 * P].rearrange("p (b n) -> p b n", b=2)
        BSI = QTB[0:CT_, :].bitcast(i32)[:, 0:NCT * RW // 2].rearrange("p (j n) -> p j n", j=NCT)
        EWT = AB[:, 0:2 * KD * FF].rearrange("p (b n) -> p b n", b=2)
        SE1 = EWT[:, 0, :].rearrange("p (k n) -> p k n", k=KD)
        SE2 = EWT[:, 1, :].rearrange("p (k n) -> p k n", k=NF)
        ERF = AB[0:2, 2 * KD * FF:2 * KD * FF + EX * D]
        GBF = GB[0:2, :, :, :].rearrange("p s i n -> p (s i n)")
        ERT = GBF[:, 0:EX * D]
        ERB = GBF[:, EX * D:2 * EX * D]
        EB1 = MIS[:, 0:EX * NF]
        BS = QTB[0:CT_, 0:NCT * RW].rearrange("p (j n) -> p j n", j=NCT)
        BTH = Z2B[:, 0:KD * CP].rearrange("p (k n) -> p k n", k=KD)
        BTL = Z2B[:, KD * CP:2 * KD * CP].rearrange("p (k n) -> p k n", k=KD)
        YV = ZN[0:CT_, 0:NCT, :]
        YC = QS[0:CT_, 0:NCT, :]
        YR = ZN2[0:CT_, 0:NCT, :]
        YF = SQO[0:CT_, :, :, :].rearrange("p a k d -> p (a k) d")
        YE = SKV[0:CT_, :, :, :].rearrange("p a k d -> p (a k) d")
        x_in = sem("x_in")
        const_done = sem("const_done")
        pool_chain = sem("pool_chain")
        kv_in = sem("kv_in")
        qo_in = sem("qo_in")
        w1_in = sem("w1_in")
        w2_in = sem("w2_in")
        ln_in = sem("ln_in")
        stage_free = sem("stage_free")
        early_free = sem("early_free")
        whk_done = sem("whk_done")
        wlk_done = sem("wlk_done")
        lnp_done = sem("lnp_done")
        whi_done = sem("whi_done")
        wlo_done = sem("wlo_done")
        bq_mm = sem("bq_mm")
        bv_mm = sem("bv_mm")
        b1_mm = sem("b1_mm")
        bo_mm = sem("bo_mm")
        bv_done = sem("bv_done")
        rows_done = sem("rows_done")
        rt_done = sem("rt_done")
        z1_done = sem("z1_done")
        t1_mm = sem("t1_mm")
        t1_hi = sem("t1_hi")
        t1_lo = sem("t1_lo")
        km_mm = sem("km_mm")
        km_read = sem("km_read")
        kx_done = sem("kx_done")
        kr_mm = sem("kr_mm")
        kr_done = sem("kr_done")
        kv_mm = sem("kv_mm")
        exp_done = sem("exp_done")
        vh_done = sem("vh_done")
        vl_done = sem("vl_done")
        el_done = sem("el_done")
        ctx_mm = sem("ctx_mm")
        edges_in = sem("edges_in")
        gin = [sem(f"gathered_{i}") for i in range(SLOTS)]
        hist_oh = sem("hist_oh")
        hist_mm = sem("hist_mm")
        deg_mm = sem("deg_mm")
        xs_done = sem("xs_done")
        xt_mm = sem("xt_mm")
        agg_init = sem("agg_init")
        th_done = sem("th_done")
        tl_done = sem("tl_done")
        tab_out = [sem("tab_out0"), sem("tab_out1")]
        d_edge = sem("d_edge")
        neg_done = sem("neg_done")
        par_done = sem("par_done")
        base_done = sem("base_done")
        miss_idx = sem("miss_idx")
        miss_in = sem("miss_in")
        miss_col = sem("miss_col")
        miss_oh = sem("miss_oh")
        miss_mm = sem("miss_mm")
        miss_added = sem("miss_added")
        idx_copied = sem("idx_copied")
        oh_done = sem("oh_done")
        pair_mm = sem("pair_mm")
        agg_done = sem("agg_done")
        late_in = sem("late_in")
        xr_in = sem("xr_in")
        gn_mm = sem("gn_mm")
        gn_read = sem("gn_read")
        xt_done = sem("xt_done")
        zf_done = sem("zf_done")
        tf_mm = sem("tf_mm")
        tf_done = sem("tf_done")
        lg_mm = sem("lg_mm")
        lg_read = sem("lg_read")
        row_hi = sem("row_hi")
        row_done = sem("row_done")
        top_done = sem("top_done")
        es_done = sem("es_done")
        oe_done = sem("oe_done")
        pos_mm = sem("pos_mm")
        route_done = sem("route_done")
        d_fin = sem("d_fin")
        d_route = sem("d_route")
        zero_in = sem("zero_in")
        scattered = sem("scattered")
        slot_in = sem("slot_in")
        et_mm = sem("et_mm")
        bt_hi = sem("bt_hi")
        bt_lo = sem("bt_lo")
        e1_mm = sem("e1_mm")
        er_done = sem("er_done")
        eh_done = sem("eh_done")
        ehl_done = sem("ehl_done")
        ey_mm = sem("ey_mm")
        ey_read = sem("ey_read")
        eb_in = sem("eb_in")
        ebias_done = sem("ebias_done")
        e1_in = sem("e1_in")
        e2_in = sem("e2_in")
        e1_hi = sem("e1_hi")
        e1_lo = sem("e1_lo")
        e2_hi = sem("e2_hi")
        e2_lo = sem("e2_lo")
        pw_done = sem("pw_done")
        er_zero = sem("er_zero")
        e_flags = sem("e_flags")
        e_nan = sem("e_nan")
        e_clean = sem("e_clean")
        d_eb = sem("d_eb")
        ey_out = sem("ey_out")
        d_exp = sem("d_exp")
        back_in = [sem(f"back_in{i}") for i in range(G)]
        fin_done = sem("fin_done")
        ctx_end = sem("ctx_end")
        cn_done = sem("cn_done")
        ct_mm = sem("ct_mm")
        ct_hi = sem("ct_hi")
        ct_lo = sem("ct_lo")
        cw_mm = sem("cw_mm")
        cw_hi = sem("cw_hi")
        cw_lo = sem("cw_lo")
        q_mm = sem("q_mm")
        q_read = sem("q_read")
        qe_done = sem("qe_done")
        qn_done = sem("qn_done")
        tq_mm = sem("tq_mm")
        tq_hi = sem("tq_hi")
        tq_lo = sem("tq_lo")
        at_mm = sem("at_mm")
        x1_done = sem("x1_done")
        z2_done = sem("z2_done")
        t2_mm = sem("t2_mm")
        t2_hi = sem("t2_hi")
        t2_lo = sem("t2_lo")
        f1_mm = sem("f1_mm")
        gelu_done = sem("gelu_done")
        hh_done = sem("hh_done")
        hl_done = sem("hl_done")
        y_mm = sem("y_mm")
        x2_done = sem("x2_done")
        d_head = sem("d_head")
        d_prep = sem("d_prep")
        d_ln1 = sem("d_ln1")
        d_sm = sem("d_sm")
        d_pre = sem("d_pre")
        d_ln2 = sem("d_ln2")
        d_kv = sem("d_kv")
        d_mid = sem("d_mid")
        d_q = sem("d_q")
        out_done = sem("out_done")

        block = ctx.enter_context(nc.Block())

        class Chain:

            def __init__(self, eng, s, r, n):
                self.eng, self.s, self.base, self.n, self.k = eng, s, r * n, n, 0

            def __call__(self, ins):
                self.k += 1
                ins.then_inc(self.s, 1)
                self.eng.wait_ge(self.s, self.base + self.k)

            def end(self):
                assert self.k == self.n, self.k

        def halves(b):
            return b.rearrange("p (k c) -> p k c", k=KD)

        x_t = A["x"].rearrange("(t p) d -> p t d", p=P)
        o_t = out.rearrange("(t p) d -> p t d", p=P)

        @block.sync
        def _(sp):
            for n in range(G):
                sp.dma_start(X[:, n * TG:(n + 1) * TG, :], x_t[:, n * TG:(n + 1) * TG, :]).then_inc(x_in, 16)
            sp.dma_start(EDI, A["edge_dst"]).then_inc(edges_in, 16)
            sp.dma_start(EIX[:, :], A["edge_src"]).then_inc(edges_in, 16)

            def w(name, l):
                return A["L0_mix_" + name][ds(l, 1), :, :].rearrange("a (k p) n -> p (a k) n", p=128)

            def early(l):
                sp.dma_start(VEC[:, :], A["mix_vec"][ds(l, 1), :, :].rearrange("a p n -> (a p) n")).then_inc(ln_in, 16)
                sp.dma_start(BR[:, :, :], A["mix_rows"][ds(l, 1), :, :, :].rearrange("a r n d -> (a r) n d")).then_inc(ln_in, 16)
                sp.dma_start(SKV[:, :, 0, :], w("Wk", l)).then_inc(kv_in, 16)
                sp.dma_start(SKV[:, :, 1, :], w("Wv", l)).then_inc(kv_in, 16)

            early(0)
            with sp.Fori(0, L) as l:
                sp.wait_ge(stage_free, l + 1)
                sp.dma_start(SQO[:, 0, :, :], w("Wq", l)).then_inc(qo_in, 16)
                sp.dma_start(SQO[:, 1, :, :], w("Wo", l)).then_inc(qo_in, 16)
                sp.dma_start(SW[:, :].rearrange("p (k n) -> p k n", k=KD), w("W1", l)).then_inc(w1_in, 16)
                for b in range(2):
                    sp.wait_ge(tab_out[b], 16 * (3 - b))
                sp.wait_ge(y_mm, l * T + 1)
                sp.dma_start(SW2.rearrange("p (k n) -> p k n", k=NF), w("W2", l)).then_inc(w2_in, 16)
                sp.wait_ge(early_free, l + 1)
                early((l + 1) % L)
            sp.wait_ge(y_mm, L * T + 1)
            for n, (dst, src) in enumerate(((GNW, A["L0_gnn_W"].rearrange("(k p) n -> p k n", p=128)),
                                            (GW, A["L0_ffn_gate_w"].rearrange("(k p) n -> p k n", p=128)),
                                            (GBR[:, :], A["L0_ffn_gate_b"].rearrange("(a n) -> a n", a=1)),
                                            (GNB, A["gnn_bias"]))):
                sp.dma_start(dst, src).then_inc(late_in, 16)
            for g in range(G):
                if g >= 1:
                    sp.wait_ge(xt_done, g * TG)
                sp.dma_start(QS[:, :, :], x_t[:, g * TG:(g + 1) * TG, :]).then_inc(xr_in, 16)

            rows = lambda ap, e: ap[ds(e * CP, CP), :].rearrange("(j p) n -> p j n", p=CT_)

            def load1(e):
                sp.dma_start(SE1, A["L0_ffn_w1"][ds(e, 1), :, :].rearrange("a (k p) n -> p (a k) n", p=128)).then_inc(e1_in, 16)

            def load2(e):
                sp.dma_start(SE2, A["L0_ffn_w2"][ds(e, 1), :, :].rearrange("a (k p) n -> p (a k) n", p=128)).then_inc(e2_in, 16)

            def store(e):
                sp.wait_ge(e_clean, e + 2)
                sp.dma_start(rows(YD, e), YR).then_inc(ey_out, 16)

            def expert(e, first=False, last=False):
                if not last:
                    sp.wait_ge(e1_lo, (e + 1) * 2)
                    load1(e + 1)
                    sp.wait_ge(et_mm, (e + 1) * 2)
                    sp.wait_ge(pw_done, e + 1)
                    sp.dma_start(BSI, rows(BUF, e + 1)).then_inc(slot_in, 16)
                if not first:
                    store(e - 1)
                if not last:
                    sp.wait_ge(e2_lo, (e + 1) * 4)
                    load2(e + 1)

            sp.wait_ge(gn_mm, T)
            load1(0)
            load2(0)
            sp.dma_start(EB1.rearrange("p (e f) -> p e f", e=EX), A["ffn_vec"].rearrange("e p f -> p e f")).then_inc(eb_in, 16)
            sp.dma_start(ERF.rearrange("p (e d) -> p e d", e=EX), A["ffn_rows"].rearrange("e r d -> r e d")).then_inc(eb_in, 16)
            sp.wait_ge(scattered, 16 * T)
            sp.dma_start(BSI, rows(BUF, 0)).then_inc(slot_in, 16)
            expert(0, first=True)
            with sp.Fori(1, EX - 1) as e:
                expert(e)
            expert(EX - 1, last=True)
            store(EX - 1)
            for g in range(G):
                sp.wait_ge(fin_done, (g + 1) * TG)
                sp.dma_start(o_t[:, g * TG:(g + 1) * TG, :], X[:, g * TG:(g + 1) * TG, :]).then_inc(out_done, 16)
            sp.wait_ge(out_done, 16 * G)

        @block.gpsimd
        def _(pool):
            n = [0]

            def step(ins):
                n[0] += 1
                ins.then_inc(pool_chain, 1)
                pool.wait_ge(pool_chain, n[0])

            step(pool.memset(ID[:, :], 0.0))
            step(pool.memset(IDH[:, :], 0.0))
            step(pool.affine_select(out=IDH[:, :], in_=IDH[:, :], compare_op=ALU.not_equal, fill=1.0, base=0,
                                    pattern=[[-1, 128]], channel_multiplier=1))
            step(pool.affine_select(out=ID[:, :], in_=ID[:, :], compare_op=ALU.not_equal, fill=1.0, base=0,
                                    pattern=[[-1, 128]], channel_multiplier=1))
            step(pool.memset(BM[:, :], 1.0))
            bm = BM[:, :].rearrange("p (h c) -> p h c", h=128 // DH)
            step(pool.affine_select(out=bm, in_=bm, compare_op=ALU.is_ge, fill=0.0, base=0,
                                    pattern=[[-DH, 128 // DH], [0, DH]], channel_multiplier=1))
            step(pool.affine_select(out=bm, in_=bm, compare_op=ALU.is_ge, fill=0.0, base=DH - 1,
                                    pattern=[[DH, 128 // DH], [0, DH]], channel_multiplier=-1))
            step(pool.memset(LOW[:, :], 0.0))
            step(pool.affine_select(out=LOW[:, :], in_=LOW[:, :], compare_op=ALU.not_equal, fill=1.0, base=-1,
                                    pattern=[[0, 1]], channel_multiplier=1))
            step(pool.memset(ONE[:, 0, :], 1.0))
            step(pool.memset(ONE[:, 1, :], QS_))
            step(pool.memset(ZR[:, :], 0.0))
            step(pool.memset(PPAD[:, :], 0.0))
            step(pool.memset(VH[:, :, :, 128:130], 1.0))
            step(pool.memset(VL[:, :, :, 128:130], 0.0))
            step(pool.iota(IOTA[:, :], [[1, 128]], base=0, channel_multiplier=0, allow_small_or_imprecise_dtypes=True))
            step(pool.iota(IOC[:, :], [[-1, EX]], base=EX, channel_multiplier=0, allow_small_or_imprecise_dtypes=True))
            step(pool.iota(IOE[:, :], [[CP, EX]], base=0, channel_multiplier=0, allow_small_or_imprecise_dtypes=True))
            step(pool.memset(ON1[:, :], 1.0))
            step(pool.memset(ONF[:, :], 1.0))
            step(pool.memset(AGG[:, :, N:NW], 0.0))
            step(pool.memset(TRI[:, :], 1.0))
            step(pool.affine_select(out=TRI[:, :], in_=TRI[:, :], compare_op=ALU.is_ge, fill=0.0, base=0,
                                    pattern=[[1, P]], channel_multiplier=-1))
            pool.memset(OH[:, :, :], 0.0).then_inc(const_done, 1)
            pool.wait_ge(const_done, 1)
            zero = OH[0:CT_, :, :].rearrange("p i n -> p (i n)").bitcast(i32)[:, 0:RW]
            for n in range(ZD):
                pool.dma_start(BUF[n * 2 * CT_:(n + 1) * 2 * CT_, :].rearrange("(p j) n -> p (j n)", j=2), zero).then_inc(zero_in, 16)

            pool.wait_ge(neg_done, 1)
            pool.partition_all_reduce(EDF, MIS[:, :], 128, RMAX).then_inc(par_done, 1)
            pool.wait_ge(neg_done, 2)
            pool.partition_all_reduce(FLG[:, :], FL1[:, :], 128, RMAX).then_inc(par_done, 1)

            pool.wait_ge(edges_in, 32)
            for b in range(2):
                pool.wait_ge(tab_out[b], 16 * (3 - b))
            with pool.Fori(0, L * G) as it:
                for b in range(NP_ // SLOTS):
                    pool.wait_ge(pair_mm, it * NP_ + b * SLOTS + 1)
                    cols = 2 * SLOTS
                    pool.tensor_copy(IB[:, b * cols:(b + 1) * cols], EIX[:, ds(it * EI + b * cols, cols)]).then_inc(idx_copied, 1)
                    pool.wait_ge(idx_copied, it * (NP_ // SLOTS) + b + 1)
                    for s in range(SLOTS):
                        q = b * SLOTS + s
                        pool.wait_ge(pair_mm, it * NP_ + q + 2)
                        pool.tensor_tensor(PPAD[:, 2 + q:3 + q], PPAD[:, 0:1], PPAD[:, 1:2], ALU.add)
                        for i in range(2):
                            pool.indirect_dma_start(
                                out=GB[:, s, i, :], out_offset=None, in_=TAB,
                                in_offset=bass.IndirectOffsetOnAxis(ap=IB[:, 2 * q + i:2 * q + i + 1], axis=0),
                            ).then_inc(gin[s], 16)

            with some_missed(pool, FLI[0:1, 0:1], base_done):
                pool.wait_ge(pair_mm, L * G * NP_ + SLOTS + 1)
                pool.sem_inc(miss_mm, 1)
                with pool.Fori(0, EW) as t:
                    pool.wait_ge(miss_mm, t * NWIN + 1)
                    pool.tensor_copy(IB[:, 0:1], EIX[:, ds(t, 1)]).then_inc(miss_idx, 1)
                    pool.wait_ge(miss_idx, t + 1)
                    pool.tensor_tensor(PPAD[:, 2:3], PPAD[:, 0:1], PPAD[:, 1:2], ALU.add)
                    pool.indirect_dma_start(out=GB[:, 0, 0, :], out_offset=None, in_=TAB,
                                            in_offset=bass.IndirectOffsetOnAxis(ap=IB[:, 0:1], axis=0)).then_inc(miss_in, 16)

            pool.sem_inc(ey_out, 16)
            pool.wait_ge(route_done, 1)
            pool.wait_ge(row_done, T)
            pool.wait_ge(zero_in, 16 * ZD)
            for t in range(T):
                pool.indirect_dma_start(out=BUF, out_offset=bass.IndirectOffsetOnAxis(ap=SIX[:, t:t + 1], axis=0),
                                        in_=ROWI[:, t, :], in_offset=None, bounds_check=EX * CP - 1,
                                        oob_is_err=False).then_inc(scattered, 16)
            with pool.Fori(0, EX) as e:
                pool.wait_ge(ey_out, e * 16 + 16)
                pool.tensor_tensor(PPAD[:, 2:3], PPAD[:, 0:1], PPAD[:, 1:2], ALU.add)
                pool.memset(YR, 0.0).then_inc(er_zero, 1)
                pool.wait_ge(ey_read, (e + 1) * NCT + 2)
                pool.tensor_tensor(PPAD[:, 3:4], PPAD[:, 0:1], PPAD[:, 1:2], ALU.add)
                pool.tensor_scalar(YF, YV, 0.0, 0.0, ALU.mult, ALU.is_equal).then_inc(e_flags, 1)
                pool.tensor_scalar(YC[:, :, :], YV, -1.0e4, 1.0e4, ALU.max, ALU.min).then_inc(e_flags, 1)
            pool.wait_ge(ey_out, 16 * EX + 16)
            pool.wait_ge(route_done, 2)
            for t in range(T):
                pool.indirect_dma_start(out=YG[:, t, :], out_offset=None, in_=YD,
                                        in_offset=bass.IndirectOffsetOnAxis(ap=GIX[:, t:t + 1], axis=0)).then_inc(back_in[t // TG], 16)

        @block.scalar
        def _(act):
            def kv_split(n):
                act.wait_ge(lnp_done, n * 3 + 1)
                act.wait_ge(kv_in, (n + 1) * 32)
                for k in range(KD):
                    act.activation(KVH[:, k, :, :], SKV[:, k, :, :], ACT.Copy, scale=G64[:, 0, k:k + 1]).then_inc(whk_done, 1)

            def hi_split(l):
                act.wait_ge(qo_in, (l + 1) * 32)
                for k in range(KD):
                    act.activation(QOH[:, 0, k, :], SQO[:, 0, k, :], ACT.Copy, scale=G64[:, 0, k:k + 1]).then_inc(whi_done, 1)
                act.activation(QOH[:, 1, :, :], SQO[:, 1, :, :], ACT.Copy, scale=WS).then_inc(whi_done, 1)
                act.wait_ge(w1_in, (l + 1) * 16)
                for k in range(KD):
                    act.activation(W1H[:, k, :], SW[:, k * FF:(k + 1) * FF], ACT.Copy, scale=G64[:, 1, k:k + 1]).then_inc(whi_done, 1)
                act.wait_ge(y_mm, l * T + 1)
                act.wait_ge(w2_in, (l + 1) * 16)
                act.activation(W2H[:, :, :], SW2.rearrange("p (k n) -> p k n", k=NF), ACT.Copy, scale=WS).then_inc(whi_done, 1)

            def z1_hi(g, n0, j):
                act.wait_ge(t1_mm, n0 + j + 1)
                act.activation(Z1H[:, :, ds((g * TG + j) * P, P)], halves(PT[j % 2][:, 0:2 * P]),
                               ACT.Copy).then_inc(t1_hi, 1)

            def head(l):
                act.wait_ge(kr_mm, l + 1)
                act.activation(KR[:, :], PA[0][0:1, 0:D], ACT.Copy, scale=-1.0).then_inc(kr_done, 1)

            def kv(l, g, it):
                for j in range(TG):
                    n = it * TG + j
                    act.wait_ge(kv_mm, n + 1)
                    act.wait_ge(el_done, n + 1 + (j == 0))
                    act.activation(EF[:, j % 2, :], PA[j % 2][0:P, 0:D], ACT.Exp, scale=SCALE / WS).then_inc(exp_done, 1)
                    act.wait_ge(ctx_mm, n + 1 + (j == 0))
                    act.activation(VH[:, j % 2, :, 0:128], halves(PA[j % 2][0:P, D:2 * D]), ACT.Copy,
                                   scale=1.0 / WS).then_inc(vh_done, 1)

            def mid(l):
                act.wait_ge(ct_mm, l + 1)
                act.activation(CTH[:, :, :], halves(PT[0][:, 0:D]), ACT.Copy).then_inc(ct_hi, 1)
                for h in range(KD):
                    act.wait_ge(cw_mm, l * KD + h + 1)
                    act.activation(CWH[:, h, :], PA[h][:, 0:D], ACT.Copy).then_inc(cw_hi, 1)

            def q_exp(it):
                act.wait_ge(q_read, (it + 1) * TG)
                act.activation(QS[:, :, :], QS[:, :, :], ACT.Exp, scale=SCALE / WS).then_inc(qe_done, 1)

            def q_hi(it, j):
                act.wait_ge(tq_mm, it * TG + j + 1)
                act.activation(QTH[:, :, j * P:(j + 1) * P], halves(PT[j % 2][:, 0:2 * P]), ACT.Copy,
                               scale=QS_).then_inc(tq_hi, 1)

            def z2_hi(it, j):
                act.wait_ge(t2_mm, it * TG + j + 1)
                act.activation(Z2H[:, :, j * P:(j + 1) * P], halves(PT[j % 2][:, 0:2 * P]),
                               ACT.Copy).then_inc(t2_hi, 1)

            def unit(it, u):
                n = it * 2 * NF + u
                t0, tn = CH[u // NF]
                f = u % NF
                act.wait_ge(f1_mm, n + 1)
                act.wait_ge(hl_done, n + 1)
                act.activation(HF[:, u % 2, 0:tn * P], PH[u % 2][:, 0:tn * P], ACT.Gelu, scale=1.0 / WS,
                               bias=B1C[:, f:f + 1]).then_inc(gelu_done, 1)
                act.wait_ge(gelu_done, n + 1)
                act.activation(HH[:, f, t0 * P:(t0 + tn) * P], HF[:, u % 2, 0:tn * P], ACT.Copy).then_inc(hh_done, 1)

            def body(g, it, first=False, last=False):
                if not last:
                    q_exp(it + 1)
                for u in range(2 * NF):
                    if not first and u in T1_AT:
                        z1_hi(g - 1, T + (it - 1) * TG, u - T1_AT[0])
                    if not last and u in TQ_AT:
                        q_hi(it + 1, u - TQ_AT[0])
                    unit(it, u)
                if not last:
                    for j in range(TG):
                        z2_hi(it + 1, j)

            for g in range(G):
                if g >= 1:
                    act.wait_ge(tab_out[(g - 1) % 2], 16 * ((g - 1) // 2 + 1))
                act.wait_ge(deg_mm, 1)
                act.wait_ge(xs_done, (g + 1) * TG)
                act.activation(TH[:, :, 0:D], ZN[:, :, :], ACT.Copy).then_inc(th_done, 1)
                for j in range(TG):
                    t = g * TG + j
                    act.wait_ge(xt_mm, t + 1)
                    act.activation(AGG[:, :, t * P:(t + 1) * P], halves(PT[j % 2][:, 0:2 * P]), ACT.Copy).then_inc(agg_init, 1)
                act.wait_ge(tl_done, g + 1)
                act.dma_start(TAB.rearrange("(t p) n -> p t n", p=P)[:, g * TG:(g + 1) * TG, :],
                              TH).then_inc(tab_out[g % 2], 16)
            act.wait_ge(tab_out[0], 48)
            with act.Fori(0, G) as g:
                for j in range(TG):
                    z1_hi(g, g * TG, j)
            kv_split(0)
            with act.Fori(0, L) as l:
                hi_split(l)
                head(l)
                with act.Fori(0, G) as g:
                    kv(l, g, l * G + g)
                mid(l)
                q_exp(l * G)
                for j in range(TG):
                    q_hi(l * G, j)
                for j in range(TG):
                    z2_hi(l * G, j)
                body(0, l * G, first=True)
                with act.Fori(1, G - 1) as g:
                    body(g, l * G + g)
                body(G - 1, l * G + G - 1, last=True)
                for j in range(TG):
                    z1_hi(G - 1, T + (l * G + G - 1) * TG, j)
                kv_split(l + 1)

            for g in range(G):
                act.wait_ge(zf_done, (g + 1) * TG)
                act.activation(ROW[:, g * TG:(g + 1) * TG, 0:D], ZN[:, :, :], ACT.Copy).then_inc(row_hi, 1)
                for j in range(TG):
                    t = g * TG + j
                    act.wait_ge(tf_mm, t + 1)
                    if t >= 2:
                        act.wait_ge(lg_mm, t - 1)
                    act.activation(EFT[:, j % 2, :], PT[j % 2][:, 0:2 * P], ACT.Copy).then_inc(tf_done, 1)
            act.sem_inc(er_done, 2)
            act.wait_ge(top_done, 1)
            act.activation(L2, L2, ACT.Exp).then_inc(es_done, 1)

            def high1(e):
                act.wait_ge(e1_in, (e + 1) * 16)
                for k in range(KD):
                    act.activation(W1H[:, k, :], SE1[:, k, :], ACT.Copy, scale=WS).then_inc(e1_hi, 1)

            def high2(e, c):
                if c == 0:
                    act.wait_ge(e2_in, (e + 1) * 16)
                    act.wait_ge(ey_mm, e * NCT + 1)
                f = slice(c * NF // 4, (c + 1) * NF // 4)
                act.activation(W2H[:, f, :], SE2[:, f, :], ACT.Copy, scale=WS).then_inc(e2_hi, 1)

            def rows_high(e):
                act.wait_ge(et_mm, e * 2 + 1)
                act.activation(BTH, PT[0][:, :].bitcast(f16)[:, 0:KD * CP].rearrange("p (k n) -> p k n", k=KD), ACT.Copy).then_inc(bt_hi, 1)

            def expert(e, last=False):
                for f in range(NF):
                    n = e * NF + f
                    act.wait_ge(e1_mm, n + 1)
                    act.wait_ge(ehl_done, n + 1)
                    act.activation(HF[:, f % 2, :], PH[f % 2][:, 0:CP], ACT.Relu, scale=1.0 / WS,
                                   bias=EB1[:, ds(e * NF + f, 1)]).then_inc(er_done, 1)
                    act.wait_ge(er_done, n + 3)
                    act.activation(HH[:, f, 0:CP], HF[:, f % 2, :], ACT.Copy).then_inc(eh_done, 1)
                    if f in W2_AT:
                        high2(e, W2_AT.index(f))
                if not last:
                    high1(e + 1)
                act.wait_ge(pw_done, e + 1)
                act.wait_ge(e_clean, e + 1)
                for j in range(NCT):
                    act.wait_ge(ey_mm, e * NCT + j + 2)
                    act.activation(YV[:, j, :], PA[j % 2][0:CT_, 0:D], ACT.Copy, scale=PW[:, ds(e * NCT + j, 1)]).then_inc(ey_read, 1)
                    if j == 0 and not last:
                        rows_high(e + 1)

            act.wait_ge(eb_in, 32)
            high1(0)
            rows_high(0)
            with act.Fori(0, EX - 1) as e:
                expert(e)
            expert(EX - 1, last=True)

        @block.vector
        def _(dve):
            dve.sem_inc(stage_free, 1)
            dve.sem_inc(el_done, 2)
            dve.sem_inc(hl_done, 2)

            def newton(ch, var, add, nt, ni):
                s = lambda n: nt[:, n, :]
                ch(dve.tensor_scalar(s(1), var, add, None, ALU.add))
                ch(dve.tensor_scalar(ni[:, :], s(1).bitcast(i32), 1, None, ALU.logical_shift_right))
                ch(dve.tensor_scalar(s(0).bitcast(i32), ni[:, :], -1.0, float(0x5f3759df), ALU.mult, ALU.add))
                for _ in range(3):
                    ch(dve.tensor_tensor(s(2), s(0), s(0), ALU.mult))
                    ch(dve.scalar_tensor_tensor(s(2), s(2), -0.5, s(1), ALU.mult, ALU.mult))
                    ch(dve.scalar_tensor_tensor(s(0), s(2), 1.5, s(0), ALU.add, ALU.mult))

            NEWTON = 12
            LN = NEWTON + 2

            def fill(column):
                dve.memset(PAD[:, column:column + 1], 0.0)

            def stats(st, j, t):
                return dve.bn_stats(st[:, j, :], t)

            def scale(ch, st, tiles, dst, done):
                fill(2 * TG + (st is ST2))
                for j in range(TG):
                    ins = dve.bn_aggr(MV[:, j, :], st[:, j, :])
                ch(ins)
                newton(ch, MV[:, :, 1], EPS, NT, NI)
                for j, t in enumerate(tiles):
                    dve.tensor_scalar(dst(j), t, MV[:, j, 0:1], NT[:, 0, j:j + 1], ALU.subtract, ALU.mult).then_inc(done, 1)

            def norm(ch, tiles, dst, done):
                fill(0)
                for j, t in enumerate(tiles):
                    ins = stats(ST, j, t)
                ch(ins)
                scale(ch, ST, tiles, dst, done)

            def tile(g, j):
                return X[:, ds(g * TG + j, 1), :].rearrange("p a d -> p (a d)")

            def tiles(g):
                return [tile(g, j) for j in range(TG)]

            def kv_split(n):
                dve.wait_ge(ln_in, (n + 1) * 32)
                dve.tensor_scalar(G64[:, 0, :], LNP[:, 0, :], WS, None, ALU.mult)
                dve.tensor_scalar(G64[:, 1, :], LNP[:, 2, :], WS, None, ALU.mult).then_inc(lnp_done, 1)
                for r in range(2):
                    dve.tensor_copy(B2[:, :, r], LNP[:, 1, :]).then_inc(lnp_done, 1)
                dve.wait_ge(lnp_done, n * 3 + 3)
                for k in range(KD):
                    dve.wait_ge(whk_done, n * KD + k + 1)
                    dve.scalar_tensor_tensor(KVL[:, k, :, :], SKV[:, k, :, :], G64[:, 0, k:k + 1], KVH[:, k, :, :],
                                             ALU.mult, ALU.subtract).then_inc(wlk_done, 1)

            def prep(l):
                ch = Chain(dve, d_prep, l, 6)
                n = l * 6
                units = iter([(m, c) for m in range(KD) for c in range(NK)])

                def maxima(count):
                    for _ in range(count):
                        m, c = next(units)
                        u = m * NK + c
                        dve.wait_ge(km_mm, l * KD * NK + u + 1)
                        dve.tensor_reduce(KM[:, m, c:c + 1], PH[u % 2][:, 0:KC[c + 1] - KC[c]], AX.X, ALU.max).then_inc(km_read, 1)

                def low(i, out, in0, by, hi):
                    dve.wait_ge(whi_done, n + i + 1)
                    dve.scalar_tensor_tensor(out, in0, by, hi, ALU.mult, ALU.subtract).then_inc(wlo_done, 1)

                dve.wait_ge(bq_mm, l + 1)
                dve.tensor_scalar(RF[:, 0, :], PA[0][0:2, 0:D], WS, None, ALU.mult).then_inc(rt_done, 1)
                dve.wait_ge(bv_mm, l + 1)
                for r in range(2):
                    ins = dve.tensor_copy(BV[:, :, r], PT[0][:, 0:KD])
                ins.then_inc(bv_done, 1)
                dve.wait_ge(b1_mm, l + 1)
                dve.tensor_tensor(B1C[:, :], PT[1][:, 0:NF], B1F, ALU.add).then_inc(rt_done, 1)
                maxima(2)
                for k in range(KD):
                    low(k, QOL[:, 0, k, :], SQO[:, 0, k, :], G64[:, 0, k:k + 1], QOH[:, 0, k, :])
                maxima(1)
                low(2, QOL[:, 1, :, :], SQO[:, 1, :, :], WS, QOH[:, 1, :, :])
                maxima(1)
                dve.wait_ge(bo_mm, l + 1)
                ch(dve.tensor_tensor(RF[:, 1, :], PA[1][0:2, 0:D], BR[:, 0, :], ALU.add))
                ch(dve.tensor_scalar(RF[:, 1, :], RF[:, 1, :], WS, None, ALU.mult))
                ch(dve.tensor_scalar(RF[:, 2, :], BR[:, 1, :], WS, None, ALU.mult))
                maxima(1)
                dve.wait_ge(rt_done, (l + 1) * 2)
                ch(dve.tensor_copy(RT[:, :, :], RF[:, :, :]))
                ch(dve.tensor_scalar(RM[:, :, :], RT[:, :, :], LOW[:, 0:1], None, ALU.mult))
                ch(dve.tensor_tensor(RB[:, :, :], RF[:, :, :], RM[:, :, :], ALU.subtract))
                ch.end()
                dve.sem_inc(rows_done, 1)
                maxima(1)
                for k in range(KD):
                    for h in range(2):
                        c = slice(h * FF // 2, (h + 1) * FF // 2)
                        dve.wait_ge(whi_done, n + 4 + k)
                        ins = dve.scalar_tensor_tensor(W1L[:, k, c], SW[:, k * FF + h * FF // 2:k * FF + (h + 1) * FF // 2],
                                                       G64[:, 1, k:k + 1], W1H[:, k, c], ALU.mult, ALU.subtract)
                        if h == 1:
                            ins.then_inc(wlo_done, 1)
                        maxima(1)
                w2 = SW2.rearrange("p (k n) -> p k n", k=NF)
                for h in range(4):
                    f = slice(h * NF // 4, (h + 1) * NF // 4)
                    dve.wait_ge(whi_done, n + 6)
                    ins = dve.scalar_tensor_tensor(W2L[:, f, :], w2[:, f, :], WS, W2H[:, f, :], ALU.mult, ALU.subtract)
                    if h == 3:
                        ins.then_inc(wlo_done, 1)
                    maxima(1)
                dve.wait_ge(wlo_done, (l + 1) * 6)
                dve.sem_inc(stage_free, 1)
                dve.sem_inc(early_free, 1)

            def z1_low(g, n0, j):
                dve.wait_ge(t1_hi, n0 + j + 1)
                cols = ds((g * TG + j) * P, P)
                dve.tensor_tensor(Z1L[:, :, cols], halves(PT[j % 2][:, 0:2 * P]), Z1H[:, :, cols],
                                  ALU.subtract).then_inc(t1_lo, 1)

            def head(l):
                dve.wait_ge(km_read, (l + 1) * KD * NK)
                dve.tensor_reduce(KX[:, :], KM[:, :, :], AX.X, ALU.max).then_inc(kx_done, 1)

            def kv(l, g, it):
                ch = Chain(dve, d_kv, it, TG)
                for j in range(TG):
                    n = it * TG + j
                    dve.wait_ge(exp_done, n + 1)
                    dve.wait_ge(ctx_mm, n + 1 + (j == 0))
                    ch(dve.tensor_scalar(EH[:, j % 2, :], EF[:, j % 2, :], ES, None, ALU.mult))
                    dve.scalar_tensor_tensor(EL[:, j % 2, :], EF[:, j % 2, :], ES, EH[:, j % 2, :],
                                             ALU.mult, ALU.subtract).then_inc(el_done, 1)
                    dve.wait_ge(vh_done, n + 1)
                    dve.scalar_tensor_tensor(VL[:, j % 2, :, 0:128], halves(PA[j % 2][0:P, D:2 * D]), 1.0 / WS,
                                             VH[:, j % 2, :, 0:128], ALU.mult, ALU.subtract).then_inc(vl_done, 1)
                ch.end()

            def mid(l):
                ch = Chain(dve, d_mid, l, 1)
                dve.wait_ge(ctx_end, l + 1)
                for h in range(KD):
                    ins = dve.reciprocal(RS[:, h:h + 1], PC[h][:, 128:129])
                ch(ins)
                for h in range(KD):
                    dve.scalar_tensor_tensor(CN[:, h, :], PC[h][:, 0:128], RS[:, h:h + 1], BM[:, :],
                                             ALU.mult, ALU.mult).then_inc(cn_done, 1)
                ch.end()
                dve.wait_ge(ct_hi, l + 1)
                dve.tensor_tensor(CTL[:, :, :], halves(PT[0][:, 0:D]), CTH[:, :, :], ALU.subtract).then_inc(ct_lo, 1)
                for h in range(KD):
                    dve.wait_ge(cw_hi, l * KD + h + 1)
                    dve.tensor_tensor(CWL[:, h, :], PA[h][:, 0:D], CWH[:, h, :], ALU.subtract).then_inc(cw_lo, 1)

            def q_max(it):
                ch = Chain(dve, d_q, it, TG)
                for j in range(TG):
                    dve.wait_ge(q_mm, it * TG + j + 1)
                    pq = PA[j % 2][0:P, 0:D].rearrange("p (h c) -> p h c", h=HEADS)
                    ch(dve.tensor_reduce(QM[:, j, :], pq, AX.X, ALU.max))
                    dve.tensor_tensor(QS[:, j, :].rearrange("p (h c) -> p h c", h=HEADS), pq,
                                      QM[:, j, :].unsqueeze(2).to_broadcast([P, HEADS, DH]), ALU.subtract).then_inc(q_read, 1)
                ch.end()

            def q_norm(it, j):
                ch = Chain(dve, d_sm, it * TG + j, 2)
                dve.wait_ge(qe_done, it + 1)
                qv = QS[:, j, :].rearrange("p (h c) -> p h c", h=HEADS)
                qr = QR[:, j * HEADS:(j + 1) * HEADS]
                ch(dve.tensor_reduce(qr, qv, AX.X, ALU.add))
                ch(dve.reciprocal(qr, qr))
                dve.tensor_tensor(qv, qv, qr.unsqueeze(2).to_broadcast([P, HEADS, DH]), ALU.mult).then_inc(qn_done, 1)
                ch.end()

            def q_low(it, j):
                dve.wait_ge(tq_hi, it * TG + j + 1)
                dve.scalar_tensor_tensor(QTL[:, :, j * P:(j + 1) * P], halves(PT[j % 2][:, 0:2 * P]), QS_,
                                         QTH[:, :, j * P:(j + 1) * P], ALU.mult, ALU.subtract).then_inc(tq_lo, 1)

            def x1(g, it):
                for j in range(TG):
                    dve.wait_ge(at_mm, it * TG + j + 1)
                    dve.scalar_tensor_tensor(tile(g, j), PA[j % 2][0:P, 0:D], 1.0 / (WS * QS_), tile(g, j),
                                             ALU.mult, ALU.add).then_inc(x1_done, 1)
                    if j >= 1:
                        dve.wait_ge(x1_done, it * TG + j)
                        fill(j - 1)
                        stats(ST, j - 1, tile(g, j - 1))
                ch = Chain(dve, d_ln2, it, LN)
                dve.wait_ge(x1_done, (it + 1) * TG)
                fill(TG - 1)
                ch(stats(ST, TG - 1, tile(g, TG - 1)))
                scale(ch, ST, tiles(g), lambda j: ZN2[:, j, :], z2_done)
                ch.end()

            def z2_low(it, j):
                dve.wait_ge(t2_hi, it * TG + j + 1)
                dve.tensor_tensor(Z2L[:, :, j * P:(j + 1) * P], halves(PT[j % 2][:, 0:2 * P]),
                                  Z2H[:, :, j * P:(j + 1) * P], ALU.subtract).then_inc(t2_lo, 1)

            def unit(it, u):
                t0, tn = CH[u // NF]
                f = u % NF
                dve.wait_ge(hh_done, it * 2 * NF + u + 1)
                cols = slice(t0 * P, (t0 + tn) * P)
                dve.tensor_tensor(HL[:, f, cols], HF[:, u % 2, 0:tn * P], HH[:, f, cols],
                                  ALU.subtract).then_inc(hl_done, 1)

            def x2(g, it, j):
                dve.wait_ge(y_mm, it * TG + j + 2)
                dve.scalar_tensor_tensor(tile(g, j), PA[j % 2][0:P, 0:D], 1.0 / WS, tile(g, j),
                                         ALU.mult, ALU.add).then_inc(x2_done, 1)
                if j >= 1:
                    dve.wait_ge(x2_done, it * TG + j + 1)
                    fill(TG + j - 1)
                    stats(ST2, j - 1, tile(g, j - 1))

            def z1(g, it):
                ch = Chain(dve, d_ln1, it, LN)
                dve.wait_ge(x2_done, (it + 1) * TG + 1)
                fill(2 * TG - 1)
                ch(stats(ST2, TG - 1, tile(g, TG - 1)))
                scale(ch, ST2, tiles(g), lambda j: ZN[:, j, :], z1_done)
                ch.end()

            def body(g, it, first=False, last=False):
                if not last:
                    q_max(it + 1)
                if not first:
                    z1(g - 1, it - 1)
                for u in range(2 * NF):
                    if u == 1:
                        onehot(it)
                    if not first and u in T1_AT:
                        z1_low(g - 1, T + (it - 1) * TG, u - T1_AT[0])
                    if not last and u in TQ_AT:
                        q_low(it + 1, u - TQ_AT[0])
                    unit(it, u)
                    if not last and NF - TG <= u < NF:
                        q_norm(it + 1, u - (NF - TG))
                if not last:
                    x1(g + 1, it + 1)
                for j in range(TG):
                    x2(g, it, j)
                    collect(it, 2 * j)
                    collect(it, 2 * j + 1)
                    if not last:
                        for i in T2_AT[j]:
                            z2_low(it + 1, i)

            def onehot(it):
                dve.wait_ge(zero_in, 16 * ZD)
                dve.wait_ge(pair_mm, it * NP_ + SLOTS + 1)
                dve.tensor_tensor(OH[:, :, :], IOTA[:, 0:W].unsqueeze(1).to_broadcast([128, EI, W]),
                                  REL[:, ds(it * EI, EI)].unsqueeze(2).to_broadcast([128, EI, W]), ALU.is_equal).then_inc(oh_done, 1)

            def collect(it, q):
                n = it * NP_ + q
                dve.wait_ge(pair_mm, n + 2 + SLOTS)
                dve.wait_ge(agg_done, n + 1)
                first = dve.value_load(BASE[0:1, ds(n, 1)], min_val=0, max_val=NW - W)
                o = AGG[:, :, ds(first, W)]
                dve.tensor_tensor(o, PC[q % 2][:, 0:2 * W].rearrange("p (k n) -> p k n", k=KD), o, ALU.add).then_inc(agg_done, 1)

            dve.wait_ge(x_in, 16 * G)
            ch0 = Chain(dve, d_head, 0, LN * G)
            for g in range(G):
                norm(ch0, [X[:, g * TG + j, :] for j in range(TG)], lambda j: X[:, g * TG + j, :], z1_done)
            ch0.end()
            dve.wait_ge(z1_done, T)

            ce = Chain(dve, d_edge, 0, 17)
            dve.wait_ge(edges_in, 32)
            ce(dve.tensor_copy(EDF, EDI))
            ce(dve.tensor_scalar(REL[:, :], EDF, 0.0, -BIG, ALU.is_lt, ALU.mult))
            dve.tensor_tensor(MIS[:, :], REL[:, :], EDF, ALU.subtract).then_inc(neg_done, 1)
            dve.wait_ge(par_done, 1)
            low = EDF.rearrange("p (q i) -> p q i", i=2)
            ce(dve.tensor_tensor(BSF, low[:, :, 0], low[:, :, 1], ALU.max))
            ce(dve.tensor_scalar(BSF, BSF, -1.0, float(NW - W), ALU.mult, ALU.min))
            ce(dve.tensor_copy(BASE[:, :], BSF))
            ce(dve.tensor_copy(EDF, EDI))
            ce(dve.tensor_tensor(REL[:, :].rearrange("p (q i) -> p q i", i=2), EDF.rearrange("p (q i) -> p q i", i=2),
                                 BSF.unsqueeze(2).to_broadcast([128, EW // 2, 2]), ALU.subtract))
            ce(dve.tensor_scalar(MIS[:, :], REL[:, :], 0.0, None, ALU.is_ge))
            ce(dve.scalar_tensor_tensor(MIS[:, :], REL[:, :], float(W), MIS[:, :], ALU.is_lt, ALU.mult))
            ce(dve.tensor_scalar(EDT, MIS[:, :], -1.0, 1.0, ALU.mult, ALU.add))
            ce(dve.tensor_tensor(EDT, EDT, EDF, ALU.mult))
            ce(dve.tensor_tensor(MIS[:, :], EDT, MIS[:, :], ALU.subtract))
            ce(dve.tensor_reduce(FL1[:, :], MIS[:, :], AX.X, ALU.max))
            dve.sem_inc(neg_done, 1)
            ce(dve.tensor_scalar(EHI, EDF, 1.0 / P, -0.496, ALU.mult, ALU.add))
            ce(dve.tensor_scalar(EHI, EHI, 12582912.0, 12582912.0, ALU.add, ALU.subtract))
            ce(dve.scalar_tensor_tensor(EDT, EHI, -float(P), EDF, ALU.mult, ALU.add))
            dve.wait_ge(par_done, 2)
            ce(dve.tensor_scalar(FLI[:, :], FLG[:, :], 0.0, None, ALU.is_ge))
            ce.end()
            dve.sem_inc(base_done, 1)

            dve.wait_ge(const_done, 1)
            dve.sem_inc(hist_mm, 2)
            with dve.Fori(0, EW // (2 * HB)) as r:
                for b in range(2):
                    dve.wait_ge(hist_mm, r * 2 + b + 1)
                    dve.tensor_tensor(OHH[:, b, :, :], IOTA[:, 0:T].unsqueeze(1).to_broadcast([128, HB, T]),
                                      EHI[:, ds((r * 2 + b) * HB, HB)].unsqueeze(2).to_broadcast([128, HB, T]), ALU.is_equal)
                    for i in range(HB):
                        ins = dve.tensor_scalar(OHL[:, b, i, :], IOTA[:, 0:P], EDT[:, ds((r * 2 + b) * HB + i, 1)], None, ALU.is_equal)
                    ins.then_inc(hist_oh, 1)
            dve.wait_ge(deg_mm, 1)
            cd = Chain(dve, d_fin, 0, NEWTON + 1)
            newton(cd, PH[0][0:P, 0:T], 1.0, DNT, DNI)
            dve.tensor_scalar(DO[:, :], DNT[:, 0, :], 1.0 / TS, None, ALU.mult)
            cd(dve.tensor_scalar(DT[:, :], DNT[:, 0, :], TS, None, ALU.mult))
            cd.end()
            for g in range(G):
                if g >= 1:
                    dve.wait_ge(th_done, g)
                    dve.wait_ge(xt_mm, g * TG)
                    dve.wait_ge(tl_done, g)
                for j in range(TG):
                    t = g * TG + j
                    dve.tensor_scalar(ZN[:, j, :], X[:, t, :], DT[:, t:t + 1], None, ALU.mult).then_inc(xs_done, 1)
                dve.wait_ge(th_done, g + 1)
                dve.tensor_tensor(TH[:, :, D:2 * D], ZN[:, :, :], TH[:, :, 0:D], ALU.subtract).then_inc(tl_done, 1)
            dve.wait_ge(tl_done, G)
            dve.wait_ge(xt_mm, T)
            dve.wait_ge(agg_init, T)
            dve.sem_inc(x2_done, 1)
            dve.sem_inc(vl_done, 1)
            dve.sem_inc(agg_done, 1)
            with dve.Fori(0, G) as g:
                ch = Chain(dve, d_pre, g, LN)
                norm(ch, tiles(g), lambda j: ZN[:, j, :], z1_done)
                ch.end()
                for j in range(TG):
                    z1_low(g, g * TG, j)
            kv_split(0)
            with dve.Fori(0, L) as l:
                prep(l)
                head(l)
                with dve.Fori(0, G) as g:
                    kv(l, g, l * G + g)
                mid(l)
                q_max(l * G)
                for j in range(TG):
                    q_norm(l * G, j)
                for j in range(TG):
                    q_low(l * G, j)
                x1(0, l * G)
                for j in range(TG):
                    z2_low(l * G, j)
                body(0, l * G, first=True)
                with dve.Fori(1, G - 1) as g:
                    body(g, l * G + g)
                body(G - 1, l * G + G - 1, last=True)
                z1(G - 1, l * G + G - 1)
                for j in range(TG):
                    z1_low(G - 1, T + (l * G + G - 1) * TG, j)
                kv_split(l + 1)

            with some_missed(dve, FLI[0:1, 0:1], base_done):
                dve.wait_ge(agg_done, L * G * NP_ + 1)
                with dve.Fori(0, EW) as t:
                    dve.tensor_copy(MW[:, :], MIS[:, ds(t, 1)]).then_inc(miss_col, 1)
                    with dve.Fori(0, NWIN) as w:
                        n = t * NWIN + w
                        dve.wait_ge(miss_mm, n + 1)
                        dve.wait_ge(miss_col, t * (NWIN + 1) + w + 1)
                        dve.tensor_scalar(OH[:, 0, :], IOTA[:, 0:W], MW[:, 0:1], None, ALU.is_equal).then_inc(miss_oh, 1)
                        dve.tensor_scalar(MW[:, :], MW[:, :], -float(W), None, ALU.add).then_inc(miss_col, 1)
                        dve.wait_ge(miss_mm, n + 2)
                        o = AGG[:, :, ds(w * W, W)]
                        dve.tensor_tensor(o, PC[0][:, 0:2 * W].rearrange("p (k n) -> p k n", k=KD), o, ALU.add).then_inc(miss_added, 1)
                        dve.wait_ge(miss_added, n + 1)

            cf = Chain(dve, d_route, 0, G * (LN + 4) + 15)
            dve.wait_ge(late_in, 64)
            dve.wait_ge(x2_done, L * T + 1)
            for g in range(G):
                for j in range(TG):
                    t = g * TG + j
                    dve.wait_ge(gn_mm, t + 1)
                    ins = dve.scalar_tensor_tensor(ZN2[:, j, :], PA[j % 2][0:P, 0:D], DO[:, t:t + 1], GNB, ALU.mult, ALU.add)
                    ins.then_inc(gn_read, 1)
                dve.wait_ge(gn_read, (g + 1) * TG)
                cf(dve.scalar_tensor_tensor(ZN2[:, :, :], ZN2[:, :, :], 0.2, ZN2[:, :, :], ALU.mult, ALU.max))
                xg = X[:, g * TG:(g + 1) * TG, :]
                cf(dve.tensor_tensor(xg, xg, ZN2[:, :, :], ALU.add))
                dve.wait_ge(xr_in, 16 * (g + 1))
                cf(dve.tensor_tensor(xg, xg, QS[:, :, :], ALU.add))
                dve.sem_inc(xt_done, TG)
                if g >= 1:
                    dve.wait_ge(row_done, g * TG)
                    dve.wait_ge(row_hi, g)
                    dve.wait_ge(tf_mm, g * TG)
                norm(cf, [X[:, g * TG + j, :] for j in range(TG)], lambda j: ZN[:, j, :], zf_done)
                cf(dve.memset(PAD[:, 0:1], 0.0))
                dve.wait_ge(row_hi, g + 1)
                dve.wait_ge(zf_done, (g + 1) * TG)
                dve.tensor_tensor(ROW[:, g * TG:(g + 1) * TG, D:2 * D], ZN[:, :, :], ROW[:, g * TG:(g + 1) * TG, 0:D],
                                  ALU.subtract).then_inc(row_done, TG)
                for j in range(TG):
                    t = g * TG + j
                    dve.wait_ge(lg_mm, t + 1)
                    dve.tensor_copy(LG[:, t, :], PH[j % 2][0:P, 0:EX]).then_inc(lg_read, 1)
            dve.wait_ge(lg_read, T)
            bc = lambda v: v.unsqueeze(2).to_broadcast([P, T, EX])
            be = lambda v: v.unsqueeze(1).to_broadcast([P, T, EX])
            r = lambda n: R1[:, n, :]
            cf(dve.tensor_reduce(r(0), LG, AX.X, ALU.max))
            dve.tensor_tensor(L2, LG, bc(r(0)), ALU.subtract).then_inc(top_done, 1)
            cf(dve.tensor_tensor(L1, LG, bc(r(0)), ALU.is_equal))
            cf(dve.tensor_tensor(L1, L1, be(IOC[:, :]), ALU.mult))
            cf(dve.tensor_reduce(r(1), L1, AX.X, ALU.max))
            cf(dve.tensor_tensor(LG, L1, bc(r(1)), ALU.is_equal))
            dve.tensor_copy(OE[:, :, :], LG).then_inc(oe_done, 1)
            dve.wait_ge(es_done, 1)
            cf(dve.tensor_reduce(r(2), L2, AX.X, ALU.add))
            cf(dve.reciprocal(r(2), r(2)))
            dve.wait_ge(row_done, T)
            dve.tensor_copy(ROW[:, :, 2 * D:RW].bitcast(f32), r(2).unsqueeze(2)).then_inc(row_done, 1)
            cf(dve.tensor_tensor(L1, LG, be(IOE[:, :]), ALU.mult))
            cf(dve.tensor_reduce(r(3), L1, AX.X, ALU.add))
            dve.wait_ge(pos_mm, 1)
            cf(dve.tensor_tensor(L1, PA[0][0:P, 0:T * EX].rearrange("p (t e) -> p t e", e=EX), LG, ALU.mult))
            cf(dve.tensor_reduce(r(4), L1, AX.X, ALU.add))
            cf(dve.tensor_scalar(r(5), r(4), float(C), None, ALU.is_le))
            cf(dve.scalar_tensor_tensor(r(0), r(4), -1.0, r(3), ALU.add, ALU.add))
            cf(dve.tensor_scalar(r(1), r(5), -BIG, BIG, ALU.mult, ALU.add))
            cf(dve.tensor_tensor(SIX[:, :], r(0), r(1), ALU.add))
            dve.tensor_scalar(r(4), r(4), float(C), -1.0, ALU.min, ALU.add).then_inc(route_done, 1)
            dve.wait_ge(route_done, 1)
            dve.tensor_tensor(GIX[:, :], r(4), r(3), ALU.add).then_inc(route_done, 1)
            cf.end()

            dve.sem_inc(ehl_done, 2)
            dve.sem_inc(ey_read, 2)
            dve.sem_inc(e_clean, 1)

            def low1(e):
                for k in range(KD):
                    dve.wait_ge(e1_hi, e * KD + k + 1)
                    dve.scalar_tensor_tensor(W1L[:, k, :], SE1[:, k, :], WS, W1H[:, k, :], ALU.mult, ALU.subtract).then_inc(e1_lo, 1)

            def low2(e, c):
                f = slice(c * NF // 4, (c + 1) * NF // 4)
                dve.wait_ge(e2_hi, e * 4 + c + 1)
                dve.scalar_tensor_tensor(W2L[:, f, :], SE2[:, f, :], WS, W2H[:, f, :], ALU.mult, ALU.subtract).then_inc(e2_lo, 1)

            def rows_low(e):
                dve.wait_ge(et_mm, e * 2 + 2)
                dve.tensor_copy(BTL, PT[1][:, :].bitcast(f16)[:, 0:KD * CP].rearrange("p (k n) -> p k n", k=KD)).then_inc(bt_lo, 1)
                dve.wait_ge(slot_in, (e + 1) * 16)
                dve.tensor_scalar(PW[:, ds(e * NCT, NCT)].unsqueeze(2), BS[:, :, 2 * D:RW].bitcast(f32), 1.0 / WS, None,
                                  ALU.mult).then_inc(pw_done, 1)

            def nans(e):
                dve.wait_ge(ey_read, (e + 1) * NCT + 2)
                dve.tensor_tensor(YE, YV, YV, ALU.is_equal).then_inc(e_nan, 1)

            def clean(e):
                ch = Chain(dve, d_exp, e, 1)
                dve.wait_ge(e_nan, e + 1)
                dve.wait_ge(er_zero, e + 1)
                dve.wait_ge(e_flags, (e + 1) * 2)
                fill(TG)
                ch(dve.copy_predicated(YR, YE.bitcast(i32), YC[:, :, :]))
                fill(TG + 1)
                dve.copy_predicated(YR, YF.bitcast(i32), YV).then_inc(e_clean, 1)
                ch.end()

            def expert(e, first=False, last=False):
                for f in range(NF):
                    dve.wait_ge(eh_done, e * NF + f + 1)
                    dve.tensor_tensor(HL[:, f, 0:CP], HF[:, f % 2, :], HH[:, f, 0:CP], ALU.subtract).then_inc(ehl_done, 1)
                    if f in W2_AT:
                        low2(e, W2_AT.index(f))
                    if f == CLEAN_AT and not first:
                        nans(e - 1)
                if not first:
                    clean(e - 1)
                if not last:
                    low1(e + 1)
                    rows_low(e + 1)

            ceb = Chain(dve, d_eb, 0, 3)
            dve.wait_ge(eb_in, 32)
            ceb(dve.tensor_scalar(ERF, ERF, WS, None, ALU.mult))
            ceb(dve.tensor_copy(ERT, ERF))
            ceb(dve.tensor_scalar(ERT, ERT, LOW[:, 0:1], None, ALU.mult))
            dve.tensor_tensor(ERB, ERF, ERT, ALU.subtract).then_inc(ebias_done, 1)
            ceb.end()
            low1(0)
            rows_low(0)
            expert(0, first=True)
            with dve.Fori(1, EX - 1) as e:
                expert(e)
            expert(EX - 1, last=True)
            nans(EX - 1)
            clean(EX - 1)
            for t in range(T):
                if t % TG == 0:
                    dve.wait_ge(back_in[t // TG], 16 * TG)
                dve.scalar_tensor_tensor(X[:, t, :], YG[:, t, :], R1[:, 5, t:t + 1], X[:, t, :], ALU.mult, ALU.add).then_inc(fin_done, 1)

        @block.tensor
        def _(pe):
            pe.sem_inc(ctx_mm, 2)
            pe.sem_inc(y_mm, 1)

            def three(o, st, mv, k, start=False, stop=False, **kw):
                n = 0
                for c in range(k):
                    for a, b in ((0, 0), (0, 1), (1, 0)):
                        ins = pe.matmul(o, st(a, c), mv(b, c), start=(start and n == 0), stop=(stop and n == 3 * k - 1), **kw)
                        n += 1
                return ins

            Z1 = (Z1H, Z1L)
            Z2 = (Z2H, Z2L)
            KV = (KVH, KVL)
            QO = (QOH, QOL)
            W1 = (W1H, W1L)
            W2 = (W2H, W2L)
            CT = (CTH, CTL)
            CW = (CWH, CWL)
            QT = (QTH, QTL)
            HX = (HH, HL)
            EXP = (EH, EL)
            VX = (VH, VL)

            def prep(l):
                pe.wait_ge(lnp_done, l * 3 + 3)
                pe.wait_ge(qo_in, (l + 1) * 32)
                pe.wait_ge(kv_in, (l + 1) * 32)
                pe.wait_ge(w1_in, (l + 1) * 16)
                pe.wait_ge(x2_done, l * T + 1)
                pe.wait_ge(t1_lo, (l + 1) * T)
                pe.wait_ge(wlk_done, (l + 1) * KD)
                for k in range(KD):
                    ins = pe.matmul(PA[0][0:2, 0:D], B2[:, k, :], SQO[:, 0, k, :], start=(k == 0), stop=(k == KD - 1))
                ins.then_inc(bq_mm, 1)
                for h in range(KD):
                    for k in range(KD):
                        ins = pe.matmul(PT[0][:, h:h + 1], SKV[:, k, 1, h * 128:(h + 1) * 128], B2[:, k, 0:1],
                                        start=(k == 0), stop=(k == KD - 1))
                ins.then_inc(bv_mm, 1)
                for f in range(NF):
                    for k in range(KD):
                        ins = pe.matmul(PT[1][:, f:f + 1], SW[:, k * FF + f * 128:k * FF + (f + 1) * 128],
                                        LNP[:, 3, k:k + 1], start=(k == 0), stop=(k == KD - 1))
                ins.then_inc(b1_mm, 1)
                for m in range(KD):
                    for c in range(NK):
                        u = m * NK + c
                        if u == 2:
                            pe.wait_ge(bv_done, l + 1)
                            for k in range(KD):
                                ins = pe.matmul(PA[1][0:2, 0:D], BV[:, k, :], SQO[:, 1, k, :], start=(k == 0), stop=(k == KD - 1))
                            ins.then_inc(bo_mm, 1)
                        if u >= 2:
                            pe.wait_ge(km_read, l * KD * NK + u - 1)
                        three(PH[u % 2][:, 0:KC[c + 1] - KC[c]], lambda a, k: KV[a][:, k, 0, m * 128:(m + 1) * 128],
                              lambda b, k: Z1[b][:, k, KC[c]:KC[c + 1]], KD, True, True).then_inc(km_mm, 1)

            def z1_t(g, n0, j):
                n = n0 + j
                pe.wait_ge(z1_done, T + n + 1)
                if j >= 2:
                    pe.wait_ge(t1_lo, n - 1)
                for h in range(KD):
                    ins = pe.transpose(PT[j % 2][:, h * P:(h + 1) * P], ZN[:, j, h * 128:(h + 1) * 128], ID[0:P, 0:P])
                ins.then_inc(t1_mm, 1)

            def head(l):
                pe.wait_ge(kx_done, l + 1)
                pe.wait_ge(rows_done, l + 1)
                pe.wait_ge(agg_done, l * G * NP_ + 1)
                for m in range(KD):
                    ins = pe.matmul(PA[0][0:1, m * 128:(m + 1) * 128], KX[:, m:m + 1], ID[:, :], start=True, stop=True)
                ins.then_inc(kr_mm, 1)
                for h in range(KD):
                    ins = pe.matmul(PC[h][:, 0:129], ZR[0:1, 0:128], ZR[0:1, 0:129], start=True, stop=False,
                                    skip_group_check=True)

            def kv(l, g, it):
                pe.wait_ge(kr_done, l + 1)
                for j in range(TG):
                    n = it * TG + j
                    t = g * TG + j
                    if j >= 2:
                        pe.wait_ge(vl_done, n)
                    else:
                        pe.wait_ge(vl_done, it * TG + 1)
                    o = PA[j % 2][0:P, 0:2 * D]
                    three(o, lambda a, k: Z1[a][:, k, ds(t * P, P)],
                          lambda b, k: KV[b][:, k, :, :].rearrange("p a d -> p (a d)"), KD, True, False, skip_group_check=True)
                    pe.matmul(PA[j % 2][0:P, 0:D], ONE[0:1, 0, 0:P], KR[0:1, :], start=False, stop=True,
                              skip_group_check=True).then_inc(kv_mm, 1)
                    if j > 0:
                        context(it, j - 1)
                context(it, TG - 1)

            def context(it, j):
                n = it * TG + j
                pe.wait_ge(el_done, n + 3)
                pe.wait_ge(vl_done, n + 1 + 1)
                for h in range(KD):
                    for a, b in ((0, 0), (0, 1), (1, 0)):
                        ins = pe.matmul(PC[h][:, 0:129], EXP[a][:, j % 2, h * 128:(h + 1) * 128], VX[b][:, j % 2, h, 0:129],
                                        start=False, stop=False, skip_group_check=True)
                ins.then_inc(ctx_mm, 1)

            def mid(l):
                for h in range(KD):
                    ins = pe.matmul(PC[h][:, 0:129], ZR[0:1, 0:128], ZR[0:1, 0:129], start=False, stop=True,
                                    skip_group_check=True)
                ins.then_inc(ctx_end, 1)
                pe.wait_ge(cn_done, (l + 1) * KD)
                for h in range(KD):
                    ins = pe.transpose(PT[0][:, h * 128:(h + 1) * 128], CN[:, h, :], ID[:, :])
                ins.then_inc(ct_mm, 1)
                pe.wait_ge(ct_lo, l + 1)
                for h in range(KD):
                    three(PA[h][:, 0:D], lambda a, k: CT[a][:, h, :], lambda b, k: QO[b][:, 1, h, :], 1,
                          True, True).then_inc(cw_mm, 1)

            def q(g, it, before):
                before()
                for j in range(TG):
                    n = it * TG + j
                    if j >= 2:
                        pe.wait_ge(q_read, n - 1)
                    o = PA[j % 2][0:P, 0:D]
                    pe.matmul(o, ONE[0:2, 0, 0:P], RB[:, 0, :], start=True, stop=False)
                    three(o, lambda a, k: Z1[a][:, k, ds((g * TG + j) * P, P)], lambda b, k: QO[b][:, 0, k, :], KD,
                          False, True).then_inc(q_mm, 1)

            def q_t(it, j):
                n = it * TG + j
                pe.wait_ge(qn_done, n + 1)
                if j >= 2:
                    pe.wait_ge(tq_lo, n - 1)
                for h in range(KD):
                    ins = pe.transpose(PT[j % 2][:, h * P:(h + 1) * P], QS[:, j, h * 128:(h + 1) * 128], ID[0:P, 0:P])
                ins.then_inc(tq_mm, 1)

            def attn(it):
                pe.wait_ge(q_read, (it + 1) * TG)
                for j in range(TG):
                    n = it * TG + j
                    pe.wait_ge(tq_lo, n + 1)
                    if j >= 2:
                        pe.wait_ge(x1_done, n - 1)
                    o = PA[j % 2][0:P, 0:D]
                    pe.matmul(o, ONE[0:2, 1, 0:P], RB[:, 1, :], start=True, stop=False)
                    three(o, lambda a, k: QT[a][:, k, j * P:(j + 1) * P], lambda b, k: CW[b][:, k, :], KD,
                          False, True).then_inc(at_mm, 1)

            def z2_t(it, j):
                n = it * TG + j
                pe.wait_ge(z2_done, n + 1)
                if j >= 2:
                    pe.wait_ge(t2_lo, n - 1)
                for h in range(KD):
                    ins = pe.transpose(PT[j % 2][:, h * P:(h + 1) * P], ZN2[:, j, h * 128:(h + 1) * 128], ID[0:P, 0:P])
                ins.then_inc(t2_mm, 1)

            def unit(it, u):
                t0, tn = CH[u // NF]
                f = u % NF
                n = it * 2 * NF + u
                if u >= 2:
                    pe.wait_ge(gelu_done, n - 1)
                else:
                    pe.wait_ge(hl_done, it * 2 * NF + 2)
                three(PH[u % 2][:, 0:tn * P], lambda a, k: W1[a][:, k, f * 128:(f + 1) * 128],
                      lambda b, k: Z2[b][:, k, t0 * P:(t0 + tn) * P], KD, True, True).then_inc(f1_mm, 1)

            def y(it, j):
                n = it * TG + j
                if j in (0, CH[1][0]):
                    pe.wait_ge(hl_done, it * 2 * NF + (NF if j == 0 else 2 * NF) + 2)
                if j >= 2:
                    pe.wait_ge(x2_done, n)
                o = PA[j % 2][0:P, 0:D]
                pe.matmul(o, ONE[0:2, 0, 0:P], RB[:, 2, :], start=True, stop=False)
                three(o, lambda a, f: HX[a][:, f, j * P:(j + 1) * P], lambda b, f: W2[b][:, f, :], NF,
                      False, True).then_inc(y_mm, 1)

            def body(g, it, first=False, last=False):
                if not last:
                    q(g + 1, it + 1, lambda: pe.wait_ge(x2_done, it * TG + 1) if not first else pe.wait_ge(x1_done, (it + 1) * TG))
                pe.wait_ge(t2_lo, (it + 1) * TG)
                for u in range(2 * NF):
                    if not first and u in T1_AT:
                        z1_t(g - 1, T + (it - 1) * TG, u - T1_AT[0])
                    if not last and u in TQ_AT:
                        if not first and u == TQ_AT[0]:
                            pe.wait_ge(t1_lo, T + it * TG)
                        q_t(it + 1, u - TQ_AT[0])
                    unit(it, u)
                if last:
                    pe.wait_ge(x2_done, it * TG + 1)
                else:
                    attn(it + 1)
                    pe.wait_ge(x1_done, (it + 2) * TG)
                for j in range(TG):
                    y(it, j)
                    pair(it, 2 * j)
                    pair(it, 2 * j + 1)
                    if not last:
                        for i in T2_AT[j]:
                            z2_t(it + 1, i)

            def route(g):
                for j in range(TG):
                    t = g * TG + j
                    pe.wait_ge(zf_done, t + 1)
                    if t >= 1:
                        pe.wait_ge(tf_done, max(1, t - 1 if j >= 2 else g * TG))
                    for h in range(KD):
                        ins = pe.transpose(PT[j % 2][:, h * P:(h + 1) * P], ZN[:, j, h * 128:(h + 1) * 128], ID[0:P, 0:P])
                    ins.then_inc(tf_mm, 1)
                    pe.wait_ge(tf_done, t + 1)
                    if t >= 1:
                        pe.wait_ge(lg_read, max(1, t - 1 if j >= 2 else g * TG))
                    o = PH[j % 2][0:P, 0:EX]
                    pe.matmul(o, ONF[:, :], GBR[:, :], start=True, stop=False)
                    for k in range(KD):
                        ins = pe.matmul(o, EFT[:, j % 2, k * P:(k + 1) * P], GW[:, k, :], start=False, stop=(k == KD - 1))
                    ins.then_inc(lg_mm, 1)

            def pair(it, q):
                n = it * NP_ + q
                s = q % SLOTS
                if q == 0:
                    pe.wait_ge(oh_done, it + 1)
                pe.wait_ge(gin[s], (it * (NP_ // SLOTS) + q // SLOTS + 1) * 32)
                if q < 2:
                    pe.wait_ge(agg_done, it * NP_ + 1)
                else:
                    pe.wait_ge(agg_done, n)
                for h in range(KD):
                    for i in range(2):
                        for part in range(2):
                            c = part * D + h * 128
                            ins = pe.matmul(PC[q % 2][:, h * W:(h + 1) * W], GB[:, s, i, c:c + 128], OH[:, 2 * q + i, :],
                                            start=(i + part == 0), stop=(i + part == 2))
                ins.then_inc(pair_mm, 1)

            pe.wait_ge(const_done, 1)
            pe.sem_inc(pair_mm, SLOTS + 1)
            deg = PH[0][0:P, 0:T]
            pe.matmul(deg, ZR[0:1, 0:P], ZR[0:1, 0:T], start=True, stop=False, skip_group_check=True)
            with pe.Fori(0, EW // (2 * HB)) as r:
                for b in range(2):
                    pe.wait_ge(hist_oh, r * 2 + b + 1)
                    for i in range(HB):
                        ins = pe.matmul(deg, OHL[:, b, i, :], OHH[:, b, i, :], start=False, stop=False, skip_group_check=True)
                    ins.then_inc(hist_mm, 1)
            pe.matmul(deg, ZR[0:1, 0:P], ZR[0:1, 0:T], start=False, stop=True, skip_group_check=True).then_inc(deg_mm, 1)
            for t in range(T):
                j = t % 2
                pe.wait_ge(xs_done, t + 1)
                if t % TG >= 2:
                    pe.wait_ge(agg_init, t - 1)
                elif t >= TG:
                    pe.wait_ge(agg_init, t // TG * TG)
                for h in range(KD):
                    b = t % TG % 2
                    ins = pe.transpose(PT[b][:, h * P:(h + 1) * P], ZN[:, t % TG, h * 128:(h + 1) * 128], ID[0:P, 0:P])
                ins.then_inc(xt_mm, 1)
            pe.wait_ge(agg_init, T)
            with pe.Fori(0, G) as g:
                for j in range(TG):
                    z1_t(g, g * TG, j)
                pe.wait_ge(t1_lo, (g + 1) * TG)
            with pe.Fori(0, L) as l:
                prep(l)
                head(l)
                with pe.Fori(0, G) as g:
                    kv(l, g, l * G + g)
                mid(l)
                q(0, l * G, lambda: pe.wait_ge(cw_lo, (l + 1) * KD))
                for j in range(TG):
                    q_t(l * G, j)
                attn(l * G)
                for j in range(TG):
                    z2_t(l * G, j)
                pe.wait_ge(wlo_done, (l + 1) * 6)
                body(0, l * G, first=True)
                with pe.Fori(1, G - 1) as g:
                    body(g, l * G + g)
                body(G - 1, l * G + G - 1, last=True)
                pe.wait_ge(t1_lo, T + (l * G + G - 1) * TG)
                for j in range(TG):
                    z1_t(G - 1, T + (l * G + G - 1) * TG, j)

            with some_missed(pe, FLI[0:1, 0:1], base_done):
                with pe.Fori(0, EW) as t:
                    with pe.Fori(0, NWIN) as w:
                        n = t * NWIN + w
                        pe.wait_ge(miss_in, t * 16 + 16)
                        pe.wait_ge(miss_oh, n + 1)
                        for h in range(KD):
                            for part in range(2):
                                c = part * D + h * 128
                                ins = pe.matmul(PC[0][:, h * W:(h + 1) * W], GB[:, 0, 0, c:c + 128], OH[:, 0, :],
                                                start=(part == 0), stop=(part == 1))
                        ins.then_inc(miss_mm, 1)
                pe.wait_ge(miss_added, EW * NWIN)

            pe.wait_ge(agg_done, L * G * NP_ + 1)
            pe.wait_ge(late_in, 64)
            pe.wait_ge(x2_done, L * T + 1)
            for t in range(T):
                j = t % TG
                if t >= 2:
                    pe.wait_ge(gn_read, t - 1 if j >= 2 else t // TG * TG)
                for k in range(KD):
                    ins = pe.matmul(PA[j % 2][0:P, 0:D], AGG[:, k, t * P:(t + 1) * P], GNW[:, k, :], start=(k == 0), stop=(k == KD - 1))
                ins.then_inc(gn_mm, 1)
                if j == TG - 1:
                    route(t // TG)

            pe.wait_ge(oe_done, 1)
            pe.wait_ge(gn_read, T)
            pos = PA[0][0:P, 0:T * EX]
            pe.matmul(pos, TRI[:, :], OE[:, :, :].rearrange("p t e -> p (t e)"), start=True, stop=False, skip_group_check=True)
            for t in range(T - 1):
                ins = pe.matmul(PA[0][0:P, (t + 1) * EX:T * EX].rearrange("p (t e) -> p t e", e=EX), ON1[:, :],
                                OE[:, t, :].unsqueeze(1).to_broadcast([P, T - 1 - t, EX]), start=False, stop=(t == T - 2),
                                skip_group_check=True)
            ins.then_inc(pos_mm, 1)

            pe.sem_inc(ey_mm, 1)
            pe.wait_ge(route_done, 2)
            BT = (BTH, BTL)

            def rows_t(e, part):
                if part == 0:
                    pe.wait_ge(slot_in, (e + 1) * 16)
                o = PT[part][:, :].bitcast(f16)
                for k in range(KD):
                    for j in range(NCT):
                        c = part * D + k * 128
                        ins = pe.transpose(o[:, k * CP + j * CT_:k * CP + (j + 1) * CT_], BS[:, j, c:c + 128], IDH[0:CT_, 0:CT_])
                ins.then_inc(et_mm, 1)

            def expert(e, last=False):
                pe.wait_ge(bt_hi, e + 1)
                pe.wait_ge(bt_lo, e + 1)
                pe.wait_ge(e1_lo, (e + 1) * 2)
                for f in range(NF):
                    n = e * NF + f
                    pe.wait_ge(er_done, n + 1)
                    three(PH[f % 2][:, 0:CP], lambda a, k: W1[a][:, k, f * 128:(f + 1) * 128], lambda b, k: BT[b][:, k, :],
                          KD, True, True).then_inc(e1_mm, 1)
                pe.wait_ge(ehl_done, (e + 1) * NF + 2)
                pe.wait_ge(e2_lo, (e + 1) * 4)
                for j in range(NCT):
                    n = e * NCT + j
                    pe.wait_ge(ey_read, n + 1)
                    o = PA[j % 2][0:CT_, 0:D]
                    three(o, lambda a, f: HX[a][:, f, j * CT_:(j + 1) * CT_], lambda b, f: W2[b][:, f, :], NF, True, False)
                    pe.matmul(o, ONE[0:2, 0, 0:CT_], ERB[:, ds(e * D, D)], start=False, stop=True).then_inc(ey_mm, 1)
                    if j < 2 and not last:
                        rows_t(e + 1, j)

            pe.wait_ge(ebias_done, 1)
            rows_t(0, 0)
            rows_t(0, 1)
            with pe.Fori(0, EX - 1) as e:
                expert(e)
            expert(EX - 1, last=True)


def kernel(**inputs):
    import numpy as _np
    import concourse.bacc as _bacc
    from concourse import mybir as _mybir
    from concourse.bass_utils import run_bass_kernel_spmd as _run

    nc = _bacc.Bacc("TRN2", target_bir_lowering=False, num_devices=1)
    arrays, args = {}, {}
    mix = {name[7:]: _np.asarray(value) for name, value in inputs.items() if name.startswith("L0_mix_")}
    columns = [mix[n].reshape(mix[n].shape[0], -1, 128).transpose(0, 2, 1) for n in ("ln1_g", "ln1_b", "ln2_g", "ln2_b", "b1")]
    rows = _np.stack([mix["bo"], mix["b2"]], axis=1)
    laid = dict(inputs, mix_vec=_np.concatenate(columns, axis=2), mix_rows=_np.stack([rows, rows], axis=1))
    for name in ("ln1_g", "ln1_b", "ln2_g", "ln2_b", "b1", "bo", "b2"):
        del laid["L0_mix_" + name]
    tiles = 400
    for name, pad in (("src", 0), ("dst", -1)):
        a = _np.asarray(laid.pop(name))
        a = _np.concatenate([a, _np.full(tiles * 128 - a.shape[0], pad, a.dtype)])
        laid["edge_" + name] = a.reshape(tiles, 128).T
    laid["gnn_bias"] = _np.tile(_np.asarray(laid.pop("L0_gnn_b"))[None, :], (125, 1))
    b1, b2 = _np.asarray(laid.pop("L0_ffn_b1")), _np.asarray(laid.pop("L0_ffn_b2"))
    laid["ffn_vec"] = b1.reshape(b1.shape[0], -1, 128).transpose(0, 2, 1)
    laid["ffn_rows"] = _np.stack([b2, b2], axis=1)
    for name, value in laid.items():
        a = _np.ascontiguousarray(value)
        arrays[f"in_{name}"] = a
        args[name] = nc.dram_tensor(f"in_{name}", a.shape, _mybir.dt.from_np(a.dtype), kind="ExternalInput").ap()
    out = nc.dram_tensor("out_0", (3125, 256), _mybir.dt.float32, kind="ExternalOutput").ap()
    build(nc, args, out)
    r = _run(nc, [arrays], core_ids=[0])
    return r.results[0]["out_0"]
```

```python
import concourse.bass as bass
from concourse import mybir
from contextlib import ExitStack

def build(nc, A, out):
    f32 = mybir.dt.float32
    f16 = mybir.dt.float16
    i32 = mybir.dt.int32
    ALU = mybir.AluOpType
    ACT = mybir.ActivationFunctionType
    AX = mybir.AxisListType
    ds = bass.ds

    def some_missed(eng, flag, ready):
        eng.wait_ge(ready, 1)
        return eng.If(eng.value_load(flag, min_val=0, max_val=1) != 0)

    RMAX = bass.bass_isa.ReduceOp.max

    N, D = A["x"].shape
    L = A["L0_mix_Wq"].shape[0]
    FF = A["L0_mix_W1"].shape[2]
    P = 125
    T = N // P
    TG = 5
    G = T // TG
    NG = P * TG
    KD = D // 128
    NF = FF // 128
    HEADS, DH = 8, 32
    CH = [(0, 3), (3, 2)]
    EPS = 1e-5
    SCALE = DH ** -0.25
    WS = 64.0
    QS_ = 1024.0
    ES = 4096.0
    PEEL = 13
    PER = 4
    WLO = 3 + 2 * 4
    W = 96
    TS = 256.0
    EW = A["edge_src"].shape[1]
    EI = EW // (L * G)
    NP_ = EI // 2
    NQ = NP_ // 2
    SLOTS = 5
    EX = A["L0_ffn_w1"].shape[0]
    C = -(-5 * N // (4 * EX))
    CT_ = 124
    NCT = -(-C // CT_)
    CP = CT_ * NCT
    RW = 2 * D + 2
    BIG = 1.0e6
    ZD = EX * CP // (2 * CT_)
    Z1_AT = ((0, 1), (2, 3), (4,), ())
    HQ = len(Z1_AT)
    HA = 9
    START = ((0, 1), (2, 3), (4,))
    T1_AT = range(2, 2 + TG)
    TQ_AT = range(NF + 2, NF + 2 + TG)
    KM_AT = range(NF + 3, NF + 3 + 2 * KD)
    T2_AT = ((), (), (0, 1), (2, 3), (4,))
    Q_AT = ((0, 1), (2, 3), (4,), (), ())
    Q_END = 2
    P_AT = ((0, 1, 2), (3, 4), (5, 6), (7, 8), (9,))
    QN_AHEAD = range(2)
    QN_AT = range(NF - 3, NF)
    RING = 4
    W2_AT = (0, 2, 4, 5)
    CLEAN_AT = 3
    assert len(QN_AHEAD) + len(QN_AT) == TG and T * P == N and G * TG == T and (T - PEEL) % PER == 0 and EI * L * G == EW and CP <= 512

    ctx = ExitStack()
    with ctx:
        def sb(name, shape, dt):
            return ctx.enter_context(nc.sbuf_tensor(name, shape, dt))

        def pb(name):
            return ctx.enter_context(nc.psum_tensor(name, [128, 512], f32))

        def sem(name):
            return ctx.enter_context(nc.semaphore(name))

        X = sb("X", [P, T, D], f32)
        ZB = sb("ZB", [128, T * RW], f16)
        Z1H = ZB[:, 0:KD * N].rearrange("p (k n) -> p k n", k=KD)
        Z1L = ZB[:, KD * N:2 * KD * N].rearrange("p (k n) -> p k n", k=KD)
        ROW = ZB[0:P, :].rearrange("p (t n) -> p t n", t=T)
        ROWI = ZB[0:P, :].bitcast(i32).rearrange("p (t n) -> p t n", t=T)
        NWIN = -(-N // W)
        NW = NWIN * W
        AB = sb("AB", [128, T * D], f32)
        AGG = AB[:, 0:KD * NW].rearrange("p (k n) -> p k n", k=KD)
        YG = AB[0:P, :].rearrange("p (t d) -> p t d", t=T)
        SW = sb("SW", [128, KD * FF], f32)
        GB = sb("GB", [128, SLOTS, 2, 2 * D], f16)
        OH = sb("OH", [128, EI, W], f16)
        EIX = sb("EIX", [128, EW], i32)
        REL = sb("REL", [128, EW], f32)
        MIS = sb("MIS", [128, EW], f32)
        slot = lambda n, dt: GB[:, n, :, :].rearrange("p i n -> p (i n)").bitcast(dt)
        EDI = slot(0, i32)[:, 0:EW]
        EDF = slot(1, f32)[:, 0:EW]
        EDT = slot(2, f32)[:, 0:EW]
        EHI = slot(3, f32)[:, 0:EW]
        BSF = slot(4, f32)[:, 0:EW // 4]
        IB = sb("IB", [128, EI], i32)
        BASE = sb("BASE", [128, EW // 4], i32)
        DNT = sb("DNT", [P, 3, T], f32)
        DNI = sb("DNI", [P, T], i32)
        DT = sb("DT", [P, T], f32)
        DO = sb("DO", [P, T], f32)
        ZN = sb("ZN", [P, TG, D], f32)
        ZN2 = sb("ZN2", [P, TG, D], f32)
        Z2B = sb("Z2B", [128, 2 * KD * NG], f16)
        Z2H = Z2B[:, 0:KD * NG].rearrange("p (k n) -> p k n", k=KD)
        Z2L = Z2B[:, KD * NG:2 * KD * NG].rearrange("p (k n) -> p k n", k=KD)
        SKV = sb("SKV", [128, KD, 2, D], f32)
        SQO = sb("SQO", [128, 2, KD, D], f32)
        KVH = sb("KVH", [128, KD, 2, D], f16)
        KVL = sb("KVL", [128, KD, 2, D], f16)
        QOH = sb("QOH", [128, 2, KD, D], f16)
        QOL = sb("QOL", [128, 2, KD, D], f16)
        W1H = sb("W1H", [128, KD, FF], f16)
        W1L = sb("W1L", [128, KD, FF], f16)
        W2H = sb("W2H", [128, NF, D], f16)
        W2L = sb("W2L", [128, NF, D], f16)
        VEC = sb("VEC", [128, 4 * KD + NF], f32)
        LNP = VEC[:, 0:4 * KD].rearrange("p (n k) -> p n k", n=4)
        B1F = VEC[:, 4 * KD:4 * KD + NF]
        G64 = sb("G64", [128, 2, KD], f32)
        B2 = sb("B2", [128, KD, 2], f32)
        B1C = sb("B1C", [128, NF], f32)
        BR = sb("BR", [2, 2, D], f32)
        BV = sb("BV", [128, KD, 2], f32)
        RF = sb("RF", [2, 3, D], f32)
        RT = sb("RT", [2, 3, D], f16)
        RM = sb("RM", [2, 3, D], f16)
        RB = sb("RB", [2, 3, D], f16)
        LOW = sb("LOW", [2, 1], f32)
        ONE = sb("ONE", [2, 2, 128], f16)
        ZR = sb("ZR", [1, 512], f16)
        ID = sb("ID", [128, 128], f32)
        IDH = sb("IDH", [128, 128], f16)
        BM = sb("BM", [128, 128], f32)
        KM = sb("KM", [128, KD, 2 * G], f32)
        KX = sb("KX", [128, KD], f32)
        KR = sb("KR", [1, D], f16)
        VH = sb("VH", [P, 2, KD, 130], f16)
        VL = sb("VL", [P, 2, KD, 130], f16)
        RS = sb("RS", [128, KD], f32)
        CN = sb("CN", [128, KD, 128], f32)
        CTH = sb("CTH", [128, KD, 128], f16)
        CTL = sb("CTL", [128, KD, 128], f16)
        CWH = sb("CWH", [128, KD, D], f16)
        CWL = sb("CWL", [128, KD, D], f16)
        QM = sb("QM", [P, TG, HEADS], f32)
        QS = sb("QS", [P, TG, D], f32)
        EF = QS[:, 0:2, :]
        EH = QS[:, 2, :].bitcast(f16).rearrange("p (b d) -> p b d", b=2)
        EL = QS[:, 3, :].bitcast(f16).rearrange("p (b d) -> p b d", b=2)
        QR = sb("QR", [P, TG * HEADS], f32)
        QTB = sb("QTB", [128, 2 * KD * NG], f16)
        QTH = QTB[:, 0:KD * NG].rearrange("p (k n) -> p k n", k=KD)
        QTL = QTB[:, KD * NG:2 * KD * NG].rearrange("p (k n) -> p k n", k=KD)
        HFB = sb("HFB", [128, RING * CH[0][1] * P], f32)
        HF = HFB[:, :].rearrange("p (b n) -> p b n", b=RING)
        HE = HFB[:, 0:3 * CP].rearrange("p (b n) -> p b n", b=3)
        HHB = sb("HHB", [128, NF * NG], f16)
        HH = HHB[:, :].rearrange("p (f n) -> p f n", f=NF)
        HLB = sb("HLB", [128, NF * NG], f16)
        HL = HLB[:, :].rearrange("p (f n) -> p f n", f=NF)
        HB = EI
        SW2 = HHB[:, :].bitcast(f32)[:, 0:NF * D]
        OHL = HHB[:, :].rearrange("p (b i n) -> p b i n", b=2, n=P)
        OHH = HLB[:, 0:2 * HB * T].rearrange("p (b i n) -> p b i n", b=2, n=T)
        th = lambda b: b[0:P, 0:TG * 2 * D].rearrange("p (j n) -> p j n", j=TG)
        TH = (th(HHB[:, :]), th(HLB[:, :]))
        EDN = slot(4, f32)[:, 0:EW]
        ST0 = CN[:, :, :].rearrange("p k n -> p (k n)")[0:P, 0:6 * T].rearrange("p (t n) -> p t n", t=T)
        MV0 = CN[:, :, :].rearrange("p k n -> p (k n)")[0:P, 6 * T:8 * T].rearrange("p (t n) -> p t n", t=T)
        IOTA = sb("IOTA", [128, 128], f16)
        IOC = sb("IOC", [P, EX], f32)
        IOE = sb("IOE", [P, EX], f32)
        TRI = sb("TRI", [P, P], f16)
        ON1 = sb("ON1", [P, P], f16)
        ONF = sb("ONF", [1, P], f32)
        GBR = sb("GBR", [1, EX], f32)
        GNW = SW[:, 0:KD * D].rearrange("p (k n) -> p k n", k=KD)
        GNB = SW[0:P, KD * D:(KD + 1) * D]
        GW = SW[:, (KD + 1) * D:(KD + 1) * D + KD * EX].rearrange("p (k n) -> p k n", k=KD)
        SKF = SKV[:, :, :, :].rearrange("p k a d -> p (k a d)")
        xr = lambda b: b[0:P, 0:2 * TG * D].bitcast(f32).rearrange("p (j n) -> p j n", j=TG)
        XR = (QS[:, :, :], xr(HHB[:, :]), xr(HLB[:, :]))
        lg = lambda n: SKF[0:P, n * T * EX:(n + 1) * T * EX].rearrange("p (t e) -> p t e", e=EX)
        LG, L1, L2 = lg(0), lg(1), lg(2)
        OE = sb("OE", [P, T, EX], f16)
        R1 = sb("R1", [P, 6, T], f32)
        SIX = sb("SIX", [P, T], i32)
        PW = sb("PW", [CT_, EX * NCT], f32)
        MW = sb("MW", [128, 1], f32)
        FL1 = sb("FL1", [128, 1], f32)
        FLG = sb("FLG", [128, 1], f32)
        FLI = sb("FLI", [128, 1], i32)
        GIX = sb("GIX", [P, T], i32)
        ST = sb("ST", [P, TG, 6], f32)
        MV = sb("MV", [P, TG, 2], f32)
        ST2 = sb("ST2", [P, TG, 6], f32)
        NT = sb("NT", [P, 3, TG], f32)
        PAD = sb("PAD", [P, 2 * TG + 4], f32)
        PPAD = sb("PPAD", [128, 2 + NP_], f32)
        NI = DNI[:, 0:TG]

        TAB = nc.dram_tensor("node_table", (N, 2 * D), f16).ap()
        BUF = nc.dram_tensor("dispatched", (EX * CP, RW // 2), i32).ap()
        YD = nc.dram_tensor("expert_out", (EX * CP, D), f32).ap()

        PT = [pb("PT0"), pb("PT1")]
        PA = [pb("PA0"), pb("PA1")]
        PH = [pb("PH0"), pb("PH1")]
        PC = [pb("PC0"), pb("PC1")]

        EFT = KVH[:, :, :, :].rearrange("p k a d -> p (k a d)").bitcast(f32)[:, 0:4 * P].rearrange("p (b n) -> p b n", b=2)
        BSI = QTB[0:CT_, :].bitcast(i32)[:, 0:NCT * RW // 2].rearrange("p (j n) -> p j n", j=NCT)
        EWT = AB[:, 0:2 * KD * FF].rearrange("p (b n) -> p b n", b=2)
        SE1 = EWT[:, 0, :].rearrange("p (k n) -> p k n", k=KD)
        SE2 = EWT[:, 1, :].rearrange("p (k n) -> p k n", k=NF)
        ERF = AB[0:2, 2 * KD * FF:2 * KD * FF + EX * D]
        GBF = GB[0:2, :, :, :].rearrange("p s i n -> p (s i n)")
        ERT = GBF[:, 0:EX * D]
        ERB = GBF[:, EX * D:2 * EX * D]
        EB1 = MIS[:, 0:EX * NF]
        BS = QTB[0:CT_, 0:NCT * RW].rearrange("p (j n) -> p j n", j=NCT)
        BTH = Z2B[:, 0:KD * CP].rearrange("p (k n) -> p k n", k=KD)
        BTL = Z2B[:, KD * CP:2 * KD * CP].rearrange("p (k n) -> p k n", k=KD)
        YV = ZN[0:CT_, 0:NCT, :]
        YC = QS[0:CT_, 0:NCT, :]
        YR = ZN2[0:CT_, 0:NCT, :]
        YF = SQO[0:CT_, :, :, :].rearrange("p a k d -> p (a k) d")
        YE = SKV[0:CT_, :, :, :].rearrange("p a k d -> p (a k) d")
        x_in = sem("x_in")
        const_done = sem("const_done")
        pool_chain = sem("pool_chain")
        kv_in = sem("kv_in")
        qo_in = sem("qo_in")
        w1_in = sem("w1_in")
        w2_in = sem("w2_in")
        ln_in = sem("ln_in")
        stage_free = sem("stage_free")
        early_free = sem("early_free")
        whk_done = sem("whk_done")
        wlk_done = sem("wlk_done")
        lnp_done = sem("lnp_done")
        whi_done = sem("whi_done")
        wlo_done = sem("wlo_done")
        bq_mm = sem("bq_mm")
        b1_mm = sem("b1_mm")
        bo_mm = sem("bo_mm")
        bv_done = sem("bv_done")
        rows_done = sem("rows_done")
        rt_done = sem("rt_done")
        z1_done = sem("z1_done")
        t1_mm = sem("t1_mm")
        t1_hi = sem("t1_hi")
        t1_lo = sem("t1_lo")
        km_mm = sem("km_mm")
        km_read = sem("km_read")
        kx_done = sem("kx_done")
        kr_mm = sem("kr_mm")
        kr_done = sem("kr_done")
        kv_mm = sem("kv_mm")
        exp_done = sem("exp_done")
        vh_done = sem("vh_done")
        vl_done = sem("vl_done")
        el_done = sem("el_done")
        ctx_mm = sem("ctx_mm")
        edges_in = sem("edges_in")
        gin = [sem(f"gathered_{i}") for i in range(SLOTS)]
        hist_oh = sem("hist_oh")
        hist_sq = sem("hist_sq")
        hist_act = sem("hist_act")
        hist_mm = sem("hist_mm")
        deg_mm = sem("deg_mm")
        xs_done = sem("xs_done")
        xt_mm = sem("xt_mm")
        agg_init = sem("agg_init")
        th_done = sem("th_done")
        tl_done = sem("tl_done")
        tab_out = [sem("tab_out0"), sem("tab_out1")]
        d_edge = sem("d_edge")
        neg_done = sem("neg_done")
        par_done = sem("par_done")
        base_done = sem("base_done")
        miss_idx = sem("miss_idx")
        miss_in = sem("miss_in")
        miss_col = sem("miss_col")
        miss_oh = sem("miss_oh")
        miss_mm = sem("miss_mm")
        miss_added = sem("miss_added")
        idx_copied = sem("idx_copied")
        oh_done = sem("oh_done")
        pair_mm = sem("pair_mm")
        agg_done = sem("agg_done")
        late_in = sem("late_in")
        xr_in = sem("xr_in")
        gn_mm = sem("gn_mm")
        gn_read = sem("gn_read")
        xt_done = sem("xt_done")
        zf_done = sem("zf_done")
        tf_mm = sem("tf_mm")
        tf_done = sem("tf_done")
        lg_mm = sem("lg_mm")
        xr_sum = sem("xr_sum")
        row_hi = sem("row_hi")
        row_done = sem("row_done")
        top_done = sem("top_done")
        es_done = sem("es_done")
        oe_done = sem("oe_done")
        pos_mm = sem("pos_mm")
        route_done = sem("route_done")
        d_fin = sem("d_fin")
        d_route = sem("d_route")
        zero_in = sem("zero_in")
        scattered = sem("scattered")
        slot_in = sem("slot_in")
        et_mm = sem("et_mm")
        bt_hi = sem("bt_hi")
        bt_lo = sem("bt_lo")
        e1_mm = sem("e1_mm")
        er_done = sem("er_done")
        eh_done = sem("eh_done")
        ehl_done = sem("ehl_done")
        ey_mm = sem("ey_mm")
        ey_read = sem("ey_read")
        eb_in = sem("eb_in")
        ebias_done = sem("ebias_done")
        e1_in = sem("e1_in")
        e2_in = sem("e2_in")
        e1_hi = sem("e1_hi")
        e1_lo = sem("e1_lo")
        e2_hi = sem("e2_hi")
        e2_lo = sem("e2_lo")
        pw_done = sem("pw_done")
        er_zero = sem("er_zero")
        e_flags = sem("e_flags")
        e_nan = sem("e_nan")
        e_clean = sem("e_clean")
        d_eb = sem("d_eb")
        ey_out = sem("ey_out")
        d_exp = sem("d_exp")
        back_in = [sem(f"back_in{i}") for i in range(G)]
        fin_done = sem("fin_done")
        ctx_end = sem("ctx_end")
        cn_done = sem("cn_done")
        ct_mm = sem("ct_mm")
        ct_hi = sem("ct_hi")
        ct_lo = sem("ct_lo")
        cw_mm = sem("cw_mm")
        cw_hi = sem("cw_hi")
        cw_lo = sem("cw_lo")
        q_mm = sem("q_mm")
        q_read = sem("q_read")
        qe_done = sem("qe_done")
        qn_done = sem("qn_done")
        tq_mm = sem("tq_mm")
        tq_hi = sem("tq_hi")
        tq_lo = sem("tq_lo")
        at_mm = sem("at_mm")
        x1_done = sem("x1_done")
        z2_done = sem("z2_done")
        t2_mm = sem("t2_mm")
        t2_hi = sem("t2_hi")
        t2_lo = sem("t2_lo")
        f1_mm = sem("f1_mm")
        gelu_done = sem("gelu_done")
        hh_done = sem("hh_done")
        hl_done = sem("hl_done")
        y_mm = sem("y_mm")
        x2_done = sem("x2_done")
        d_head = sem("d_head")
        d_prep = sem("d_prep")
        d_ln1 = sem("d_ln1")
        d_sm = sem("d_sm")
        d_ln2 = sem("d_ln2")
        d_kv = sem("d_kv")
        d_mid = sem("d_mid")
        d_q = sem("d_q")
        out_done = sem("out_done")

        block = ctx.enter_context(nc.Block())

        class Chain:

            def __init__(self, eng, s, r, n):
                self.eng, self.s, self.base, self.n, self.k = eng, s, r * n, n, 0

            def __call__(self, ins):
                self.k += 1
                ins.then_inc(self.s, 1)
                self.eng.wait_ge(self.s, self.base + self.k)

            def end(self):
                assert self.k == self.n, self.k

        def halves(b):
            return b.rearrange("p (k c) -> p k c", k=KD)

        x_t = A["x"].rearrange("(t p) d -> p t d", p=P)
        o_t = out.rearrange("(t p) d -> p t d", p=P)

        @block.sync
        def _(sp):
            sp.dma_start(EDI, A["edge_dst"]).then_inc(edges_in, 16)
            for n in range(G):
                sp.dma_start(X[:, n * TG:(n + 1) * TG, :], x_t[:, n * TG:(n + 1) * TG, :]).then_inc(x_in, 16)
            sp.dma_start(EIX[:, :], A["edge_src"]).then_inc(edges_in, 16)

            def w(name, l):
                return A["L0_mix_" + name][ds(l, 1), :, :].rearrange("a (k p) n -> p (a k) n", p=128)

            def early(l):
                sp.dma_start(VEC[:, :], A["mix_vec"][ds(l, 1), :, :].rearrange("a p n -> (a p) n")).then_inc(ln_in, 16)
                sp.dma_start(BR[:, :, :], A["mix_rows"][ds(l, 1), :, :, :].rearrange("a r n d -> (a r) n d")).then_inc(ln_in, 16)
                sp.dma_start(SKV[:, :, 0, :], w("Wk", l)).then_inc(kv_in, 16)
                sp.dma_start(SKV[:, :, 1, :], w("Wv", l)).then_inc(kv_in, 16)

            early(0)
            with sp.Fori(0, L) as l:
                sp.wait_ge(stage_free, l + 1)
                sp.dma_start(SQO[:, 0, :, :], w("Wq", l)).then_inc(qo_in, 16)
                sp.dma_start(SQO[:, 1, :, :], w("Wo", l)).then_inc(qo_in, 16)
                sp.dma_start(SW[:, :].rearrange("p (k n) -> p k n", k=KD), w("W1", l)).then_inc(w1_in, 16)
                for b in range(2):
                    sp.wait_ge(tab_out[b], 16 * (3 - b))
                sp.wait_ge(y_mm, l * T + 1)
                sp.dma_start(SW2.rearrange("p (k n) -> p k n", k=NF), w("W2", l)).then_inc(w2_in, 16)
                sp.wait_ge(early_free, l + 1)
                early((l + 1) % L)
            sp.wait_ge(y_mm, L * T + 1)
            for n, (dst, src) in enumerate(((GNW, A["L0_gnn_W"].rearrange("(k p) n -> p k n", p=128)),
                                            (GW, A["L0_ffn_gate_w"].rearrange("(k p) n -> p k n", p=128)),
                                            (GBR[:, :], A["L0_ffn_gate_b"].rearrange("(a n) -> a n", a=1)),
                                            (GNB, A["gnn_bias"]))):
                sp.dma_start(dst, src).then_inc(late_in, 16)
            for g in range(G):
                if g >= 3:
                    sp.wait_ge(xt_done, (G - 3) * TG)
                sp.dma_start(XR[g % 3], x_t[:, g * TG:(g + 1) * TG, :]).then_inc(xr_in, 16)

            rows = lambda ap, e: ap[ds(e * CP, CP), :].rearrange("(j p) n -> p j n", p=CT_)

            def load1(e):
                sp.dma_start(SE1, A["L0_ffn_w1"][ds(e, 1), :, :].rearrange("a (k p) n -> p (a k) n", p=128)).then_inc(e1_in, 16)

            def load2(e):
                sp.dma_start(SE2, A["L0_ffn_w2"][ds(e, 1), :, :].rearrange("a (k p) n -> p (a k) n", p=128)).then_inc(e2_in, 16)

            def store(e):
                sp.wait_ge(e_clean, e + 2)
                sp.dma_start(rows(YD, e), YR).then_inc(ey_out, 16)

            def expert(e, first=False, last=False):
                if not last:
                    sp.wait_ge(e1_lo, (e + 1) * 2)
                    load1(e + 1)
                    sp.wait_ge(et_mm, (e + 1) * 2)
                    sp.wait_ge(pw_done, e + 1)
                    sp.dma_start(BSI, rows(BUF, e + 1)).then_inc(slot_in, 16)
                if not first:
                    store(e - 1)
                if not last:
                    sp.wait_ge(e2_lo, (e + 1) * 4)
                    load2(e + 1)

            sp.wait_ge(gn_mm, T)
            load1(0)
            load2(0)
            sp.dma_start(EB1.rearrange("p (e f) -> p e f", e=EX), A["ffn_vec"].rearrange("e p f -> p e f")).then_inc(eb_in, 16)
            sp.dma_start(ERF.rearrange("p (e d) -> p e d", e=EX), A["ffn_rows"].rearrange("e r d -> r e d")).then_inc(eb_in, 16)
            sp.wait_ge(scattered, 16 * T)
            sp.dma_start(BSI, rows(BUF, 0)).then_inc(slot_in, 16)
            expert(0, first=True)
            with sp.Fori(1, EX - 1) as e:
                expert(e)
            expert(EX - 1, last=True)
            store(EX - 1)
            for g in range(G):
                sp.wait_ge(fin_done, (g + 1) * TG)
                sp.dma_start(o_t[:, g * TG:(g + 1) * TG, :], X[:, g * TG:(g + 1) * TG, :]).then_inc(out_done, 16)
            sp.wait_ge(out_done, 16 * G)

        @block.gpsimd
        def _(pool):
            n = [0]

            def step(ins):
                n[0] += 1
                ins.then_inc(pool_chain, 1)
                pool.wait_ge(pool_chain, n[0])

            step(pool.memset(ID[:, :], 0.0))
            step(pool.memset(IDH[:, :], 0.0))
            step(pool.affine_select(out=IDH[:, :], in_=IDH[:, :], compare_op=ALU.not_equal, fill=1.0, base=0,
                                    pattern=[[-1, 128]], channel_multiplier=1))
            step(pool.affine_select(out=ID[:, :], in_=ID[:, :], compare_op=ALU.not_equal, fill=1.0, base=0,
                                    pattern=[[-1, 128]], channel_multiplier=1))
            step(pool.memset(BM[:, :], 1.0))
            bm = BM[:, :].rearrange("p (h c) -> p h c", h=128 // DH)
            step(pool.affine_select(out=bm, in_=bm, compare_op=ALU.is_ge, fill=0.0, base=0,
                                    pattern=[[-DH, 128 // DH], [0, DH]], channel_multiplier=1))
            step(pool.affine_select(out=bm, in_=bm, compare_op=ALU.is_ge, fill=0.0, base=DH - 1,
                                    pattern=[[DH, 128 // DH], [0, DH]], channel_multiplier=-1))
            step(pool.memset(LOW[:, :], 0.0))
            step(pool.affine_select(out=LOW[:, :], in_=LOW[:, :], compare_op=ALU.not_equal, fill=1.0, base=-1,
                                    pattern=[[0, 1]], channel_multiplier=1))
            step(pool.memset(ONE[:, 0, :], 1.0))
            step(pool.memset(ONE[:, 1, :], QS_))
            step(pool.memset(ZR[:, :], 0.0))
            step(pool.memset(PPAD[:, :], 0.0))
            step(pool.memset(VH[:, :, :, 128:130], 1.0))
            step(pool.memset(VL[:, :, :, 128:130], 0.0))
            step(pool.iota(IOTA[:, :], [[1, 128]], base=0, channel_multiplier=0, allow_small_or_imprecise_dtypes=True))
            step(pool.iota(IOC[:, :], [[-1, EX]], base=EX, channel_multiplier=0, allow_small_or_imprecise_dtypes=True))
            step(pool.iota(IOE[:, :], [[CP, EX]], base=0, channel_multiplier=0, allow_small_or_imprecise_dtypes=True))
            step(pool.memset(ON1[:, :], 1.0))
            step(pool.memset(ONF[:, :], 1.0))
            step(pool.memset(AGG[:, :, N:NW], 0.0))
            step(pool.memset(TRI[:, :], 1.0))
            step(pool.affine_select(out=TRI[:, :], in_=TRI[:, :], compare_op=ALU.is_ge, fill=0.0, base=0,
                                    pattern=[[1, P]], channel_multiplier=-1))
            pool.memset(OH[:, :, :], 0.0).then_inc(const_done, 1)
            pool.wait_ge(const_done, 1)
            zero = OH[0:CT_, :, :].rearrange("p i n -> p (i n)").bitcast(i32)[:, 0:RW]
            for n in range(ZD):
                pool.dma_start(BUF[n * 2 * CT_:(n + 1) * 2 * CT_, :].rearrange("(p j) n -> p (j n)", j=2), zero).then_inc(zero_in, 16)

            pool.wait_ge(neg_done, 1)
            pool.partition_all_reduce(EDF, MIS[:, :], 128, RMAX).then_inc(par_done, 1)
            pool.wait_ge(neg_done, 2)
            pool.partition_all_reduce(FLG[:, :], FL1[:, :], 128, RMAX).then_inc(par_done, 1)

            for g in range(G):
                pool.wait_ge(tl_done, g + 1)
                pool.dma_start(TAB.rearrange("(t p) n -> p t n", p=P)[:, g * TG:(g + 1) * TG, :], TH[g % 2]).then_inc(tab_out[g % 2], 16)

            pool.wait_ge(edges_in, 32)
            for b in range(2):
                pool.wait_ge(tab_out[b], 16 * (3 - b))
            with pool.Fori(0, L * G) as it:
                for b in range(NP_ // SLOTS):
                    pool.wait_ge(pair_mm, it * NP_ + b * SLOTS + 1)
                    cols = 2 * SLOTS
                    pool.tensor_copy(IB[:, b * cols:(b + 1) * cols], EIX[:, ds(it * EI + b * cols, cols)]).then_inc(idx_copied, 1)
                    pool.wait_ge(idx_copied, it * (NP_ // SLOTS) + b + 1)
                    for s in range(SLOTS):
                        q = b * SLOTS + s
                        pool.wait_ge(pair_mm, it * NP_ + q + 2)
                        pool.tensor_tensor(PPAD[:, 2 + q:3 + q], PPAD[:, 0:1], PPAD[:, 1:2], ALU.add)
                        for i in range(2):
                            pool.indirect_dma_start(
                                out=GB[:, s, i, :], out_offset=None, in_=TAB,
                                in_offset=bass.IndirectOffsetOnAxis(ap=IB[:, 2 * q + i:2 * q + i + 1], axis=0),
                            ).then_inc(gin[s], 16)

            with some_missed(pool, FLI[0:1, 0:1], base_done):
                pool.wait_ge(pair_mm, L * G * NP_ + SLOTS + 1)
                pool.sem_inc(miss_mm, 1)
                with pool.Fori(0, EW) as t:
                    pool.wait_ge(miss_mm, t * NWIN + 1)
                    pool.tensor_copy(IB[:, 0:1], EIX[:, ds(t, 1)]).then_inc(miss_idx, 1)
                    pool.wait_ge(miss_idx, t + 1)
                    pool.tensor_tensor(PPAD[:, 2:3], PPAD[:, 0:1], PPAD[:, 1:2], ALU.add)
                    pool.indirect_dma_start(out=GB[:, 0, 0, :], out_offset=None, in_=TAB,
                                            in_offset=bass.IndirectOffsetOnAxis(ap=IB[:, 0:1], axis=0)).then_inc(miss_in, 16)

            pool.sem_inc(ey_out, 16)
            pool.wait_ge(x2_done, L * T + 1)
            for g in range(G):
                pool.wait_ge(xr_in, 48 if g < 3 else 16 * G)
                pool.tensor_tensor(XR[g % 3], XR[g % 3], X[:, g * TG:(g + 1) * TG, :], ALU.add).then_inc(xr_sum, 1)
            pool.wait_ge(route_done, 1)
            pool.wait_ge(row_done, T)
            pool.wait_ge(zero_in, 16 * ZD)
            for t in range(T):
                pool.indirect_dma_start(out=BUF, out_offset=bass.IndirectOffsetOnAxis(ap=SIX[:, t:t + 1], axis=0),
                                        in_=ROWI[:, t, :], in_offset=None, bounds_check=EX * CP - 1,
                                        oob_is_err=False).then_inc(scattered, 16)
            def zero(e):
                pool.wait_ge(ey_out, e * 16 + 16)
                pool.tensor_tensor(PPAD[:, 2:3], PPAD[:, 0:1], PPAD[:, 1:2], ALU.add)
                pool.memset(YR, 0.0).then_inc(er_zero, 1)

            with pool.Fori(0, EX - 1) as e:
                zero(e)
                pool.wait_ge(ey_read, (e + 1) * NCT + 2)
                pool.tensor_tensor(PPAD[:, 3:4], PPAD[:, 0:1], PPAD[:, 1:2], ALU.add)
                pool.tensor_scalar(YF, YV, 0.0, 0.0, ALU.mult, ALU.is_equal).then_inc(e_flags, 1)
                pool.tensor_scalar(YC[:, :, :], YV, -1.0e4, 1.0e4, ALU.max, ALU.min).then_inc(e_flags, 1)
            zero(EX - 1)
            pool.wait_ge(ey_out, 16 * EX + 16)
            pool.wait_ge(route_done, 2)
            for t in range(T):
                pool.indirect_dma_start(out=YG[:, t, :], out_offset=None, in_=YD,
                                        in_offset=bass.IndirectOffsetOnAxis(ap=GIX[:, t:t + 1], axis=0)).then_inc(back_in[t // TG], 16)

        @block.scalar
        def _(act):
            def kv_split(n):
                act.wait_ge(lnp_done, n * 3 + 1)
                act.wait_ge(kv_in, (n + 1) * 32)
                for k in range(KD):
                    act.activation(KVH[:, k, :, :], SKV[:, k, :, :], ACT.Copy, scale=G64[:, 0, k:k + 1]).then_inc(whk_done, 1)

            def split(l, i):
                if i < KD:
                    act.wait_ge(qo_in, (l + 1) * 32)
                    act.activation(QOH[:, 0, i, :], SQO[:, 0, i, :], ACT.Copy, scale=G64[:, 0, i:i + 1]).then_inc(whi_done, 1)
                elif i == 2:
                    act.activation(QOH[:, 1, :, :], SQO[:, 1, :, :], ACT.Copy, scale=WS).then_inc(whi_done, 1)
                elif i in (3, 5):
                    k = (i - 3) // 2
                    act.wait_ge(w1_in, (l + 1) * 16)
                    act.activation(W1H[:, k, :], SW[:, k * FF:(k + 1) * FF], ACT.Copy, scale=G64[:, 1, k:k + 1]).then_inc(whi_done, 1)
                elif i in (7, 9):
                    f = slice((i - 7) // 2 * NF // 2, (i - 5) // 2 * NF // 2)
                    act.wait_ge(w2_in, (l + 1) * 16)
                    act.activation(W2H[:, f, :], SW2.rearrange("p (k n) -> p k n", k=NF)[:, f, :], ACT.Copy,
                                   scale=WS).then_inc(whi_done, 1)

            def z1_hi(g, n0, j):
                act.wait_ge(t1_mm, n0 + j + 1)
                act.activation(Z1H[:, :, ds((g * TG + j) * P, P)], halves(PT[j % 2][:, 0:2 * P]),
                               ACT.Copy).then_inc(t1_hi, 1)

            def head(l):
                act.wait_ge(kr_mm, l + 1)
                act.activation(KR[:, :], PT[0][0:1, 0:D], ACT.Copy, scale=-1.0).then_inc(kr_done, 1)

            def kv(l, t, b):
                n = l * T + t
                act.wait_ge(kv_mm, n + 1)
                act.wait_ge(el_done, n + 1)
                act.activation(EF[:, b, :], PA[b][0:P, 0:D], ACT.Exp, scale=SCALE / WS).then_inc(exp_done, 1)
                act.wait_ge(ctx_mm, n + 1)
                act.activation(VH[:, b, :, 0:128], halves(PA[b][0:P, D:2 * D]), ACT.Copy, scale=1.0 / WS).then_inc(vh_done, 1)

            def mid(l):
                act.wait_ge(ct_mm, l + 1)
                act.activation(CTH[:, :, :], halves(PT[0][:, 0:D]), ACT.Copy).then_inc(ct_hi, 1)
                for h in range(KD):
                    act.wait_ge(cw_mm, l * KD + h + 1)
                    act.activation(CWH[:, h, :], PA[h][:, 0:D], ACT.Copy).then_inc(cw_hi, 1)

            def q_exp(it):
                act.wait_ge(q_read, (it + 1) * TG)
                act.activation(QS[:, :, :], QS[:, :, :], ACT.Exp, scale=SCALE / WS).then_inc(qe_done, 1)

            def q_hi(it, j):
                act.wait_ge(tq_mm, it * TG + j + 1)
                act.activation(QTH[:, :, j * P:(j + 1) * P], halves(PT[j % 2][:, 0:2 * P]), ACT.Copy,
                               scale=QS_).then_inc(tq_hi, 1)

            def z2_hi(it, j):
                act.wait_ge(t2_mm, it * TG + j + 1)
                act.activation(Z2H[:, :, j * P:(j + 1) * P], halves(PT[j % 2][:, 0:2 * P]),
                               ACT.Copy).then_inc(t2_hi, 1)

            def unit(it, u):
                n = it * 2 * NF + u
                if u < 2 * NF:
                    t0, tn = CH[u // NF]
                    f = u % NF
                    act.wait_ge(f1_mm, n + 1)
                    act.wait_ge(hl_done, n + 3 - RING if u >= RING else it * 2 * NF + 2)
                    act.activation(HF[:, u % RING, 0:tn * P], PH[u % 2][:, 0:tn * P], ACT.Gelu, scale=1.0 / WS,
                                   bias=B1C[:, f:f + 1]).then_inc(gelu_done, 1)
                if u >= 1:
                    t0, tn = CH[(u - 1) // NF]
                    act.wait_ge(gelu_done, n)
                    act.activation(HH[:, (u - 1) % NF, t0 * P:(t0 + tn) * P], HF[:, (u - 1) % RING, 0:tn * P], ACT.Copy).then_inc(hh_done, 1)

            def body(l, g, it, first=False, last=False, ahead=True):
                for u in range(2 * NF):
                    if first and u == 4:
                        kv_split(l + 1)
                    if not first and u in T1_AT:
                        z1_hi(g - 1, T + (it - 1) * TG, u - T1_AT[0])
                    if not last and u in TQ_AT:
                        q_hi(it + 1, u - TQ_AT[0])
                    unit(it, u)
                unit(it, 2 * NF)
                for j in range(TG * (not last)):
                    z2_hi(it + 1, j)
                    if ahead and j == T2_AT[Q_END][-1]:
                        q_exp(it + 2)

            def block(n, b):
                act.wait_ge(hist_mm, n + 1)
                for i in range(HB - HA, HB):
                    ins = act.activation(OHL[:, b, i, :], IOTA[:, 0:P], ACT.Square, bias=EDN[:, ds(n * HB + i, 1)])
                ins.then_inc(hist_sq, 1)
                act.wait_ge(hist_sq, n + 1)
                act.activation(OHL[:, b, HB - HA:HB, :], OHL[:, b, HB - HA:HB, :], ACT.Relu, scale=-1.0, bias=1.0).then_inc(hist_act, 1)

            kv_split(0)
            act.wait_ge(const_done, 1)
            act.wait_ge(neg_done, 2)
            with act.Fori(0, G) as g:
                for c in range(HQ):
                    block(g * HQ + c, c % 2)
                    for j in Z1_AT[c]:
                        z1_hi(g, g * TG, j)

            act.wait_ge(deg_mm, 1)
            for g in range(G):
                if g >= 2:
                    act.wait_ge(tab_out[g % 2], 16 * (g // 2))
                act.wait_ge(xs_done, (g + 1) * TG)
                act.activation(TH[g % 2][:, :, 0:D], (ZN, ZN2)[g % 2][:, :, :], ACT.Copy).then_inc(th_done, 1)
                for j in range(TG):
                    t = g * TG + j
                    act.wait_ge(xt_mm, t + 1)
                    act.activation(AGG[:, :, t * P:(t + 1) * P], halves(PT[j % 2][:, 0:2 * P]), ACT.Copy).then_inc(agg_init, 1)
            act.wait_ge(tab_out[0], 48)
            act.wait_ge(tab_out[1], 32)
            with act.Fori(0, L) as l:
                head(l)
                for t in range(PEEL):
                    kv(l, t, t % 2)
                    split(l, t)
                with act.Fori(0, (T - PEEL) // PER) as r:
                    for i in range(PER):
                        kv(l, r * PER + PEEL + i, (PEEL + i) % 2)
                mid(l)
                q_exp(l * G)
                for j in range(TG):
                    q_hi(l * G, j)
                for j in range(TG):
                    z2_hi(l * G, j)
                q_exp(l * G + 1)
                body(l, 0, l * G, first=True)
                with act.Fori(1, G - 2) as g:
                    body(l, g, l * G + g)
                body(l, G - 2, l * G + G - 2, ahead=False)
                body(l, G - 1, l * G + G - 1, last=True, ahead=False)
                for j in range(TG):
                    z1_hi(G - 1, T + (l * G + G - 1) * TG, j)

            for g in range(G):
                for j in range(TG):
                    t = g * TG + j
                    act.wait_ge(tf_mm, t + 1)
                    if t >= 2:
                        act.wait_ge(lg_mm, t - 1)
                    act.activation(EFT[:, t % 2, :], PT[t % 2][:, 0:2 * P], ACT.Copy).then_inc(tf_done, 1)
                act.activation(ROW[:, g * TG:(g + 1) * TG, 0:D], (ZN, ZN2)[g % 2][:, :, :], ACT.Copy).then_inc(row_hi, 1)
            act.sem_inc(er_done, 2)
            act.wait_ge(top_done, 1)
            act.activation(L2, L2, ACT.Exp).then_inc(es_done, 1)

            def high1(e):
                act.wait_ge(e1_in, (e + 1) * 16)
                for k in range(KD):
                    act.activation(W1H[:, k, :], SE1[:, k, :], ACT.Copy, scale=WS).then_inc(e1_hi, 1)

            def high2(e, c):
                if c == 0:
                    act.wait_ge(e2_in, (e + 1) * 16)
                    act.wait_ge(ey_mm, e * NCT + 1)
                f = slice(c * NF // 4, (c + 1) * NF // 4)
                act.activation(W2H[:, f, :], SE2[:, f, :], ACT.Copy, scale=WS).then_inc(e2_hi, 1)

            def rows_high(e):
                act.wait_ge(et_mm, e * 2 + 1)
                act.activation(BTH, PT[0][:, :].bitcast(f16)[:, 0:KD * CP].rearrange("p (k n) -> p k n", k=KD), ACT.Copy).then_inc(bt_hi, 1)

            def hidden_high(e, f):
                act.wait_ge(er_done, e * NF + f + 3)
                act.activation(HH[:, f, 0:CP], HE[:, f % 3, :], ACT.Copy).then_inc(eh_done, 1)

            def expert(e, last=False):
                for f in range(NF):
                    n = e * NF + f
                    act.wait_ge(e1_mm, n + 1)
                    act.wait_ge(ehl_done, n if f >= 3 else e * NF + 2)
                    act.activation(HE[:, f % 3, :], PH[f % 2][:, 0:CP], ACT.Relu, scale=1.0 / WS,
                                   bias=EB1[:, ds(e * NF + f, 1)]).then_inc(er_done, 1)
                    if f >= 1:
                        hidden_high(e, f - 1)
                    if f in W2_AT:
                        high2(e, W2_AT.index(f))
                hidden_high(e, NF - 1)
                if not last:
                    high1(e + 1)
                act.wait_ge(pw_done, e + 1)
                act.wait_ge(e_clean, e + 1)
                for j in range(NCT):
                    act.wait_ge(ey_mm, e * NCT + j + 2)
                    act.activation(YV[:, j, :], PA[j % 2][0:CT_, 0:D], ACT.Copy, scale=PW[:, ds(e * NCT + j, 1)]).then_inc(ey_read, 1)
                    if j == 0 and not last:
                        rows_high(e + 1)

            act.wait_ge(eb_in, 32)
            high1(0)
            rows_high(0)
            with act.Fori(0, EX - 1) as e:
                expert(e)
            expert(EX - 1, last=True)

        @block.vector
        def _(dve):
            dve.sem_inc(hist_mm, 2)
            dve.sem_inc(stage_free, 1)
            dve.sem_inc(el_done, 2)
            dve.sem_inc(hl_done, 2)

            def newton(ch, var, add, nt, ni):
                s = lambda n: nt[:, n, :]
                ch(dve.tensor_scalar(s(1), var, add, None, ALU.add))
                ch(dve.tensor_scalar(ni[:, :], s(1).bitcast(i32), 1, None, ALU.logical_shift_right))
                ch(dve.tensor_scalar(s(0).bitcast(i32), ni[:, :], -1.0, float(0x5f3759df), ALU.mult, ALU.add))
                for _ in range(3):
                    ch(dve.tensor_tensor(s(2), s(0), s(0), ALU.mult))
                    ch(dve.scalar_tensor_tensor(s(2), s(2), -0.5, s(1), ALU.mult, ALU.mult))
                    ch(dve.scalar_tensor_tensor(s(0), s(2), 1.5, s(0), ALU.add, ALU.mult))

            NEWTON = 12
            LN = NEWTON + 2

            def fill(column):
                dve.memset(PAD[:, column:column + 1], 0.0)

            def stats(st, j, t):
                return dve.bn_stats(st[:, j, :], t)

            def scale(ch, st, tiles, dst, done):
                fill(2 * TG + (st is ST2))
                for j in range(TG):
                    ins = dve.bn_aggr(MV[:, j, :], st[:, j, :])
                ch(ins)
                newton(ch, MV[:, :, 1], EPS, NT, NI)
                for j, t in enumerate(tiles):
                    dve.tensor_scalar(dst(j), t, MV[:, j, 0:1], NT[:, 0, j:j + 1], ALU.subtract, ALU.mult).then_inc(done, 1)

            def tile(g, j):
                return X[:, ds(g * TG + j, 1), :].rearrange("p a d -> p (a d)")

            def tiles(g):
                return [tile(g, j) for j in range(TG)]

            def kv_split(n):
                dve.wait_ge(ln_in, (n + 1) * 32)
                dve.tensor_scalar(G64[:, 0, :], LNP[:, 0, :], WS, None, ALU.mult)
                dve.tensor_scalar(G64[:, 1, :], LNP[:, 2, :], WS, None, ALU.mult).then_inc(lnp_done, 1)
                for r in range(2):
                    dve.tensor_copy(B2[:, :, r], LNP[:, 1, :]).then_inc(lnp_done, 1)
                dve.wait_ge(lnp_done, n * 3 + 3)
                for k in range(KD):
                    dve.wait_ge(whk_done, n * KD + k + 1)
                    dve.scalar_tensor_tensor(KVL[:, k, :, :], SKV[:, k, :, :], G64[:, 0, k:k + 1], KVH[:, k, :, :],
                                             ALU.mult, ALU.subtract).then_inc(wlk_done, 1)

            def biases(l):
                dve.wait_ge(b1_mm, l + 1)
                dve.tensor_tensor(B1C[:, :], PH[1][:, KD:KD + NF], B1F, ALU.add).then_inc(rt_done, 1)
                for r in range(2):
                    ins = dve.tensor_copy(BV[:, :, r], PH[1][:, 0:KD])
                ins.then_inc(bv_done, 1)
                dve.wait_ge(bq_mm, l + 1)
                dve.tensor_scalar(RF[:, 0, :], PH[0][0:2, 0:D], WS, None, ALU.mult).then_inc(rt_done, 1)

            def split(l, i):
                n = l * 7

                def low(hi, out, in0, by, high):
                    dve.wait_ge(whi_done, n + hi)
                    dve.scalar_tensor_tensor(out, in0, by, high, ALU.mult, ALU.subtract).then_inc(wlo_done, 1)

                if i < KD:
                    low(i + 1, QOL[:, 0, i, :], SQO[:, 0, i, :], G64[:, 0, i:i + 1], QOH[:, 0, i, :])
                elif i == 2:
                    low(3, QOL[:, 1, :, :], SQO[:, 1, :, :], WS, QOH[:, 1, :, :])
                elif i == 3:
                    ch = Chain(dve, d_prep, l * 2, 3)
                    dve.wait_ge(bo_mm, l + 1)
                    ch(dve.tensor_tensor(RF[:, 1, :], PH[1][0:2, 0:D], BR[:, 0, :], ALU.add))
                    ch(dve.tensor_scalar(RF[:, 1, :], RF[:, 1, :], WS, None, ALU.mult))
                    ch(dve.tensor_scalar(RF[:, 2, :], BR[:, 1, :], WS, None, ALU.mult))
                    ch.end()
                elif i == 4:
                    ch = Chain(dve, d_prep, l * 2 + 1, 3)
                    dve.wait_ge(rt_done, (l + 1) * 2)
                    ch(dve.tensor_copy(RT[:, :, :], RF[:, :, :]))
                    ch(dve.tensor_scalar(RM[:, :, :], RT[:, :, :], LOW[:, 0:1], None, ALU.mult))
                    ch(dve.tensor_tensor(RB[:, :, :], RF[:, :, :], RM[:, :, :], ALU.subtract))
                    ch.end()
                    dve.sem_inc(rows_done, 1)
                elif i < 9:
                    k, h = divmod(i - 5, 2)
                    c = slice(h * FF // 2, (h + 1) * FF // 2)
                    low(4 + k, W1L[:, k, c], SW[:, k * FF + h * FF // 2:k * FF + (h + 1) * FF // 2], G64[:, 1, k:k + 1], W1H[:, k, c])
                else:
                    h = i - 9
                    f = slice(h * NF // 4, (h + 1) * NF // 4)
                    low(6 + h // 2, W2L[:, f, :], SW2.rearrange("p (k n) -> p k n", k=NF)[:, f, :], WS, W2H[:, f, :])
                if i == PEEL - 1:
                    dve.wait_ge(wlo_done, (l + 1) * WLO)
                    dve.sem_inc(stage_free, 1)
                    dve.sem_inc(early_free, 1)

            def km(g, kg, u):
                m, c = divmod(u, 2)
                dve.wait_ge(km_mm, kg * 2 * KD + u + 1)
                dve.tensor_reduce(KM[:, m, ds(g * 2 + c, 1)], PA[u % 2][:, 0:CH[c][1] * P], AX.X, ALU.max).then_inc(km_read, 1)

            def z1_low(g, n0, j):
                dve.wait_ge(t1_hi, n0 + j + 1)
                cols = ds((g * TG + j) * P, P)
                dve.tensor_tensor(Z1L[:, :, cols], halves(PT[j % 2][:, 0:2 * P]), Z1H[:, :, cols],
                                  ALU.subtract).then_inc(t1_lo, 1)

            def head(l):
                dve.wait_ge(km_read, (l + 1) * G * 2 * KD)
                dve.tensor_reduce(KX[:, :], KM[:, :, :], AX.X, ALU.max).then_inc(kx_done, 1)

            def kv(l, t, b):
                n = l * T + t
                dve.wait_ge(exp_done, n + 1)
                dve.wait_ge(ctx_mm, n + 1)
                dve.tensor_scalar(EH[:, b, :], EF[:, b, :], ES, None, ALU.mult).then_inc(d_kv, 1)
                dve.wait_ge(d_kv, n + 1)
                dve.scalar_tensor_tensor(EL[:, b, :], EF[:, b, :], ES, EH[:, b, :], ALU.mult, ALU.subtract).then_inc(el_done, 1)
                dve.wait_ge(vh_done, n + 1)
                dve.scalar_tensor_tensor(VL[:, b, :, 0:128], halves(PA[b][0:P, D:2 * D]), 1.0 / WS, VH[:, b, :, 0:128],
                                         ALU.mult, ALU.subtract).then_inc(vl_done, 1)

            def mid(l):
                ch = Chain(dve, d_mid, l, 1)
                dve.wait_ge(ctx_end, l + 1)
                for h in range(KD):
                    ins = dve.reciprocal(RS[:, h:h + 1], PC[h][:, 128:129])
                ch(ins)
                for h in range(KD):
                    dve.scalar_tensor_tensor(CN[:, h, :], PC[h][:, 0:128], RS[:, h:h + 1], BM[:, :],
                                             ALU.mult, ALU.mult).then_inc(cn_done, 1)
                ch.end()
                q_max(l * G, 0)
                q_max(l * G, 1)
                dve.wait_ge(ct_hi, l + 1)
                dve.tensor_tensor(CTL[:, :, :], halves(PT[0][:, 0:D]), CTH[:, :, :], ALU.subtract).then_inc(ct_lo, 1)
                q_max(l * G, 2)
                q_max(l * G, 3)
                for h in range(KD):
                    dve.wait_ge(cw_hi, l * KD + h + 1)
                    dve.tensor_tensor(CWL[:, h, :], PA[h][:, 0:D], CWH[:, h, :], ALU.subtract).then_inc(cw_lo, 1)
                q_max(l * G, TG - 1)

            def q_max(it, j):
                n = it * TG + j
                dve.wait_ge(q_mm, n + 1)
                pq = PH[j % 2][0:P, 0:D].rearrange("p (h c) -> p h c", h=HEADS)
                dve.tensor_reduce(QM[:, j, :], pq, AX.X, ALU.max).then_inc(d_q, 1)
                dve.wait_ge(d_q, n + 1)
                dve.tensor_tensor(QS[:, j, :].rearrange("p (h c) -> p h c", h=HEADS), pq,
                                  QM[:, j, :].unsqueeze(2).to_broadcast([P, HEADS, DH]), ALU.subtract).then_inc(q_read, 1)

            def q_norm(it, j):
                ch = Chain(dve, d_sm, it * TG + j, 2)
                dve.wait_ge(qe_done, it + 1)
                qv = QS[:, j, :].rearrange("p (h c) -> p h c", h=HEADS)
                qr = QR[:, j * HEADS:(j + 1) * HEADS]
                ch(dve.tensor_reduce(qr, qv, AX.X, ALU.add))
                ch(dve.reciprocal(qr, qr))
                dve.tensor_tensor(qv, qv, qr.unsqueeze(2).to_broadcast([P, HEADS, DH]), ALU.mult).then_inc(qn_done, 1)
                ch.end()

            def q_low(it, j):
                dve.wait_ge(tq_hi, it * TG + j + 1)
                dve.scalar_tensor_tensor(QTL[:, :, j * P:(j + 1) * P], halves(PT[j % 2][:, 0:2 * P]), QS_,
                                         QTH[:, :, j * P:(j + 1) * P], ALU.mult, ALU.subtract).then_inc(tq_lo, 1)

            def x1(g, it):
                for j in range(TG):
                    dve.wait_ge(at_mm, it * TG + j + 1)
                    dve.scalar_tensor_tensor(tile(g, j), PA[j % 2][0:P, 0:D], 1.0 / (WS * QS_), tile(g, j),
                                             ALU.mult, ALU.add).then_inc(x1_done, 1)
                    if j >= 1:
                        dve.wait_ge(x1_done, it * TG + j)
                        fill(j - 1)
                        stats(ST, j - 1, tile(g, j - 1))
                ch = Chain(dve, d_ln2, it, LN)
                dve.wait_ge(x1_done, (it + 1) * TG)
                fill(TG - 1)
                ch(stats(ST, TG - 1, tile(g, TG - 1)))
                scale(ch, ST, tiles(g), lambda j: ZN2[:, j, :], z2_done)
                ch.end()

            def z2_low(it, j):
                dve.wait_ge(t2_hi, it * TG + j + 1)
                dve.tensor_tensor(Z2L[:, :, j * P:(j + 1) * P], halves(PT[j % 2][:, 0:2 * P]),
                                  Z2H[:, :, j * P:(j + 1) * P], ALU.subtract).then_inc(t2_lo, 1)

            def unit(it, u):
                t0, tn = CH[u // NF]
                f = u % NF
                dve.wait_ge(hh_done, it * 2 * NF + u + 1)
                cols = slice(t0 * P, (t0 + tn) * P)
                dve.tensor_tensor(HL[:, f, cols], HF[:, u % RING, 0:tn * P], HH[:, f, cols],
                                  ALU.subtract).then_inc(hl_done, 1)

            def x2(g, it, j):
                dve.wait_ge(y_mm, it * TG + j + 2)
                dve.scalar_tensor_tensor(tile(g, j), PA[(j + 1) % 2][0:P, 0:D], 1.0 / WS, tile(g, j),
                                         ALU.mult, ALU.add).then_inc(x2_done, 1)
                if j >= 1:
                    dve.wait_ge(x2_done, it * TG + j + 1)
                    fill(TG + j - 1)
                    stats(ST2, j - 1, tile(g, j - 1))

            def z1(g, it):
                ch = Chain(dve, d_ln1, it, LN)
                dve.wait_ge(x2_done, (it + 1) * TG + 1)
                fill(2 * TG - 1)
                ch(stats(ST2, TG - 1, tile(g, TG - 1)))
                scale(ch, ST2, tiles(g), lambda j: ZN[:, j, :], z1_done)
                ch.end()

            def body(l, g, it, first=False, last=False, ahead=True):
                if not first:
                    z1(g - 1, it - 1)
                for u in range(2 * NF):
                    if first and u == 2:
                        kv_split(l + 1)
                    if u == 1:
                        onehot(it)
                    if not first and u in T1_AT:
                        z1_low(g - 1, T + (it - 1) * TG, u - T1_AT[0])
                    if not last and u in TQ_AT:
                        q_low(it + 1, u - TQ_AT[0])
                    if not first and u in KM_AT:
                        km(g - 1, it - 1 + G, u - KM_AT[0])
                    if u >= 1:
                        unit(it, u - 1)
                    if not last and u in QN_AT:
                        q_norm(it + 1, len(QN_AHEAD) + u - QN_AT[0])
                unit(it, 2 * NF - 1)
                if not last:
                    x1(g + 1, it + 1)
                for j in range(TG):
                    x2(g, it, j)
                    if j == TG - 1 and not last:
                        z2_low(it + 1, j)
                    collect(it, j)
                    if ahead:
                        for i in Q_AT[j]:
                            q_max(it + 2, i)
                    if j < TG - 1 and not last:
                        for i in T2_AT[j]:
                            z2_low(it + 1, i)
                    if ahead and j == TG - 2:
                        for i in QN_AHEAD:
                            q_norm(it + 2, i)

            def onehot(it):
                dve.wait_ge(zero_in, 16 * ZD)
                dve.wait_ge(pair_mm, it * NP_ + SLOTS + 1)
                dve.tensor_tensor(OH[:, :, :], IOTA[:, 0:W].unsqueeze(1).to_broadcast([128, EI, W]),
                                  REL[:, ds(it * EI, EI)].unsqueeze(2).to_broadcast([128, EI, W]), ALU.is_equal).then_inc(oh_done, 1)

            def collect(it, c):
                n = it * NQ + c
                first = dve.value_load(BASE[0:1, ds(n, 1)], min_val=0, max_val=NW - W)
                dve.wait_ge(pair_mm, it * NP_ + 2 * c + 3 + SLOTS)
                dve.wait_ge(agg_done, n + 1)
                o = AGG[:, :, ds(first, W)]
                dve.tensor_tensor(o, PC[c % 2][:, 0:2 * W].rearrange("p (k n) -> p k n", k=KD), o, ALU.add).then_inc(agg_done, 1)

            def norm_all(ch, dst):
                fill(0)
                for t in range(T):
                    ins = dve.bn_stats(ST0[:, t, :], X[:, t, :])
                ch(ins)
                fill(1)
                for t in range(T):
                    ins = dve.bn_aggr(MV0[:, t, :], ST0[:, t, :])
                ch(ins)
                newton(ch, MV0[:, :, 1], EPS, DNT, DNI)

            ce = Chain(dve, d_edge, 0, 18)
            dve.wait_ge(edges_in, 32)
            ce(dve.tensor_copy(EDF, EDI))
            ce(dve.tensor_scalar(REL[:, :], EDF, 0.0, -BIG, ALU.is_lt, ALU.mult))
            dve.tensor_tensor(MIS[:, :], REL[:, :], EDF, ALU.subtract).then_inc(neg_done, 1)

            dve.wait_ge(x_in, 16 * G)
            ch0 = Chain(dve, d_head, 0, LN * 2)
            norm_all(ch0, X)
            for t in range(T):
                dve.tensor_scalar(X[:, t, :], X[:, t, :], MV0[:, t, 0:1], DNT[:, 0, t:t + 1], ALU.subtract, ALU.mult).then_inc(z1_done, 1)

            dve.wait_ge(par_done, 1)
            ce(dve.tensor_reduce(BSF, EDF.rearrange("p (q i) -> p q i", i=4), AX.X, ALU.max))
            ce(dve.tensor_scalar(BSF, BSF, -1.0, float(NW - W), ALU.mult, ALU.min))
            ce(dve.tensor_copy(BASE[:, :], BSF))
            ce(dve.tensor_copy(EDF, EDI))
            ce(dve.tensor_tensor(REL[:, :].rearrange("p (q i) -> p q i", i=4), EDF.rearrange("p (q i) -> p q i", i=4),
                                 BSF.unsqueeze(2).to_broadcast([128, EW // 4, 4]), ALU.subtract))
            ce(dve.tensor_scalar(EHI, EDF, 1.0 / P, -0.496, ALU.mult, ALU.add))
            ce(dve.tensor_scalar(EHI, EHI, 12582912.0, 12582912.0, ALU.add, ALU.subtract))
            ce(dve.scalar_tensor_tensor(EDN, EHI, float(P), EDF, ALU.mult, ALU.subtract))
            ce(dve.tensor_scalar(MIS[:, :], REL[:, :], 0.0, None, ALU.is_ge))
            ce(dve.scalar_tensor_tensor(MIS[:, :], REL[:, :], float(W), MIS[:, :], ALU.is_lt, ALU.mult))
            ce(dve.tensor_scalar(EDT, MIS[:, :], -1.0, 1.0, ALU.mult, ALU.add))
            ce(dve.tensor_tensor(EDT, EDT, EDF, ALU.mult))
            ce(dve.tensor_tensor(MIS[:, :], EDT, MIS[:, :], ALU.subtract))
            ce(dve.tensor_reduce(FL1[:, :], MIS[:, :], AX.X, ALU.max))
            dve.sem_inc(neg_done, 1)
            ce(dve.tensor_scalar(EDT, EDN, -1.0, None, ALU.mult))

            dve.wait_ge(z1_done, T)
            norm_all(ch0, None)
            ch0.end()
            kv_split(0)
            dve.wait_ge(par_done, 2)
            ce(dve.tensor_scalar(FLI[:, :], FLG[:, :], 0.0, None, ALU.is_ge))
            ce.end()
            dve.sem_inc(base_done, 1)

            def block(n, b):
                dve.wait_ge(hist_mm, n + 1)
                dve.tensor_tensor(OHH[:, b, :, :], IOTA[:, 0:T].unsqueeze(1).to_broadcast([128, HB, T]),
                                  EHI[:, ds(n * HB, HB)].unsqueeze(2).to_broadcast([128, HB, T]), ALU.is_equal)
                for i in range(HB - HA):
                    ins = dve.tensor_scalar(OHL[:, b, i, :], IOTA[:, 0:P], EDT[:, ds(n * HB + i, 1)], None, ALU.is_equal)
                ins.then_inc(hist_oh, 1)

            dve.wait_ge(const_done, 1)
            with dve.Fori(0, G) as g:
                for j in range(TG):
                    t = g * TG + j
                    dve.tensor_scalar(ZN[:, j, :], tile(g, j), MV0[:, ds(t, 1), 0], DNT[:, 0, ds(t, 1)], ALU.subtract,
                                      ALU.mult).then_inc(z1_done, 1)
                for c in range(HQ):
                    block(g * HQ + c, c % 2)
                    for j in Z1_AT[c]:
                        z1_low(g, g * TG, j)
                    if c == 2:
                        for u in range(2 * KD):
                            km(g, g, u)
            dve.wait_ge(deg_mm, 1)
            cd = Chain(dve, d_fin, 0, NEWTON + 1)
            newton(cd, PH[0][0:P, 0:T], 1.0, DNT, DNI)
            dve.tensor_scalar(DO[:, :], DNT[:, 0, :], 1.0 / TS, None, ALU.mult)
            cd(dve.tensor_scalar(DT[:, :], DNT[:, 0, :], TS, None, ALU.mult))
            cd.end()
            for g in range(G + 1):
                if g >= 2:
                    dve.wait_ge(th_done, g - 1)
                    dve.wait_ge(xt_mm, (g - 1) * TG)
                    dve.wait_ge(tl_done, g - 1)
                for j in range(TG * (g < G)):
                    t = g * TG + j
                    dve.tensor_scalar((ZN, ZN2)[g % 2][:, j, :], X[:, t, :], DT[:, t:t + 1], None, ALU.mult).then_inc(xs_done, 1)
                if g >= 1:
                    b = (g - 1) % 2
                    dve.wait_ge(th_done, g)
                    dve.tensor_tensor(TH[b][:, :, D:2 * D], (ZN, ZN2)[b][:, :, :], TH[b][:, :, 0:D], ALU.subtract).then_inc(tl_done, 1)
            dve.wait_ge(tl_done, G)
            dve.wait_ge(xt_mm, T)
            dve.wait_ge(agg_init, T)
            dve.sem_inc(x2_done, 1)
            dve.sem_inc(vl_done, 2)
            dve.sem_inc(agg_done, 1)
            with dve.Fori(0, L) as l:
                head(l)
                biases(l)
                for t in range(PEEL):
                    kv(l, t, t % 2)
                    split(l, t)
                with dve.Fori(0, (T - PEEL) // PER) as r:
                    for i in range(PER):
                        kv(l, r * PER + PEEL + i, (PEEL + i) % 2)
                mid(l)
                for j in range(TG):
                    q_norm(l * G, j)
                for j in range(TG):
                    q_low(l * G, j)
                x1(0, l * G)
                for pair in START:
                    for j in pair:
                        q_max(l * G + 1, j)
                    for j in pair:
                        z2_low(l * G, j)
                for i in QN_AHEAD:
                    q_norm(l * G + 1, i)
                body(l, 0, l * G, first=True)
                with dve.Fori(1, G - 2) as g:
                    body(l, g, l * G + g)
                body(l, G - 2, l * G + G - 2, ahead=False)
                body(l, G - 1, l * G + G - 1, last=True, ahead=False)
                z1(G - 1, l * G + G - 1)
                for j in range(TG):
                    z1_low(G - 1, T + (l * G + G - 1) * TG, j)
                for u in range(2 * KD):
                    km(G - 1, (l + 1) * G + G - 1, u)

            with some_missed(dve, FLI[0:1, 0:1], base_done):
                dve.wait_ge(agg_done, L * G * NQ + 1)
                with dve.Fori(0, EW) as t:
                    dve.tensor_copy(MW[:, :], MIS[:, ds(t, 1)]).then_inc(miss_col, 1)
                    with dve.Fori(0, NWIN) as w:
                        n = t * NWIN + w
                        dve.wait_ge(miss_mm, n + 1)
                        dve.wait_ge(miss_col, t * (NWIN + 1) + w + 1)
                        dve.tensor_scalar(OH[:, 0, :], IOTA[:, 0:W], MW[:, 0:1], None, ALU.is_equal).then_inc(miss_oh, 1)
                        dve.tensor_scalar(MW[:, :], MW[:, :], -float(W), None, ALU.add).then_inc(miss_col, 1)
                        dve.wait_ge(miss_mm, n + 2)
                        o = AGG[:, :, ds(w * W, W)]
                        dve.tensor_tensor(o, PC[0][:, 0:2 * W].rearrange("p (k n) -> p k n", k=KD), o, ALU.add).then_inc(miss_added, 1)
                        dve.wait_ge(miss_added, n + 1)

            cf = Chain(dve, d_route, 0, 2 * G + LN + 1 + 15)
            dve.wait_ge(late_in, 64)
            dve.wait_ge(x2_done, L * T + 1)
            for g in range(G):
                V = (ZN, ZN2)[g % 2]
                for j in range(TG):
                    t = g * TG + j
                    dve.wait_ge(gn_mm, t + 1)
                    dve.scalar_tensor_tensor(V[:, j, :], PA[t % 2][0:P, 0:D], DO[:, t:t + 1], GNB, ALU.mult, ALU.add).then_inc(gn_read, 1)
                dve.wait_ge(gn_read, (g + 1) * TG)
                cf(dve.scalar_tensor_tensor(V[:, :, :], V[:, :, :], 0.2, V[:, :, :], ALU.mult, ALU.max))
                dve.wait_ge(xr_sum, G if g >= 3 else g + 1)
                cf(dve.tensor_tensor(X[:, g * TG:(g + 1) * TG, :], XR[g % 3], V[:, :, :], ALU.add))
                dve.sem_inc(xt_done, TG)
                fill(g)
                for t in range(g * TG, (g + 1) * TG):
                    ins = dve.bn_stats(ST0[:, t, :], X[:, t, :])
            cf(ins)
            fill(G)
            for t in range(T):
                ins = dve.bn_aggr(MV0[:, t, :], ST0[:, t, :])
            cf(ins)
            newton(cf, MV0[:, :, 1], EPS, DNT, DNI)
            for g in range(G + 1):
                if g >= 2:
                    dve.wait_ge(row_done, (g - 1) * TG)
                    dve.wait_ge(row_hi, g - 1)
                    dve.wait_ge(tf_mm, (g - 1) * TG)
                for j in range(TG * (g < G)):
                    t = g * TG + j
                    dve.tensor_scalar((ZN, ZN2)[g % 2][:, j, :], X[:, t, :], MV0[:, t, 0:1], DNT[:, 0, t:t + 1], ALU.subtract,
                                      ALU.mult).then_inc(zf_done, 1)
                if g >= 1:
                    c = slice((g - 1) * TG, g * TG)
                    dve.wait_ge(row_hi, g)
                    dve.wait_ge(zf_done, g * TG)
                    dve.tensor_tensor(ROW[:, c, D:2 * D], (ZN, ZN2)[(g - 1) % 2][:, :, :], ROW[:, c, 0:D], ALU.subtract).then_inc(row_done, TG)
            dve.wait_ge(lg_mm, T)
            cf(dve.tensor_copy(LG, PC[0][0:P, 0:T * EX].rearrange("p (t e) -> p t e", e=EX)))
            bc = lambda v: v.unsqueeze(2).to_broadcast([P, T, EX])
            be = lambda v: v.unsqueeze(1).to_broadcast([P, T, EX])
            r = lambda n: R1[:, n, :]
            cf(dve.tensor_reduce(r(0), LG, AX.X, ALU.max))
            dve.tensor_tensor(L2, LG, bc(r(0)), ALU.subtract).then_inc(top_done, 1)
            cf(dve.tensor_tensor(L1, LG, bc(r(0)), ALU.is_equal))
            cf(dve.tensor_tensor(L1, L1, be(IOC[:, :]), ALU.mult))
            cf(dve.tensor_reduce(r(1), L1, AX.X, ALU.max))
            cf(dve.tensor_tensor(LG, L1, bc(r(1)), ALU.is_equal))
            dve.tensor_copy(OE[:, :, :], LG).then_inc(oe_done, 1)
            dve.wait_ge(es_done, 1)
            cf(dve.tensor_reduce(r(2), L2, AX.X, ALU.add))
            cf(dve.reciprocal(r(2), r(2)))
            dve.wait_ge(row_done, T)
            dve.tensor_copy(ROW[:, :, 2 * D:RW].bitcast(f32), r(2).unsqueeze(2)).then_inc(row_done, 1)
            cf(dve.tensor_tensor(L1, LG, be(IOE[:, :]), ALU.mult))
            cf(dve.tensor_reduce(r(3), L1, AX.X, ALU.add))
            dve.wait_ge(pos_mm, 1)
            cf(dve.tensor_tensor(L1, PA[0][0:P, 0:T * EX].rearrange("p (t e) -> p t e", e=EX), LG, ALU.mult))
            cf(dve.tensor_reduce(r(4), L1, AX.X, ALU.add))
            cf(dve.tensor_scalar(r(5), r(4), float(C), None, ALU.is_le))
            cf(dve.scalar_tensor_tensor(r(0), r(4), -1.0, r(3), ALU.add, ALU.add))
            cf(dve.tensor_scalar(r(1), r(5), -BIG, BIG, ALU.mult, ALU.add))
            cf(dve.tensor_tensor(SIX[:, :], r(0), r(1), ALU.add))
            dve.tensor_scalar(r(4), r(4), float(C), -1.0, ALU.min, ALU.add).then_inc(route_done, 1)
            dve.wait_ge(route_done, 1)
            dve.tensor_tensor(GIX[:, :], r(4), r(3), ALU.add).then_inc(route_done, 1)
            cf.end()

            dve.sem_inc(ehl_done, 2)
            dve.sem_inc(ey_read, 2)
            dve.sem_inc(e_clean, 1)

            def low1(e):
                for k in range(KD):
                    dve.wait_ge(e1_hi, e * KD + k + 1)
                    dve.scalar_tensor_tensor(W1L[:, k, :], SE1[:, k, :], WS, W1H[:, k, :], ALU.mult, ALU.subtract).then_inc(e1_lo, 1)

            def low2(e, c):
                f = slice(c * NF // 4, (c + 1) * NF // 4)
                dve.wait_ge(e2_hi, e * 4 + c + 1)
                dve.scalar_tensor_tensor(W2L[:, f, :], SE2[:, f, :], WS, W2H[:, f, :], ALU.mult, ALU.subtract).then_inc(e2_lo, 1)

            def rows_low(e):
                dve.wait_ge(et_mm, e * 2 + 2)
                dve.tensor_copy(BTL, PT[1][:, :].bitcast(f16)[:, 0:KD * CP].rearrange("p (k n) -> p k n", k=KD)).then_inc(bt_lo, 1)
                dve.wait_ge(slot_in, (e + 1) * 16)
                dve.tensor_scalar(PW[:, ds(e * NCT, NCT)].unsqueeze(2), BS[:, :, 2 * D:RW].bitcast(f32), 1.0 / WS, None,
                                  ALU.mult).then_inc(pw_done, 1)

            def nans(e):
                dve.wait_ge(ey_read, (e + 1) * NCT + 2)
                dve.tensor_tensor(YE, YV, YV, ALU.is_equal).then_inc(e_nan, 1)

            def clean(e):
                ch = Chain(dve, d_exp, e, 1)
                dve.wait_ge(e_nan, e + 1)
                dve.wait_ge(er_zero, e + 1)
                dve.wait_ge(e_flags, (e + 1) * 2)
                fill(TG)
                ch(dve.copy_predicated(YR, YE.bitcast(i32), YC[:, :, :]))
                fill(TG + 1)
                dve.copy_predicated(YR, YF.bitcast(i32), YV).then_inc(e_clean, 1)
                ch.end()

            def expert(e, first=False, last=False):
                for f in range(NF):
                    dve.wait_ge(eh_done, e * NF + f + 1)
                    dve.tensor_tensor(HL[:, f, 0:CP], HE[:, f % 3, :], HH[:, f, 0:CP], ALU.subtract).then_inc(ehl_done, 1)
                    if f in W2_AT:
                        low2(e, W2_AT.index(f))
                    if f == CLEAN_AT and not first:
                        nans(e - 1)
                if not first:
                    clean(e - 1)
                if not last:
                    low1(e + 1)
                    rows_low(e + 1)

            ceb = Chain(dve, d_eb, 0, 3)
            dve.wait_ge(eb_in, 32)
            ceb(dve.tensor_scalar(ERF, ERF, WS, None, ALU.mult))
            ceb(dve.tensor_copy(ERT, ERF))
            ceb(dve.tensor_scalar(ERT, ERT, LOW[:, 0:1], None, ALU.mult))
            dve.tensor_tensor(ERB, ERF, ERT, ALU.subtract).then_inc(ebias_done, 1)
            ceb.end()
            low1(0)
            rows_low(0)
            expert(0, first=True)
            with dve.Fori(1, EX - 1) as e:
                expert(e)
            expert(EX - 1, last=True)
            nans(EX - 1)
            dve.tensor_scalar(YF, YV, 0.0, 0.0, ALU.mult, ALU.is_equal).then_inc(e_flags, 1)
            dve.tensor_scalar(YC[:, :, :], YV, -1.0e4, 1.0e4, ALU.max, ALU.min).then_inc(e_flags, 1)
            clean(EX - 1)
            for t in range(T):
                if t % TG == 0:
                    dve.wait_ge(back_in[t // TG], 16 * TG)
                dve.scalar_tensor_tensor(X[:, t, :], YG[:, t, :], R1[:, 5, t:t + 1], X[:, t, :], ALU.mult, ALU.add).then_inc(fin_done, 1)

        @block.tensor
        def _(pe):
            pe.sem_inc(ctx_mm, 2)
            pe.sem_inc(y_mm, 1)

            def three(o, st, mv, k, start=False, stop=False, **kw):
                n = 0
                for c in range(k):
                    for a, b in ((0, 0), (0, 1), (1, 0)):
                        ins = pe.matmul(o, st(a, c), mv(b, c), start=(start and n == 0), stop=(stop and n == 3 * k - 1), **kw)
                        n += 1
                return ins

            Z1 = (Z1H, Z1L)
            Z2 = (Z2H, Z2L)
            KV = (KVH, KVL)
            QO = (QOH, QOL)
            W1 = (W1H, W1L)
            W2 = (W2H, W2L)
            CT = (CTH, CTL)
            CW = (CWH, CWL)
            QT = (QTH, QTL)
            HX = (HH, HL)
            EXP = (EH, EL)
            VX = (VH, VL)

            def biases(l):
                pe.wait_ge(lnp_done, l * 3 + 3)
                pe.wait_ge(qo_in, (l + 1) * 32)
                pe.wait_ge(kv_in, (l + 1) * 32)
                pe.wait_ge(w1_in, (l + 1) * 16)
                pe.wait_ge(x2_done, l * T + 1)
                for f in range(NF):
                    for k in range(KD):
                        ins = pe.matmul(PH[1][:, KD + f:KD + f + 1], SW[:, k * FF + f * 128:k * FF + (f + 1) * 128],
                                        LNP[:, 3, k:k + 1], start=(k == 0), stop=(k == KD - 1))
                for h in range(KD):
                    for k in range(KD):
                        ins = pe.matmul(PH[1][:, h:h + 1], SKV[:, k, 1, h * 128:(h + 1) * 128], B2[:, k, 0:1],
                                        start=(k == 0), stop=(k == KD - 1))
                ins.then_inc(b1_mm, 1)
                for k in range(KD):
                    ins = pe.matmul(PH[0][0:2, 0:D], B2[:, k, :], SQO[:, 0, k, :], start=(k == 0), stop=(k == KD - 1))
                ins.then_inc(bq_mm, 1)

            def bias_out(l):
                pe.wait_ge(bv_done, l + 1)
                pe.wait_ge(rt_done, l * 2 + 1)
                for k in range(KD):
                    ins = pe.matmul(PH[1][0:2, 0:D], BV[:, k, :], SQO[:, 1, k, :], start=(k == 0), stop=(k == KD - 1))
                ins.then_inc(bo_mm, 1)

            def km(l, g, kg, u):
                m, c = divmod(u, 2)
                t0, tn = CH[c]
                if u == 0:
                    pe.wait_ge(whk_done, (l + 1) * KD)
                    pe.wait_ge(t1_lo, (kg + 1) * TG)
                if u >= 2:
                    pe.wait_ge(km_read, kg * 2 * KD + u - 1)
                for k in range(KD):
                    ins = pe.matmul(PA[u % 2][:, 0:tn * P], KVH[:, k, 0, m * 128:(m + 1) * 128],
                                    Z1H[:, k, ds((g * TG + t0) * P, tn * P)], start=(k == 0), stop=(k == KD - 1))
                ins.then_inc(km_mm, 1)

            def z1_t(g, n0, j):
                n = n0 + j
                pe.wait_ge(z1_done, T + n + 1)
                if j >= 2:
                    pe.wait_ge(t1_lo, n - 1)
                for h in range(KD):
                    ins = pe.transpose(PT[j % 2][:, h * P:(h + 1) * P], ZN[:, j, h * 128:(h + 1) * 128], ID[0:P, 0:P])
                ins.then_inc(t1_mm, 1)

            def head(l):
                pe.wait_ge(kx_done, l + 1)
                pe.wait_ge(agg_done, l * G * NQ + 1)
                for m in range(KD):
                    ins = pe.matmul(PT[0][0:1, m * 128:(m + 1) * 128], KX[:, m:m + 1], ID[:, :], start=True, stop=True)
                ins.then_inc(kr_mm, 1)
                for h in range(KD):
                    ins = pe.matmul(PC[h][:, 0:129], ZR[0:1, 0:128], ZR[0:1, 0:129], start=True, stop=False,
                                    skip_group_check=True)

            def kv(l, t, b):
                n = l * T + t
                pe.wait_ge(vl_done, n + 1)
                three(PA[b][0:P, 0:2 * D], lambda a, k: Z1[a][:, k, ds(t * P, P)],
                      lambda c, k: KV[c][:, k, :, :].rearrange("p a d -> p (a d)"), KD, True, False, skip_group_check=True)
                pe.wait_ge(kr_done, l + 1)
                pe.matmul(PA[b][0:P, 0:D], ONE[0:1, 0, 0:P], KR[0:1, :], start=False, stop=True,
                          skip_group_check=True).then_inc(kv_mm, 1)

            def context(l, t, b):
                n = l * T + t
                pe.wait_ge(el_done, n + 3)
                pe.wait_ge(vl_done, n + 3)
                for h in range(KD):
                    for x, y in ((0, 0), (0, 1), (1, 0)):
                        ins = pe.matmul(PC[h][:, 0:129], EXP[x][:, b, h * 128:(h + 1) * 128], VX[y][:, b, h, 0:129],
                                        start=False, stop=False, skip_group_check=True)
                ins.then_inc(ctx_mm, 1)

            def mid(l):
                for h in range(KD):
                    ins = pe.matmul(PC[h][:, 0:129], ZR[0:1, 0:128], ZR[0:1, 0:129], start=False, stop=True,
                                    skip_group_check=True)
                ins.then_inc(ctx_end, 1)
                q(0, l * G, 0)
                q(0, l * G, 1)
                pe.wait_ge(cn_done, (l + 1) * KD)
                for h in range(KD):
                    ins = pe.transpose(PT[0][:, h * 128:(h + 1) * 128], CN[:, h, :], ID[:, :])
                ins.then_inc(ct_mm, 1)
                q(0, l * G, 2)
                q(0, l * G, 3)
                pe.wait_ge(ct_lo, l + 1)
                for h in range(KD):
                    three(PA[h][:, 0:D], lambda a, k: CT[a][:, h, :], lambda b, k: QO[b][:, 1, h, :], 1,
                          True, True).then_inc(cw_mm, 1)

            def q(g, it, j):
                n = it * TG + j
                if j >= 2:
                    pe.wait_ge(q_read, n - 1)
                o = PH[j % 2][0:P, 0:D]
                pe.matmul(o, ONE[0:2, 0, 0:P], RB[:, 0, :], start=True, stop=False)
                three(o, lambda a, k: Z1[a][:, k, ds((g * TG + j) * P, P)], lambda b, k: QO[b][:, 0, k, :], KD,
                      False, True).then_inc(q_mm, 1)

            def q_t(it, j):
                n = it * TG + j
                pe.wait_ge(qn_done, n + 1)
                if j >= 2:
                    pe.wait_ge(tq_lo, n - 1)
                for h in range(KD):
                    ins = pe.transpose(PT[j % 2][:, h * P:(h + 1) * P], QS[:, j, h * 128:(h + 1) * 128], ID[0:P, 0:P])
                ins.then_inc(tq_mm, 1)

            def attn(it):
                pe.wait_ge(q_read, (it + 1) * TG)
                for j in range(TG):
                    n = it * TG + j
                    pe.wait_ge(tq_lo, n + 1)
                    if j >= 2:
                        pe.wait_ge(x1_done, n - 1)
                    o = PA[j % 2][0:P, 0:D]
                    pe.matmul(o, ONE[0:2, 1, 0:P], RB[:, 1, :], start=True, stop=False)
                    three(o, lambda a, k: QT[a][:, k, j * P:(j + 1) * P], lambda b, k: CW[b][:, k, :], KD,
                          False, True).then_inc(at_mm, 1)

            def z2_t(it, j):
                n = it * TG + j
                pe.wait_ge(z2_done, n + 1)
                if j >= 2:
                    pe.wait_ge(t2_lo, n - 1)
                for h in range(KD):
                    ins = pe.transpose(PT[j % 2][:, h * P:(h + 1) * P], ZN2[:, j, h * 128:(h + 1) * 128], ID[0:P, 0:P])
                ins.then_inc(t2_mm, 1)

            def unit(it, u):
                t0, tn = CH[u // NF]
                f = u % NF
                n = it * 2 * NF + u
                if u >= 2:
                    pe.wait_ge(gelu_done, n - 1)
                else:
                    pe.wait_ge(hl_done, it * 2 * NF + 2)
                three(PH[u % 2][:, 0:tn * P], lambda a, k: W1[a][:, k, f * 128:(f + 1) * 128],
                      lambda b, k: Z2[b][:, k, t0 * P:(t0 + tn) * P], KD, True, True).then_inc(f1_mm, 1)

            def y(it, j):
                n = it * TG + j
                if j in (0, CH[1][0]):
                    pe.wait_ge(hl_done, it * 2 * NF + (NF if j == 0 else 2 * NF) + 2)
                if j >= 2:
                    pe.wait_ge(x2_done, n)
                o = PA[(j + 1) % 2][0:P, 0:D]
                pe.matmul(o, ONE[0:2, 0, 0:P], RB[:, 2, :], start=True, stop=False)
                three(o, lambda a, f: HX[a][:, f, j * P:(j + 1) * P], lambda b, f: W2[b][:, f, :], NF,
                      False, True).then_inc(y_mm, 1)

            def body(l, g, it, first=False, last=False, ahead=True):
                if not last:
                    pe.wait_ge(q_read, (it + 2) * TG)
                pe.wait_ge(t2_lo, (it + 1) * TG)
                for u in range(2 * NF):
                    if not first and u in T1_AT:
                        z1_t(g - 1, T + (it - 1) * TG, u - T1_AT[0])
                    if not last and u in TQ_AT:
                        if not first and u == TQ_AT[0]:
                            pe.wait_ge(t1_lo, T + it * TG)
                        q_t(it + 1, u - TQ_AT[0])
                    if not first and u in KM_AT:
                        km(l + 1, g - 1, it - 1 + G, u - KM_AT[0])
                    unit(it, u)
                if not first:
                    pe.wait_ge(km_read, (it + G) * 2 * KD)
                if last:
                    pe.wait_ge(x2_done, it * TG + 1)
                else:
                    attn(it + 1)
                    pe.wait_ge(x1_done, (it + 2) * TG - 1)
                for j in range(TG):
                    if j == 1 and not last:
                        pe.wait_ge(x1_done, (it + 2) * TG)
                    y(it, j)
                    if j == TG - 1 and not last:
                        z2_t(it + 1, j)
                    for n in P_AT[j]:
                        pair(it, n)
                    if ahead:
                        for i in Q_AT[j]:
                            q(g + 2, it + 2, i)
                    if j < TG - 1 and not last:
                        for i in T2_AT[j]:
                            z2_t(it + 1, i)

            def logits(t):
                pe.wait_ge(tf_done, t + 1)
                o = PC[0][0:P, t * EX:(t + 1) * EX]
                pe.matmul(o, ONF[:, :], GBR[:, :], start=True, stop=False)
                for k in range(KD):
                    ins = pe.matmul(o, EFT[:, t % 2, k * P:(k + 1) * P], GW[:, k, :], start=False, stop=(k == KD - 1))
                ins.then_inc(lg_mm, 1)

            def pair(it, q):
                n = it * NP_ + q
                s = q % SLOTS
                if q == 0:
                    pe.wait_ge(oh_done, it + 1)
                pe.wait_ge(gin[s], (it * (NP_ // SLOTS) + q // SLOTS + 1) * 32)
                if q in (0, 2):
                    pe.wait_ge(agg_done, it * NQ + 1)
                elif q % 2 == 0:
                    pe.wait_ge(agg_done, it * NQ + q // 2)
                for h in range(KD):
                    for i in range(2):
                        for part in range(2):
                            c = part * D + h * 128
                            ins = pe.matmul(PC[q // 2 % 2][:, h * W:(h + 1) * W], GB[:, s, i, c:c + 128], OH[:, 2 * q + i, :],
                                            start=(h + q % 2 + i + part == 0), stop=(h + q % 2 + i + part == 4),
                                            skip_group_check=True)
                ins.then_inc(pair_mm, 1)

            pe.wait_ge(const_done, 1)
            pe.sem_inc(pair_mm, SLOTS + 1)
            deg = PH[0][0:P, 0:T]
            pe.matmul(deg, ZR[0:1, 0:P], ZR[0:1, 0:T], start=True, stop=False, skip_group_check=True)
            def block(n, b):
                pe.wait_ge(hist_oh, n + 1)
                pe.wait_ge(hist_act, n + 1)
                for i in range(HB):
                    ins = pe.matmul(deg, OHL[:, b, i, :], OHH[:, b, i, :], start=False, stop=False, skip_group_check=True)
                ins.then_inc(hist_mm, 1)

            with pe.Fori(0, G) as g:
                for c in range(HQ):
                    for j in Z1_AT[c]:
                        z1_t(g, g * TG, j)
                    block(g * HQ + c, c % 2)
                    if c == 2:
                        for u in range(2 * KD):
                            km(0, g, g, u)
            pe.matmul(deg, ZR[0:1, 0:P], ZR[0:1, 0:T], start=False, stop=True, skip_group_check=True).then_inc(deg_mm, 1)
            for t in range(T):
                j = t % TG
                pe.wait_ge(xs_done, t + 1)
                if j >= 2:
                    pe.wait_ge(agg_init, t - 1)
                elif t >= TG:
                    pe.wait_ge(agg_init, t // TG * TG)
                for h in range(KD):
                    ins = pe.transpose(PT[j % 2][:, h * P:(h + 1) * P], (ZN, ZN2)[t // TG % 2][:, j, h * 128:(h + 1) * 128], ID[0:P, 0:P])
                ins.then_inc(xt_mm, 1)
            pe.wait_ge(agg_init, T)
            with pe.Fori(0, L) as l:
                pe.wait_ge(wlk_done, (l + 1) * KD)
                biases(l)
                head(l)
                for t in range(PEEL):
                    kv(l, t, t % 2)
                    if t >= 1:
                        context(l, t - 1, (t - 1) % 2)
                    if t == 2:
                        bias_out(l)
                with pe.Fori(0, (T - PEEL) // PER) as r:
                    for i in range(PER):
                        t = r * PER + PEEL + i
                        kv(l, t, (PEEL + i) % 2)
                        context(l, t - 1, (PEEL + i - 1) % 2)
                context(l, T - 1, (T - 1) % 2)
                pe.wait_ge(rows_done, l + 1)
                mid(l)
                q(0, l * G, TG - 1)
                for j in range(TG):
                    q_t(l * G, j)
                pe.wait_ge(cw_lo, (l + 1) * KD)
                attn(l * G)
                for tiles in START:
                    for j in tiles:
                        q(1, l * G + 1, j)
                    for j in tiles:
                        z2_t(l * G, j)
                pe.wait_ge(wlo_done, (l + 1) * WLO)
                body(l, 0, l * G, first=True)
                with pe.Fori(1, G - 2) as g:
                    body(l, g, l * G + g)
                body(l, G - 2, l * G + G - 2, ahead=False)
                body(l, G - 1, l * G + G - 1, last=True, ahead=False)
                pe.wait_ge(t1_lo, T + (l * G + G - 1) * TG)
                for j in range(TG):
                    z1_t(G - 1, T + (l * G + G - 1) * TG, j)
                for u in range(2 * KD):
                    km(l + 1, G - 1, (l + 1) * G + G - 1, u)

            with some_missed(pe, FLI[0:1, 0:1], base_done):
                with pe.Fori(0, EW) as t:
                    with pe.Fori(0, NWIN) as w:
                        n = t * NWIN + w
                        pe.wait_ge(miss_in, t * 16 + 16)
                        pe.wait_ge(miss_oh, n + 1)
                        for h in range(KD):
                            for part in range(2):
                                c = part * D + h * 128
                                ins = pe.matmul(PC[0][:, h * W:(h + 1) * W], GB[:, 0, 0, c:c + 128], OH[:, 0, :],
                                                start=(part == 0), stop=(part == 1))
                        ins.then_inc(miss_mm, 1)
                pe.wait_ge(miss_added, EW * NWIN)

            pe.wait_ge(agg_done, L * G * NQ + 1)
            pe.wait_ge(late_in, 64)
            pe.wait_ge(x2_done, L * T + 1)
            pe.wait_ge(km_read, (L + 1) * G * 2 * KD)
            for t in range(T):
                if t >= 2:
                    pe.wait_ge(gn_read, t - 1)
                for k in range(KD):
                    ins = pe.matmul(PA[t % 2][0:P, 0:D], AGG[:, k, t * P:(t + 1) * P], GNW[:, k, :], start=(k == 0), stop=(k == KD - 1))
                ins.then_inc(gn_mm, 1)
            for t in range(T + 1):
                if t < T:
                    pe.wait_ge(zf_done, t + 1)
                    if t >= 2:
                        pe.wait_ge(tf_done, t - 1)
                    for h in range(KD):
                        ins = pe.transpose(PT[t % 2][:, h * P:(h + 1) * P], (ZN, ZN2)[t // TG % 2][:, t % TG, h * 128:(h + 1) * 128], ID[0:P, 0:P])
                    ins.then_inc(tf_mm, 1)
                if t >= 1:
                    logits(t - 1)

            pe.wait_ge(oe_done, 1)
            pe.wait_ge(gn_read, T)
            pos = PA[0][0:P, 0:T * EX]
            pe.matmul(pos, TRI[:, :], OE[:, :, :].rearrange("p t e -> p (t e)"), start=True, stop=False, skip_group_check=True)
            for t in range(T - 1):
                ins = pe.matmul(PA[0][0:P, (t + 1) * EX:T * EX].rearrange("p (t e) -> p t e", e=EX), ON1[:, :],
                                OE[:, t, :].unsqueeze(1).to_broadcast([P, T - 1 - t, EX]), start=False, stop=(t == T - 2),
                                skip_group_check=True)
            ins.then_inc(pos_mm, 1)

            pe.sem_inc(ey_mm, 1)
            pe.wait_ge(route_done, 2)
            BT = (BTH, BTL)

            def rows_t(e, part):
                if part == 0:
                    pe.wait_ge(slot_in, (e + 1) * 16)
                o = PT[part][:, :].bitcast(f16)
                for k in range(KD):
                    for j in range(NCT):
                        c = part * D + k * 128
                        ins = pe.transpose(o[:, k * CP + j * CT_:k * CP + (j + 1) * CT_], BS[:, j, c:c + 128], IDH[0:CT_, 0:CT_])
                ins.then_inc(et_mm, 1)

            def expert(e, last=False):
                pe.wait_ge(bt_hi, e + 1)
                pe.wait_ge(bt_lo, e + 1)
                pe.wait_ge(e1_lo, (e + 1) * 2)
                for f in range(NF):
                    n = e * NF + f
                    pe.wait_ge(er_done, n + 1)
                    three(PH[f % 2][:, 0:CP], lambda a, k: W1[a][:, k, f * 128:(f + 1) * 128], lambda b, k: BT[b][:, k, :],
                          KD, True, True).then_inc(e1_mm, 1)
                for j in range(NCT):
                    n = e * NCT + j
                    pe.wait_ge(ey_read, n + 1)
                    o = PA[j % 2][0:CT_, 0:D]
                    for f in range(NF):
                        if j == 0:
                            pe.wait_ge(ehl_done, e * NF + f + 3)
                            pe.wait_ge(e2_lo, e * 4 + f * 4 // NF + 1)
                        three(o, lambda a, _: HX[a][:, f, j * CT_:(j + 1) * CT_], lambda b, _: W2[b][:, f, :], 1, f == 0, False)
                    pe.matmul(o, ONE[0:2, 0, 0:CT_], ERB[:, ds(e * D, D)], start=False, stop=True).then_inc(ey_mm, 1)
                    if j < 2 and not last:
                        rows_t(e + 1, j)

            pe.wait_ge(ebias_done, 1)
            rows_t(0, 0)
            rows_t(0, 1)
            with pe.Fori(0, EX - 1) as e:
                expert(e)
            expert(EX - 1, last=True)


def kernel(**inputs):
    import numpy as _np
    import concourse.bacc as _bacc
    from concourse import mybir as _mybir
    from concourse.bass_utils import run_bass_kernel_spmd as _run

    nc = _bacc.Bacc("TRN2", target_bir_lowering=False, num_devices=1)
    arrays, args = {}, {}
    mix = {name[7:]: _np.asarray(value) for name, value in inputs.items() if name.startswith("L0_mix_")}
    columns = [mix[n].reshape(mix[n].shape[0], -1, 128).transpose(0, 2, 1) for n in ("ln1_g", "ln1_b", "ln2_g", "ln2_b", "b1")]
    rows = _np.stack([mix["bo"], mix["b2"]], axis=1)
    laid = dict(inputs, mix_vec=_np.concatenate(columns, axis=2), mix_rows=_np.stack([rows, rows], axis=1))
    for name in ("ln1_g", "ln1_b", "ln2_g", "ln2_b", "b1", "bo", "b2"):
        del laid["L0_mix_" + name]
    tiles = 400
    for name, pad in (("src", 0), ("dst", -1)):
        a = _np.asarray(laid.pop(name))
        a = _np.concatenate([a, _np.full(tiles * 128 - a.shape[0], pad, a.dtype)])
        laid["edge_" + name] = a.reshape(tiles, 128).T
    laid["gnn_bias"] = _np.tile(_np.asarray(laid.pop("L0_gnn_b"))[None, :], (125, 1))
    b1, b2 = _np.asarray(laid.pop("L0_ffn_b1")), _np.asarray(laid.pop("L0_ffn_b2"))
    laid["ffn_vec"] = b1.reshape(b1.shape[0], -1, 128).transpose(0, 2, 1)
    laid["ffn_rows"] = _np.stack([b2, b2], axis=1)
    for name, value in laid.items():
        a = _np.ascontiguousarray(value)
        arrays[f"in_{name}"] = a
        args[name] = nc.dram_tensor(f"in_{name}", a.shape, _mybir.dt.from_np(a.dtype), kind="ExternalInput").ap()
    out = nc.dram_tensor("out_0", (3125, 256), _mybir.dt.float32, kind="ExternalOutput").ap()
    build(nc, args, out)
    r = _run(nc, [arrays], core_ids=[0])
    return r.results[0]["out_0"]
```
